# Optimizing a Trainium2 kernel written in Bass

```python
import numpy as np
import jax
import jax.numpy as jnp

def _softmax(x, axis=-1):
    return jax.nn.softmax(x, axis=axis)

def _gelu(x):
    return jax.nn.gelu(x, approximate=True)

def _silu(x):
    return jax.nn.silu(x)

def _sigmoid(x):
    return jax.nn.sigmoid(x)

def _layernorm(x, axis=-1, eps=1e-05):
    m = jnp.mean(x, axis=axis, keepdims=True)
    v = jnp.var(x, axis=axis, keepdims=True)
    return (x - m) / jnp.sqrt(v + eps)

def _scatter_add(tgt, idx, src, axis=0):
    return tgt.at[idx].add(src)

def _segment_sum(src, seg, n):
    return jax.ops.segment_sum(src, seg, n)
kernel_name = 'mk_adaln_d1_jaxref_r8_755656'

def setup_inputs(seed: int=0):
    np.random.seed(seed)
    _w = jnp.asarray

    def _L0_attn_setup():
        import jax, jax.numpy as jnp
        import numpy as np
        EPS_LN = 1e-06
        STAB = 0.001

        def layer_norm(x, gamma, beta):
            mu = jnp.mean(x, axis=-1, keepdims=True)
            var = jnp.mean(jnp.square(x - mu), axis=-1, keepdims=True)
            return (x - mu) * jax.lax.rsqrt(var + EPS_LN) * gamma + beta
        key = jax.random.key(seed)
        B, L, E, H, F = (8, 256, 128, 16, 512)
        dh = E // H
        ks = jax.random.split(key, 12)
        s_attn = 1.0 / np.sqrt(E)
        s_ffn1 = 1.0 / np.sqrt(E)
        s_ffn2 = 1.0 / np.sqrt(F)
        return {'x': jax.random.normal(ks[0], (B, L, E), jnp.float32), 'gamma1': jnp.ones((E,), jnp.float32), 'beta1': jnp.zeros((E,), jnp.float32), 'wq': jax.random.normal(ks[1], (E, H, dh), jnp.float32) * s_attn, 'wk': jax.random.normal(ks[2], (E, H, dh), jnp.float32) * s_attn, 'wv': jax.random.normal(ks[3], (E, H, dh), jnp.float32) * s_attn, 'wo': jax.random.normal(ks[4], (H, dh, E), jnp.float32) * s_attn, 'w1': jax.random.normal(ks[5], (E, F), jnp.float32) * s_ffn1, 'b1': jnp.zeros((F,), jnp.float32), 'w2': jax.random.normal(ks[6], (F, E), jnp.float32) * s_ffn2, 'b2': jnp.zeros((E,), jnp.float32)}
    _L0_attn_in = _L0_attn_setup()

    def _L0_ffn_setup():
        import jax, jax.numpy as jnp
        import numpy as np
        EPS = 1e-06
        TOP_K = 2

        def rms_norm(x, scale, eps=EPS):
            xf = x.astype(jnp.float32)
            mean_sq = jnp.mean(xf * xf, axis=-1, keepdims=True)
            return (xf * (scale.astype(jnp.float32) * jax.lax.rsqrt(mean_sq + eps))).astype(x.dtype)
        key = jax.random.key(seed)
        k0, k1, k2, k3 = jax.random.split(key, 4)
        B, S, D, H, E = (2, 256, 128, 352, 8)
        x = jax.random.normal(k0, (B, S, D), dtype=jnp.float32)
        norm_scale = jnp.ones((D,), dtype=jnp.float32)
        w_router = jax.random.normal(k1, (E, D), dtype=jnp.float32) * 0.02
        w_up = jax.random.normal(k2, (E, 2 * H, D), dtype=jnp.float32) * 0.02
        w_down = jax.random.normal(k3, (E, D, H), dtype=jnp.float32) * 0.02
        return {'x': x, 'norm_scale': norm_scale, 'w_router': w_router, 'w_up': w_up, 'w_down': w_down}
    _L0_ffn_in = _L0_ffn_setup()
    _L0_c = _w((lambda *s: np.random.randn(*s).astype(np.float32) * 0.05)(4, 128))
    _L0_wmod = _w((lambda *s: np.random.randn(*s).astype(np.float32) * 0.05)(128, 6 * 128) * 128 ** (-0.5))
    _d = {'L0_attn_x': _L0_attn_in['x'], 'L0_attn_gamma1': _L0_attn_in['gamma1'], 'L0_attn_beta1': _L0_attn_in['beta1'], 'L0_attn_wq': _L0_attn_in['wq'], 'L0_attn_wk': _L0_attn_in['wk'], 'L0_attn_wv': _L0_attn_in['wv'], 'L0_attn_wo': _L0_attn_in['wo'], 'L0_attn_w1': _L0_attn_in['w1'], 'L0_attn_b1': _L0_attn_in['b1'], 'L0_attn_w2': _L0_attn_in['w2'], 'L0_attn_b2': _L0_attn_in['b2'], 'L0_ffn_norm_scale': _L0_ffn_in['norm_scale'], 'L0_ffn_w_router': _L0_ffn_in['w_router'], 'L0_ffn_w_up': _L0_ffn_in['w_up'], 'L0_ffn_w_down': _L0_ffn_in['w_down'], 'L0_c': _L0_c, 'L0_wmod': _L0_wmod}
    _x0 = _d['L0_attn_x']
    _d['L0_attn_x'] = jax.random.normal(jax.random.fold_in(jax.random.key(seed), 1), (4, 1024, 128), dtype=_x0.dtype)
    del _x0
    return _d

def reference(L0_attn_x, L0_attn_gamma1, L0_attn_beta1, L0_attn_wq, L0_attn_wk, L0_attn_wv, L0_attn_wo, L0_attn_w1, L0_attn_b1, L0_attn_w2, L0_attn_b2, L0_ffn_norm_scale, L0_ffn_w_router, L0_ffn_w_up, L0_ffn_w_down, L0_c, L0_wmod):

    def _L0_attn_ref(x, gamma1, beta1, wq, wk, wv, wo, w1, b1, w2, b2):
        import jax, jax.numpy as jnp
        import numpy as np
        EPS_LN = 1e-06
        STAB = 0.001

        def layer_norm(x, gamma, beta):
            mu = jnp.mean(x, axis=-1, keepdims=True)
            var = jnp.mean(jnp.square(x - mu), axis=-1, keepdims=True)
            return (x - mu) * jax.lax.rsqrt(var + EPS_LN) * gamma + beta
        ln1 = layer_norm(x, gamma1, beta1)
        q = jnp.einsum('ble,ehd->blhd', ln1, wq)
        k = jnp.einsum('ble,ehd->blhd', ln1, wk)
        v = jnp.einsum('ble,ehd->blhd', ln1, wv)
        qp = jax.nn.relu(q) + STAB
        kp = jax.nn.relu(k) + STAB
        kvs = jnp.einsum('blhm,blhd->bhmd', kp, v)
        num = jnp.einsum('blhm,bhmd->blhd', qp, kvs)
        ksum = jnp.sum(kp, axis=1)
        den = jnp.einsum('blhm,bhm->blh', qp, ksum)
        att = num / den[..., None]
        attn_out = jnp.einsum('blhd,hde->ble', att, wo)
        add1 = attn_out + x
        ln2 = layer_norm(add1, gamma1, beta1)
        h = jax.nn.gelu(jnp.einsum('ble,ef->blf', ln2, w1) + b1, approximate=False)
        out2 = jax.nn.gelu(jnp.einsum('blf,fe->ble', h, w2) + b2, approximate=False)
        return out2 + add1

    def _L0_ffn_ref(x, norm_scale, w_router, w_up, w_down):
        import jax, jax.numpy as jnp
        import numpy as np
        EPS = 1e-06
        TOP_K = 2

        def rms_norm(x, scale, eps=EPS):
            xf = x.astype(jnp.float32)
            mean_sq = jnp.mean(xf * xf, axis=-1, keepdims=True)
            return (xf * (scale.astype(jnp.float32) * jax.lax.rsqrt(mean_sq + eps))).astype(x.dtype)
        skip = x
        xn = rms_norm(x, norm_scale)
        scores = jnp.einsum('bsd,ed->bse', xn, w_router)
        _, ids = jax.lax.top_k(scores, TOP_K)
        probs = jax.nn.softmax(scores, axis=-1)
        c = jnp.take_along_axis(probs, ids, axis=-1)
        h = jnp.einsum('bsd,ehd->bseh', xn, w_up)
        val, gate = jnp.split(h, 2, axis=-1)
        h = val * jax.nn.silu(gate)
        y = jnp.einsum('bseh,edh->bsed', h, w_down)
        yk = jnp.take_along_axis(y, ids[..., None], axis=2)
        out = jnp.sum(yk * c[..., None], axis=2)
        return out + skip
    x = L0_attn_x
    mod = (_silu(L0_c) @ L0_wmod).reshape(L0_c.shape[0], 6, 1, -1)
    sa, ca, ga, sb, cb, gb = (mod[:, 0], mod[:, 1], mod[:, 2], mod[:, 3], mod[:, 4], mod[:, 5])
    ga = (2 * (ga >= 0) - 1) * jnp.maximum(jnp.abs(ga), 0.25)
    gb = (2 * (gb >= 0) - 1) * jnp.maximum(jnp.abs(gb), 0.25)
    h = _layernorm(x, axis=-1) * (1 + ca) + sa
    x = x + ga * _L0_attn_ref(h, L0_attn_gamma1, L0_attn_beta1, L0_attn_wq, L0_attn_wk, L0_attn_wv, L0_attn_wo, L0_attn_w1, L0_attn_b1, L0_attn_w2, L0_attn_b2)
    h = _layernorm(x, axis=-1) * (1 + cb) + sb
    x = x + gb * _L0_ffn_ref(h, L0_ffn_norm_scale, L0_ffn_w_router, L0_ffn_w_up, L0_ffn_w_down)
    return x

_drawn_inputs = setup_inputs


def setup_inputs(seed=0):
    import zlib

    import numpy as np

    out = dict(_drawn_inputs(seed))
    spreads = {'L0_attn_gamma1': (1.0, 0.6),
     'L0_attn_beta1': (0.0, 0.285),
     'L0_attn_b1': (0.0, 0.736),
     'L0_attn_b2': (0.0, 0.5),
     'L0_ffn_norm_scale': (1.0, 0.6)}
    factors = {'L0_attn_wq': 3.184, 'L0_ffn_w_router': 8.0, 'L0_ffn_w_up': 8.0, 'L0_ffn_w_down': 8.0}
    for name, (base, spread) in spreads.items():
        noise = np.random.default_rng([zlib.crc32(name.encode()), seed]).standard_normal(out[name].shape)
        drawn = base * np.exp(spread * noise) if base else spread * noise
        out[name] = jnp.asarray(drawn.astype(out[name].dtype))
    for name, factor in factors.items():
        out[name] = (out[name] * factor).astype(out[name].dtype)
    return out
```

```python
from contextlib import ExitStack

import concourse.bass as bass
from concourse import mybir

F32 = mybir.dt.float32
BF16 = mybir.dt.bfloat16
I32 = mybir.dt.int32
U32 = mybir.dt.uint32
ALU = mybir.AluOpType
ACT = mybir.ActivationFunctionType
AX = mybir.AxisListType

P = 128
B, L, D = 4, 1024, 128
H, DH = 16, 8
F = 512
FC = F // P
E, TOPK, HM = 8, 2, 352
HC = -(-HM // P)
LASTH = HM - (HC - 1) * P
R = L // P
GT = 4
G = R // GT
GN = GT * D
STAB = 0.001
EPS_OUT, EPS_IN = 1e-5, 1e-6
NKV = D + H
TOK = B * L
CAP = TOK + P
ROW = D + 2
GATE, DEST = D, D + 1
NT = 72
UN = 8
NOWHERE = 1 << 20
RPAD = 96
MOD_SHIFT_A, MOD_SCALE_A, MOD_GATE_A, MOD_SHIFT_B, MOD_SCALE_B, MOD_GATE_B = range(6)
GAMMA, BETA, NSCALE, BIAS2, BIAS1 = 0, 1, 2, 3, 4


def build(nc, x, c_t, wmod, vecs, wq, wk, wv, wo, w1, w2, wr_t, w_up, w_down, out):
    rows_dram = nc.dram_tensor("expert_rows", (E * CAP, ROW), F32).ap()
    pair_dram = nc.dram_tensor("pair_outputs", (TOPK * TOK, D), F32).ap()

    with ExitStack() as ctx:
        def sb(name, shape, dt=F32):
            return ctx.enter_context(nc.sbuf_tensor(name, shape, dt))

        def sem(name):
            return ctx.enter_context(nc.semaphore(name))

        cT = sb("cT", [P, B])
        silu_c = sb("silu_c", [P, B])
        silu_cb = sb("silu_cb", [P, B, P])
        wmod_sb = sb("wmod_sb", [P, 6 * D])
        mod = sb("mod", [P, B, 6, D])
        vec = sb("vec", [P, 4 + FC])
        wq_sb, wk_sb, wv_sb, wo_sb = (sb(n, [P, D]) for n in ("wq_sb", "wk_sb", "wv_sb", "wo_sb"))
        w1_sb = sb("w1_sb", [P, F])
        w2_sb = sb("w2_sb", [P, FC, D])
        wr_sb = sb("wr_sb", [P, RPAD])
        up_sb = sb("up_sb", [P, E, 2 * HM])
        down_sb = sb("down_sb", [P, E, HC * D])
        ident = sb("ident", [P, P])
        before = sb("before", [P, P], BF16)
        ones = sb("ones", [P, P], BF16)
        same_head = sb("same_head", [P, NKV])
        neg_half = sb("neg_half", [P, GT])
        expert_no = sb("expert_no", [P, E])
        region = sb("region", [P, E])
        tile_no = sb("tile_no", [1, NT])
        level = sb("level", [1, TOK // P])
        dest_all = sb("dest_all", [P, B, R, TOPK], I32)
        gate_diag = sb("gate_diag", [P, B, P])
        gate_sign = sb("gate_sign", [P, B, 2, D])
        x_all = sb("x_all", [P, B, R * D])
        h_all = sb("h_all", [P, B, R * D])
        q_all = sb("q_all", [P, B, G * GN])
        kvs_all = sb("kvs_all", [P, B, NKV])
        xhat = [sb(f"xhat{j}", [P, GN]) for j in range(G)]
        scaled = [sb(f"scaled{j}", [P, GN]) for j in range(G)]
        unit1 = [sb(f"unit1{j}", [P, GN]) for j in range(G)]
        ln1T = [sb(f"ln1T{j}", [P, GN]) for j in range(G)]
        kfeat = [sb(f"kfeat{j}", [P, GN]) for j in range(G)]
        vones = [sb(f"vones{j}", [P, GT, D + 4]) for j in range(G)]
        def stats(name):
            return [(sb(f"{name}_st{j}", [P, GT, 6]), sb(f"{name}_mv{j}", [P, GT, 2]),
                     sb(f"{name}_ve{j}", [P, GT]), sb(f"{name}_rs{j}", [P, GT])) for j in range(G)]
        st_x, st_h, st_a, st_y = stats("x"), stats("h"), stats("a"), stats("y")
        sumsq = [sb(f"sumsq{j}", [P, GT]) for j in range(G)]
        ms_eps = [sb(f"ms_eps{j}", [P, GT]) for j in range(G)]
        rms = [sb(f"rms{j}", [P, GT]) for j in range(G)]
        qf = [sb(f"qf{j}", [P, GN]) for j in range(G)]
        rden = [sb(f"rden{j}", [P, GT, H]) for j in range(G)]
        att = [sb(f"att{j}", [P, GN]) for j in range(G)]
        attT = sb("attT", [P, GN])
        add1 = [sb(f"add1{j}", [P, GN]) for j in range(G)]
        unit2 = [sb(f"unit2{j}", [P, GN]) for j in range(G)]
        hidT = sb("hidT", [P, FC, GN])
        yhat = sb("yhat", [P, GN])
        square = sb("square", [P, D])
        ffnT, gx, normed, ln2T, xnT = xhat, scaled, unit1, ln1T, kfeat
        score = sb("score", [P, R, E])
        top = sb("top", [P, R, E])
        top_ix = sb("top_ix", [P, R, E], U32)
        top_f = sb("top_f", [P, TOPK, R])
        onehot = sb("onehot", [P, TOPK, R, E])
        picked = sb("picked", [P, R, E], BF16)
        picked_n = sb("picked_n", [P, E])
        carry = sb("carry", [P, E], BF16)
        carry_f = sb("carry_f", [P, E])
        below = sb("below", [P, R, E])
        expin = sb("expin", [P, R, E])
        expo = sb("expo", [P, R, E])
        expsum = sb("expsum", [P, R])
        rsum = sb("rsum", [P, R])
        slotrow = sb("slotrow", [P, R, E])
        pickrow = sb("pickrow", [P, TOPK, R, E])
        slot_f = sb("slot_f", [P, TOPK, R])
        slot = sb("slot", [P, TOPK * R], U32)
        token_rows = sb("token_rows", [P, R, TOPK, ROW])
        pad_rows = sb("pad_rows", [P, ROW])
        count = sb("count", [1, E])
        cmp_level = sb("cmp_level", [1, E, TOK // P])
        tiles = sb("tiles", [1, E])
        tiles_end = sb("tiles_end", [1, E])
        q_free = q_all[:, :, :].rearrange("p b n -> p (b n)")
        hid_free = hidT[:, :, :].rearrange("p c n -> p (c n)")
        past = q_free[0:1, 0:NT * E].rearrange("p (t e) -> p t e", t=NT)
        past_tiles = q_free[0:1, NT * E:2 * NT * E].rearrange("p (t e) -> p t e", t=NT)
        tab = sb("tab", [1, 6, NT])
        pad_f = sb("pad_f", [1, E])
        pad_at = sb("pad_at", [1, E], I32)
        tile_row = sb("tile_row", [1, NT], I32)
        tile_expert = sb("tile_expert", [1, NT], I32)
        slots_in = [token_rows[:, s_, 0, :] for s_ in range(UN)]
        xT = [sb(f"xT{s}", [P, P]) for s in range(2)]
        act_g = [hid_free[:, s_ * HM:(s_ + 1) * HM] for s_ in range(2)]
        hid = [hid_free[:, (2 + s_) * HM:(3 + s_) * HM] for s_ in range(2)]
        hT = [sb(f"hT{s}", [P, HC * P]) for s in range(2)]
        y_sb = [sb(f"y_sb{s}", [P, D]) for s in range(UN)]
        pair_in = [[q_free[:, (TOPK * j + k) * GN:(TOPK * j + k + 1) * GN] for k in range(TOPK)] for j in range(G)]
        res = [q_free[:, (TOPK * G + j) * GN:(TOPK * G + j + 1) * GN] for j in range(G)]

        banks = [ctx.enter_context(nc.psum_tensor(f"bank{i}", [P, 512], F32)) for i in range(8)]
        trb, kb, vb, qb, kvb = banks[0:2], banks[2], banks[3], banks[4], banks[5]
        ta, tl, wb, ob, fb, nb = banks[0], banks[1], banks[2], banks[3], banks[4:6], banks[6:8]
        SC0 = 2 * NKV
        xtb, gb_, vb_, htb, yb = banks[0], banks[1], banks[2], banks[4], banks[5]

        S = {}

        def s(name):
            if name not in S:
                S[name] = sem(name)
            return S[name]

        STARTED = {"normed_copied", "normed_T", "exp_done", "rank_mm", "gates_ready"}

        def ge(eng, name, value):
            if isinstance(value, int) and value <= 0:
                return
            eng.wait_ge(s(name), value + (name in STARTED))

        def ge_apart(eng, name, value, passed):
            ge(eng, name, value)
            if not isinstance(value, int):
                eng.sem_inc(s(passed), 1)

        for name in ("sp_passed", "pool_passed", "dve_passed", "in_c", "in_vec", "in_x0", "in_x1", "in_x2", "in_x3", "in_w", "in_w2", "in_exp",
                     "k_const", "pool_const", "silu_done", "silu_rows", "mod_mm", "mod_hi", "mod_lo", "mod_ready", "gate_step",
                     "x_raw", "x_stats", "x_ve", "x_rstd", "xhat_ready", "scaled_ready", "h_ready", "h_raw", "h_stats",
                     "h_ve", "h_rstd", "unit1_ready", "unit1_T", "ln1_ready", "k_mm", "v_mm", "q_mm",
                     "kfeat_ready", "v_ready", "q_ready", "kvs_mm", "kvs_ready",
                     "qf0", "qf1", "num_mm", "rden_ready", "att_ready", "att_T", "attT_ready", "wo_mm", "add1_ready",
                     "a_raw", "a_stats", "a_ve", "a_rstd", "gx_half", "gx_ready", "unit2_ready", "unit2_T", "ln2_ready",
                     "ff1_mm", "hid_ready", "ff2_mm", "ffn_ready", "gate_mm", "x2_ready", "y_raw", "y_stats",
                     "y_ve", "y_rstd", "yhat_ready", "yscaled", "h3_ready", "square_done", "ms_ready", "rms_ready", "normed_ready",
                     "normed_copied", "normed_T", "xn_ready", "score_mm", "score_ready", "top_ready", "topix_ready", "topf_ready", "onehot_ready",
                     "picked_ready", "pickedn_ready", "carry_ready", "below_ready", "rank_mm", "expin_ready", "exp_done", "expsum_ready", "rsum_ready",
                     "gates_ready", "dest_ready", "slotrow_ready", "pickrow_ready", "slotf_ready", "slot_ready", "scattered",
                     "count_mm", "tab_step", "pads_ready", "tables_ready", "pads_written",
                     "z_scaled", "z_ready",
                     *(f"in_s{u}" for u in range(UN)), "x_T", "xT_ready", "g_mm", "g_ready", "v2_mm", "hid2_ready",
                     "hid_T", "hT_ready", "y_mm", "y_ready", *(f"out_s{u}" for u in range(UN)),
                     "pair0", "pair1", "pairsum", "pairgate", "res_ready", "stored0", "stored1"):
            s(name)

        block = ctx.enter_context(nc.Block())

        def batch(t, b):
            return t[:, b, :] if isinstance(b, int) else t[:, bass.ds(b, 1), :].rearrange("p a n -> p (a n)")

        def group(t, b, j):
            return t[:, b, j * GN:(j + 1) * GN] if isinstance(b, int) else \
                t[:, bass.ds(b, 1), j * GN:(j + 1) * GN].rearrange("p a n -> p (a n)")

        def tile(t, b, r):
            return t[:, b, r * D:(r + 1) * D] if isinstance(b, int) else \
                t[:, bass.ds(b, 1), r * D:(r + 1) * D].rearrange("p a n -> p (a n)")

        def mod_rows(b, which):
            m = mod[:, b, which, :] if isinstance(b, int) else \
                mod[:, bass.ds(b, 1), which, :].rearrange("p a n -> p (a n)")
            return m.unsqueeze(1).to_broadcast([P, GT, D])

        def by_tile(ap):
            return ap.rearrange("p (t d) -> p t d", t=GT)

        @block.sync
        def _(sp):
            for name in ("normed_copied",):
                sp.sem_inc(s(name), 1)
            xv = x.rearrange("b (p r) d -> b p (r d)", p=P)
            sp.dma_start(cT[:, :], c_t).then_inc(s("in_c"), 16)
            sp.dma_start(x_all[:, 0, :], xv[0]).then_inc(s("in_x0"), 16)
            sp.dma_start(wmod_sb[:, :], wmod).then_inc(s("in_c"), 16)
            sp.dma_start(vec[:, :], vecs).then_inc(s("in_vec"), 16)
            for t, w in ((wk_sb, wk), (wv_sb, wv), (wq_sb, wq)):
                sp.dma_start(t[:, :], w).then_inc(s("in_w"), 16)
            for b in range(1, B):
                sp.dma_start(x_all[:, b, :], xv[b]).then_inc(s(f"in_x{b}"), 16)
            sp.dma_start(wo_sb[:, :], wo).then_inc(s("in_w2"), 16)
            sp.dma_start(w1_sb[:, :], w1).then_inc(s("in_w2"), 16)
            sp.dma_start(w2_sb[:, :, :], w2.rearrange("(c p) e -> p c e", p=P)).then_inc(s("in_w2"), 16)
            sp.wait_ge(s("pool_const"), 1)
            sp.dma_start(wr_sb[:, 0:E], wr_t).then_inc(s("in_w2"), 16)
            sp.dma_start(up_sb[:, :, :].rearrange("p e n -> p (e n)"), w_up.rearrange("p e n -> p (e n)")).then_inc(s("in_exp"), 16)
            for c in range(HC):
                n = min(P, HM - c * P)
                sp.dma_start(down_sb[0:n, :, c * D:(c + 1) * D], w_down[c * P:c * P + n]).then_inc(s("in_exp"), 16)

            def load_q(b, j):
                ge_apart(sp, "q_ready", G * b + j + 1, "sp_passed")
                ge_apart(sp, "num_mm", G * (b - 1) + j + 1, "sp_passed")
                sp.dma_start(qf[j][:, :], group(q_all, b, j)).then_inc(s(f"qf{j}"), 16)

            def copy_normed(b, j):
                ge_apart(sp, "normed_ready", G * b + j + 1, "sp_passed")
                if j == 0:
                    ge_apart(sp, "scattered", 16 * TOPK * R * b, "sp_passed")
                for k in range(TOPK):
                    sp.dma_start(token_rows[:, j * GT:(j + 1) * GT, k, 0:D], by_tile(normed[j][:, :])).then_inc(s("normed_copied"), 16)
                ge_apart(sp, "normed_copied", 32 * (G * b + j + 1), "sp_passed")

            for j in range(G):
                load_q(0, j)

            def a2(b, has_before, has_after):
                if has_before:
                    copy_normed(b - 1, 1)
                if has_after:
                    for j in range(G):
                        load_q(b + 1, j)
                copy_normed(b, 0)

            a2(0, False, True)
            with sp.Fori(1, B - 1) as b:
                a2(b, True, True)
            a2(B - 1, True, False)
            copy_normed(B - 1, 1)

            sp.wait_ge(s("pads_ready"), 1)
            for e in range(E):
                at = sp.value_load(pad_at[0:1, e:e + 1], min_val=0, max_val=E * CAP - P)
                sp.dma_start(rows_dram[bass.ds(at, P), :], pad_rows[:, :]).then_inc(s("pads_written"), 16)
            sp.wait_ge(s("pads_written"), 16 * E)
            ge(sp, "scattered", 16 * TOPK * R * B)
            sp.wait_ge(s("tables_ready"), 1)

            def load_slots(i, first):
                t = tile_row[0:1, 0:UN] if first else tile_row[0:1, bass.ds(UN * i, UN)]
                rows = nc.values_load_multi_w_load_instructions(
                    t, [mybir.EngineType.SP], min_val=0, max_val=E * CAP - P,
                    skip_runtime_bounds_check_because="the table is made above, within these bounds")[1]
                for u in range(UN):
                    if not first:
                        ge_apart(sp, f"out_s{u}", 16 * i, "sp_passed")
                    sp.dma_start(slots_in[u][:, :], rows_dram[bass.ds(rows[u], P), :]).then_inc(s(f"in_s{u}"), 16)

            load_slots(0, True)
            with sp.Fori(1, NT // UN) as i:
                load_slots(i, False)

            for u in range(UN):
                ge(sp, f"out_s{u}", 16 * (NT // UN))
            pv = pair_dram.rearrange("(k b p r) d -> k b p (r d)", k=TOPK, b=B, p=P)
            ov = out.rearrange("b (p r) d -> b p (r d)", p=P)

            def ds(b):
                return bass.ds(b, 1)

            def fetch(b, j):
                ge(sp, "pairsum", G * (b - 1) + j + 1)
                for k in range(TOPK):
                    sp.dma_start(pair_in[j][k][:, :],
                                 pv[k, ds(b), :, j * GN:(j + 1) * GN].rearrange("a p n -> p (a n)")).then_inc(s(f"pair{j}"), 16)

            def store(b, j):
                ge(sp, "res_ready", G * b + j + 1)
                sp.dma_start(ov[ds(b), :, j * GN:(j + 1) * GN].rearrange("a p n -> p (a n)"), res[j][:, :]).then_inc(s(f"stored{j}"), 16)

            for j in range(G):
                fetch(0, j)
            with sp.Fori(1, B) as b:
                for j in range(G):
                    fetch(b, j)
                    store(b - 1, j)
            for j in range(G):
                store(B - 1, j)
            for j in range(G):
                sp.wait_ge(s(f"stored{j}"), 16 * B)

        @block.gpsimd
        def _(pool):
            n = [0]

            def step(ins):
                n[0] += 1
                ins.then_inc(s("k_const"), 1)
                pool.wait_ge(s("k_const"), n[0])

            pool.memset(wr_sb[:, :], 0.0).then_inc(s("pool_const"), 1)
            pool.memset(neg_half[:, :], -0.5)
            step(pool.memset(ident[:, :], 0.0))
            step(pool.affine_select(out=ident[:, :], in_=ident[:, :], compare_op=ALU.not_equal, fill=1.0, base=0,
                                    pattern=[[-1, P]], channel_multiplier=1))
            pool.memset(ones[:, :], 1.0)
            pool.memset(before[:, :], 1.0)
            for j in range(G):
                pool.memset(vones[j][:, :, D:D + 1], 1.0)
            pool.memset(pad_rows[:, :], 0.0)
            step(pool.memset(same_head[:, :], 1.0))
            step(pool.affine_select(out=before[:, :], in_=before[:, :], compare_op=ALU.is_gt, fill=0.0, base=0,
                                    pattern=[[1, P]], channel_multiplier=-1))
            for cols, reps in ((same_head[:, 0:D], [0, DH]), (same_head[:, D:NKV], [0, 1])):
                v = cols.rearrange("p (h d) -> p h d", h=H)
                step(pool.affine_select(out=v, in_=v, compare_op=ALU.is_ge, fill=0.0, base=0,
                                        pattern=[[-DH, H], reps], channel_multiplier=1))
                step(pool.affine_select(out=v, in_=v, compare_op=ALU.is_ge, fill=0.0, base=DH - 1,
                                        pattern=[[DH, H], reps], channel_multiplier=-1))
            pool.iota(pad_rows[:, DEST:DEST + 1].bitcast(I32), pattern=[[0, 1]], base=NOWHERE, channel_multiplier=1)
            pool.iota(expert_no[:, :], pattern=[[1, E]], base=0, channel_multiplier=0, allow_small_or_imprecise_dtypes=True)
            pool.iota(region[:, :], pattern=[[CAP, E]], base=0, channel_multiplier=0, allow_small_or_imprecise_dtypes=True)
            pool.iota(tile_no[:, :], pattern=[[1, NT]], base=0, channel_multiplier=0, allow_small_or_imprecise_dtypes=True)
            pool.iota(level[:, :], pattern=[[P, TOK // P]], base=0, channel_multiplier=0, allow_small_or_imprecise_dtypes=True)
            step(pool.iota(dest_all[:, :, :, :], pattern=[[L, B], [1, R], [TOK, TOPK]], base=0, channel_multiplier=R))
            pool.memset(square[0:1, 0:1], 0.0).then_inc(s("pool_const"), 1)

            def rsqrt(name, mv, ve, rs, eps, g):
                ge_apart(pool, f"{name}_stats", g + 1, "pool_passed")
                pool.tensor_scalar(ve[:, :], mv[:, :, 1], eps, None, ALU.add).then_inc(s(f"{name}_ve"), 1)
                ge(pool, f"{name}_ve", g + 1)
                pool.tensor_tensor(rs[:, :], ve[:, :], neg_half[:, :], ALU.pow).then_inc(s(f"{name}_rstd"), 1)

            def scale_x(b, j):
                ge_apart(pool, "xhat_ready", G * b + j + 1, "pool_passed")
                pool.tensor_tensor(by_tile(scaled[j][:, :]), by_tile(xhat[j][:, :]), mod_rows(b, MOD_SCALE_A), ALU.mult)\
                    .then_inc(s("scaled_ready"), 1)

            def a1(b, last):
                for j in range(G):
                    scale_x(b, j)
                    if not (last and j == G - 1):
                        nj = (j + 1) % G
                        rsqrt("x", *st_x[nj][1:], EPS_OUT, G * b + j + 1)
                    rsqrt("h", *st_h[j][1:], EPS_IN, G * b + j)

            rsqrt("x", *st_x[0][1:], EPS_OUT, 0)
            pool.wait_ge(s("mod_ready"), 1)
            a1(0, False)
            with pool.Fori(1, B - 1) as b:
                a1(b, False)
            a1(B - 1, True)

            def gate_add(b, j):
                ge(pool, "add1_ready", G * b + j + 1)
                ge_apart(pool, "x2_ready", G * (b - 1) + j + 1, "pool_passed")
                pool.tensor_tensor(by_tile(gx[j][:, :]), by_tile(add1[j][:, :]), mod_rows(b, MOD_GATE_A), ALU.mult)\
                    .then_inc(s("gx_half"), 1)
                ge_apart(pool, "gx_half", G * b + j + 1, "pool_passed")
                pool.tensor_tensor(gx[j][:, :], gx[j][:, :], group(x_all, b, j), ALU.add).then_inc(s("gx_ready"), 1)

            def rms_rsqrt(b, j):
                g = G * b + j
                ge_apart(pool, "square_done", GT * (g + 1), "pool_passed")
                pool.tensor_scalar(ms_eps[j][:, :], sumsq[j][:, :], 1.0 / D, EPS_IN, ALU.mult, ALU.add).then_inc(s("ms_ready"), 1)
                ge(pool, "ms_ready", g + 1)
                pool.tensor_tensor(rms[j][:, :], ms_eps[j][:, :], neg_half[:, :], ALU.pow).then_inc(s("rms_ready"), 1)

            def scatter(b, part):
                ge(pool, "slot_ready", b + 1)
                ge(pool, "dest_ready", b + 1)
                ge(pool, "gates_ready", b + 1)
                ge_apart(pool, "normed_copied", 32 * G * (b + 1), "pool_passed")
                for n_ in range(part * 4, part * 4 + 4):
                    r, k = n_ % R, n_ // R
                    pool.indirect_dma_start(rows_dram, bass.IndirectOffsetOnAxis(ap=slot[:, n_:n_ + 1], axis=0),
                                            token_rows[:, r, k, :], None, bounds_check=E * CAP - 1,
                                            oob_is_err=False).then_inc(s("scattered"), 16)

            def head(b, j):
                rsqrt("a", *st_a[j][1:], EPS_IN, G * b + j)
                gate_add(b, j)

            head(0, 0)
            head(0, 1)

            def a2(b, has_before, has_after):
                if has_after:
                    head(b + 1, 0)
                rsqrt("y", *st_y[0][1:], EPS_OUT, G * b)
                if has_before:
                    scatter(b - 1, 0)
                rms_rsqrt(b, 0)
                if has_before:
                    scatter(b - 1, 1)
                if has_after:
                    head(b + 1, 1)
                if has_before:
                    scatter(b - 1, 2)
                rsqrt("y", *st_y[1][1:], EPS_OUT, G * b + 1)
                rms_rsqrt(b, 1)
                if has_before:
                    scatter(b - 1, 3)

            a2(0, False, True)
            with pool.Fori(1, B - 1) as b:
                a2(b, True, True)
            a2(B - 1, True, False)
            for part in range(4):
                scatter(B - 1, part)

            def send(i, u):
                ge_apart(pool, "y_ready", UN * i + u + 1, "pool_passed")
                pool.indirect_dma_start(pair_dram, bass.IndirectOffsetOnAxis(ap=slots_in[u][:, DEST:DEST + 1].bitcast(U32), axis=0),
                                        y_sb[u][:, :], None, bounds_check=TOPK * TOK - 1,
                                        oob_is_err=False).then_inc(s(f"out_s{u}"), 16)

            with pool.Fori(0, NT // UN) as i:
                for u in range(UN):
                    send(i, u)

        @block.scalar
        def _(act):
            for name in ("exp_done",):
                act.sem_inc(s(name), 1)
            gamma, beta = vec[:, GAMMA:GAMMA + 1], vec[:, BETA:BETA + 1]
            act.wait_ge(s("in_c"), 32)
            act.activation(silu_c[:, :], cT[:, :], ACT.Silu).then_inc(s("silu_done"), 1)
            act.wait_ge(s("mod_mm"), 1)
            for b in range(B):
                act.activation(mod[:, b, 0:4, :].rearrange("p a d -> p (a d)"), banks[b][:, :], ACT.Copy).then_inc(s("mod_lo"), 1)
            act.wait_ge(s("in_vec"), 16)

            def a1(b):
                for j in range(G):
                    g = G * b + j
                    ge(act, "unit1_T", g + 1)
                    ge(act, "k_mm", g - 1)
                    ge(act, "v_mm", g - 1)
                    ge(act, "q_mm", g - 1)
                    act.activation(ln1T[j][:, :], trb[j][:, :], ACT.Identity, bias=beta, scale=gamma).then_inc(s("ln1_ready"), 1)
                    ge(act, "v_mm", g + 1)
                    ge(act, "kvs_mm", g - 1)
                    act.activation(vones[j][:, :, 0:D], by_tile(vb[:, :]), ACT.Copy).then_inc(s("v_ready"), 1)

            a1(0)
            with act.Fori(1, B) as b:
                a1(b)

            def att_out(b, j):
                ge(act, "att_T", G * b + j + 1)
                ge(act, "wo_mm", G * b + j)
                act.activation(attT[:, :], ta[:, :], ACT.Copy).then_inc(s("attT_ready"), 1)

            def ln2_out(b, j):
                ge(act, "unit2_T", G * b + j + 1)
                ge(act, "ff1_mm", FC * (G * (b - 1) + j + 1))
                act.activation(ln2T[j][:, :], tl[:, :], ACT.Identity, bias=beta, scale=gamma).then_inc(s("ln2_ready"), 1)

            def gelu1(b, j):
                g = G * b + j
                for c in range(FC):
                    ge(act, "ff1_mm", FC * g + c + 1)
                    if c == 0:
                        ge(act, "ff2_mm", g)
                    act.activation(hidT[:, c, :], fb[c % 2][:, :], ACT.Gelu, bias=vec[:, BIAS1 + c:BIAS1 + c + 1]).then_inc(s("hid_ready"), 1)

            def gelu2(b, j):
                g = G * b + j
                ge(act, "ff2_mm", g + 1)
                ge(act, "gate_mm", g - 1)
                act.activation(ffnT[j][:, :], ob[:, :], ACT.Gelu, bias=vec[:, BIAS2:BIAS2 + 1]).then_inc(s("ffn_ready"), 1)

            def squares(b, j):
                g = G * b + j
                ge(act, "h3_ready", g + 1)
                ge(act, "ms_ready", g - 1)
                for t in range(GT):
                    ge(act, "square_done", GT * g + t)
                    act.activation(square[:, :], tile(h_all, b, j * GT + t), ACT.Square,
                                   accum_out=sumsq[j][:, t:t + 1]).then_inc(s("square_done"), 1)

            def xn_out(b, j):
                ge(act, "normed_T", G * b + j + 1)
                act.activation(xnT[j][:, :], (ta if j == 0 else tl)[:, :], ACT.Copy, scale=vec[:, NSCALE:NSCALE + 1]).then_inc(s("xn_ready"), 1)

            def exps(b):
                ge(act, "expin_ready", b + 1)
                ge(act, "gates_ready", b)
                act.activation(expo[:, :, :], expin[:, :, :], ACT.Exp).then_inc(s("exp_done"), 1)

            def a2(b, has_before, has_after):
                gelu1(b, 0)
                ln2_out(b, 1)
                gelu2(b, 0)
                if has_after:
                    att_out(b + 1, 0)
                if has_before:
                    xn_out(b - 1, 0)
                    xn_out(b - 1, 1)
                gelu1(b, 1)
                if has_before:
                    exps(b - 1)
                if has_after:
                    ln2_out(b + 1, 0)
                gelu2(b, 1)
                squares(b, 0)
                if has_after:
                    att_out(b + 1, 1)
                squares(b, 1)

            att_out(0, 0)
            ln2_out(0, 0)
            att_out(0, 1)
            a2(0, False, True)
            with act.Fori(1, B - 1) as b:
                a2(b, True, True)
            a2(B - 1, True, False)
            xn_out(B - 1, 0)
            xn_out(B - 1, 1)
            exps(B - 1)

            def silu(j, p):
                ge(act, "g_mm", j + 1)
                ge(act, "hid2_ready", j - 1)
                act.activation(act_g[p][:, :], gb_[:, 0:HM], ACT.Silu).then_inc(s("g_ready"), 1)

            def hidden_out(j, p):
                ge(act, "hid_T", j + 1)
                ge(act, "y_mm", j - 1)
                act.activation(hT[p][:, 0:(HC - 1) * P], htb[:, 0:(HC - 1) * P], ACT.Copy).then_inc(s("hT_ready"), 1)
                act.activation(hT[p][0:LASTH, (HC - 1) * P:], htb[0:LASTH, (HC - 1) * P:HC * P], ACT.Copy).then_inc(s("hT_ready"), 1)

            def b_step(j, u, one_before):
                if one_before:
                    hidden_out(j - 1, (u + 1) % 2)
                silu(j, u % 2)

            for u in range(UN):
                b_step(u, u, u >= 1)
            with act.Fori(1, NT // UN) as i:
                for u in range(UN):
                    b_step(UN * i + u, u, True)
            hidden_out(NT - 1, 1)

        @block.vector
        def _(dve):
            for name in ("gates_ready",):
                dve.sem_inc(s(name), 1)
            dve.wait_ge(s("silu_done"), 1)
            dve.tensor_copy(silu_cb[:, :, :], silu_c[:, :].unsqueeze(2).to_broadcast([P, B, P])).then_inc(s("silu_rows"), 1)

            def norm_stats(name, st, src, g):
                for t in range(GT):
                    ins = dve.bn_stats(st[0][:, t, :], src[t])
                ins.then_inc(s(f"{name}_raw"), 1)
                ge_apart(dve, f"{name}_raw", g + 1, "dve_passed")
                for t in range(GT):
                    ins = dve.bn_aggr(st[1][:, t, :], st[0][:, t, :])
                ins.then_inc(s(f"{name}_stats"), 1)

            def normalise(name, st, src, dst, done, g):
                ge(dve, f"{name}_rstd", g + 1)
                for t in range(GT):
                    ins = dve.tensor_scalar(dst[:, t * D:(t + 1) * D], src[t], st[1][:, t, 0:1], st[3][:, t:t + 1],
                                            ALU.subtract, ALU.mult)
                ins.then_inc(s(done), 1)

            def x_tiles(b, j):
                return [tile(x_all, b, j * GT + t) for t in range(GT)]

            def h_tiles(b, j):
                return [tile(h_all, b, j * GT + t) for t in range(GT)]

            dve.wait_ge(s("in_x0"), 16)
            norm_stats("x", st_x[0], x_tiles(0, 0), 0)
            dve.wait_ge(s("mod_mm"), 1)
            for b in range(B):
                dve.tensor_copy(mod[:, b, 4:6, :].rearrange("p a d -> p (a d)"), banks[B + b][:, 0:2 * D]).then_inc(s("mod_hi"), 1)
            dve.wait_ge(s("mod_hi"), B)
            dve.wait_ge(s("mod_lo"), B)
            for m in (MOD_SCALE_A, MOD_SCALE_B):
                ins = dve.tensor_scalar(mod[:, :, m, :], mod[:, :, m, :], 1.0, None, ALU.add)
            ins.then_inc(s("mod_ready"), 1)
            for n_, m in enumerate((MOD_GATE_A, MOD_GATE_B)):
                v, sign = mod[:, :, m, :], gate_sign[:, :, n_, :]
                dve.tensor_scalar(sign, v, 0.0, 0.5, ALU.is_ge, ALU.subtract).then_inc(s("gate_step"), 1)
                dve.wait_ge(s("gate_step"), 4 * n_ + 1)
                dve.tensor_tensor(v, v, sign, ALU.mult).then_inc(s("gate_step"), 1)
                dve.wait_ge(s("gate_step"), 4 * n_ + 2)
                dve.tensor_scalar(v, v, 0.125, 4.0, ALU.max, ALU.mult).then_inc(s("gate_step"), 1)
                dve.wait_ge(s("gate_step"), 4 * n_ + 3)
                dve.tensor_tensor(v, v, sign, ALU.mult).then_inc(s("gate_step"), 1)
            dve.wait_ge(s("gate_step"), 8)
            dve.wait_ge(s("pool_const"), 2)
            dve.tensor_tensor(gate_diag[:, :, :], mod[:, :, MOD_GATE_A, :], ident[:, :].unsqueeze(1).to_broadcast([P, B, P]),
                              ALU.mult).then_inc(s("mod_ready"), 1)
            dve.memset(carry[:, :], 0.0)
            dve.memset(carry_f[:, :], 0.0).then_inc(s("carry_ready"), 1)

            def features(b, j):
                g = G * b + j
                ge(dve, "k_mm", g + 1)
                ge(dve, "kvs_mm", g - 1)
                dve.tensor_scalar(kfeat[j][:, :], kb[:, :], 0.0, STAB, ALU.max, ALU.add).then_inc(s("kfeat_ready"), 1)
                ge(dve, "q_mm", g + 1)
                dve.tensor_scalar(group(q_all, b, j), qb[:, :], 0.0, STAB, ALU.max, ALU.add).then_inc(s("q_ready"), 1)

            def keep_kvs(b):
                ge(dve, "kvs_mm", G * (b + 1))
                kv = batch(kvs_all, b)
                dve.tensor_tensor(kv[:, 0:D], kvb[:, 0:D], same_head[:, 0:D], ALU.mult)
                dve.tensor_scalar(kv[:, D:NKV], same_head[:, D:NKV], kvb[:, D:D + 1], None, ALU.mult).then_inc(s("kvs_ready"), 1)

            def a1(b, first, last):
                for j in range(G):
                    g = G * b + j
                    normalise("x", st_x[j], x_tiles(b, j), xhat[j], "xhat_ready", g)
                    if not (last and j == G - 1):
                        nb_, nj = (b, 1) if j == 0 else (b + 1, 0)
                        norm_stats("x", st_x[nj], x_tiles(nb_, nj), g + 1)
                    ge(dve, "scaled_ready", g + 1)
                    dve.tensor_tensor(by_tile(group(h_all, b, j)), by_tile(scaled[j][:, :]), mod_rows(b, MOD_SHIFT_A), ALU.add)\
                        .then_inc(s("h_ready"), 1)
                    ge_apart(dve, "h_ready", g + 1, "dve_passed")
                    norm_stats("h", st_h[j], h_tiles(b, j), g)
                    if not (first and j == 0):
                        pb, pj = (b, 0) if j == 1 else (b - 1, 1)
                        features(pb, pj)
                    normalise("h", st_h[j], h_tiles(b, j), unit1[j], "unit1_ready", g)
                    if j == 0 and not first:
                        keep_kvs(b - 1)

            for b in range(1, B):
                dve.wait_ge(s(f"in_x{b}"), 16)
            a1(0, True, False)
            with dve.Fori(1, B - 1) as b:
                a1(b, False, False)
            a1(B - 1, False, True)
            features(B - 1, 1)
            keep_kvs(B - 1)

            def attend(b, j):
                g = G * b + j
                ge(dve, "num_mm", g + 1)
                for h in range(2):
                    v = nb[h][:, 0:2 * NKV].rearrange("p (t n) -> p t n", t=2)
                    ins = dve.reciprocal(rden[j][:, 2 * h:2 * h + 2, :], v[:, :, D:NKV])
                ins.then_inc(s("rden_ready"), 1)
                ge(dve, "rden_ready", g + 1)
                for h in range(2):
                    v = nb[h][:, 0:2 * NKV].rearrange("p (t n) -> p t n", t=2)[:, :, 0:D]
                    ins = dve.tensor_tensor(
                        att[j][:, 2 * h * D:(2 * h + 2) * D].rearrange("p (t h d) -> p t h d", t=2, h=H),
                        v.rearrange("p t (h d) -> p t h d", h=H),
                        rden[j][:, 2 * h:2 * h + 2, :].unsqueeze(3).to_broadcast([P, 2, H, DH]), ALU.mult)
                ins.then_inc(s("att_ready"), 1)

            def residual(b, j):
                g = G * b + j
                ge(dve, "wo_mm", g + 1)
                ge(dve, "gx_ready", g - 1)
                dve.tensor_tensor(add1[j][:, :], wb[:, :], group(h_all, b, j), ALU.add).then_inc(s("add1_ready"), 1)
                ge(dve, "add1_ready", g + 1)
                norm_stats("a", st_a[j], [add1[j][:, t * D:(t + 1) * D] for t in range(GT)], g)

            def unit(b, j):
                g = G * b + j
                ge(dve, "unit2_T", g - 1)
                normalise("a", st_a[j], [add1[j][:, t * D:(t + 1) * D] for t in range(GT)], unit2[j], "unit2_ready", g)

            def first_sum(b, j):
                g = G * b + j
                ge(dve, "gate_mm", g + 1)
                ge(dve, "gx_ready", g + 1)
                dve.tensor_tensor(group(x_all, b, j), wb[:, :], gx[j][:, :], ALU.add).then_inc(s("x2_ready"), 1)
                ge_apart(dve, "x2_ready", g + 1, "dve_passed")
                norm_stats("y", st_y[j], x_tiles(b, j), g)

            def modulate(b, j):
                g = G * b + j
                normalise("y", st_y[j], x_tiles(b, j), yhat, "yhat_ready", g)
                ge(dve, "yhat_ready", g + 1)
                dve.tensor_tensor(by_tile(yhat[:, :]), by_tile(yhat[:, :]), mod_rows(b, MOD_SCALE_B), ALU.mult).then_inc(s("yscaled"), 1)
                ge(dve, "yscaled", g + 1)
                dve.tensor_tensor(by_tile(group(h_all, b, j)), by_tile(yhat[:, :]), mod_rows(b, MOD_SHIFT_B), ALU.add).then_inc(s("h3_ready"), 1)

            def rms_norm(b, j):
                g = G * b + j
                ge(dve, "rms_ready", g + 1)
                ge(dve, "normed_copied", 32 * (g - 1))
                ge(dve, "normed_T", g - 1)
                for t in range(GT):
                    ins = dve.tensor_scalar(normed[j][:, t * D:(t + 1) * D], tile(h_all, b, j * GT + t), rms[j][:, t:t + 1], None, ALU.mult)
                ins.then_inc(s("normed_ready"), 1)

            def choose(b):
                ge(dve, "score_mm", G * (b + 1))
                dve.tensor_copy(score[:, :, :], nb[0][:, SC0:SC0 + R * E].rearrange("p (r e) -> p r e", e=E)).then_inc(s("score_ready"), 1)
                ge_apart(dve, "score_ready", b + 1, "dve_passed")
                for r in range(R):
                    ins = dve.max(top[:, r, :], score[:, r, :])
                ins.then_inc(s("top_ready"), 1)
                ge_apart(dve, "top_ready", b + 1, "dve_passed")
                for r in range(R):
                    ins = dve.max_index(top_ix[:, r, :], top[:, r, :], score[:, r, :])
                ins.then_inc(s("topix_ready"), 1)
                ge(dve, "exp_done", b)
                dve.tensor_tensor(expin[:, :, :], top[:, :, :], top[:, :, 0:1].to_broadcast([P, R, E]), ALU.subtract).then_inc(s("expin_ready"), 1)
                ge(dve, "topix_ready", b + 1)
                dve.tensor_copy(top_f[:, :, :], top_ix[:, :, 0:TOPK].rearrange("p r k -> p k r")).then_inc(s("topf_ready"), 1)
                ge(dve, "topf_ready", b + 1)
                dve.tensor_tensor(onehot[:, :, :, :].rearrange("p k r e -> p (k r) e"),
                                  top_f[:, :, :].rearrange("p k r -> p (k r)").unsqueeze(2).to_broadcast([P, TOPK * R, E]),
                                  expert_no[:, :].unsqueeze(1).to_broadcast([P, TOPK * R, E]), ALU.is_equal).then_inc(s("onehot_ready"), 1)
                ge(dve, "onehot_ready", b + 1)
                ge(dve, "rank_mm", b)
                dve.tensor_tensor(picked[:, :, :], onehot[:, 0, :, :], onehot[:, 1, :, :], ALU.add).then_inc(s("picked_ready"), 1)

            def place(b):
                ge(dve, "rank_mm", b + 1)
                dve.tensor_tensor(slotrow[:, :, :], nb[1][:, SC0:SC0 + R * E].rearrange("p (r e) -> p r e", e=E),
                                  region[:, :].unsqueeze(1).to_broadcast([P, R, E]), ALU.add).then_inc(s("slotrow_ready"), 1)
                dve.tensor_reduce(picked_n[:, :], picked[:, :, :].rearrange("p r e -> p e r"), AX.X, ALU.add).then_inc(s("pickedn_ready"), 1)
                ge(dve, "slotrow_ready", b + 1)
                for k in range(TOPK):
                    ins = dve.tensor_tensor(pickrow[:, k, :, :], onehot[:, k, :, :], slotrow[:, :, :], ALU.mult)
                ins.then_inc(s("pickrow_ready"), 1)
                ge(dve, "pickedn_ready", b + 1)
                dve.tensor_tensor(carry_f[:, :], carry_f[:, :], picked_n[:, :], ALU.add).then_inc(s("below_ready"), 1)
                ge(dve, "pickrow_ready", b + 1)
                dve.tensor_reduce(slot_f[:, :, :].rearrange("p k r -> p (k r)"), pickrow[:, :, :, :].rearrange("p k r e -> p (k r) e"),
                                  AX.X, ALU.add).then_inc(s("slotf_ready"), 1)
                ge(dve, "below_ready", b + 1)
                dve.tensor_copy(carry[:, :], carry_f[:, :]).then_inc(s("carry_ready"), 1)
                ge(dve, "slotf_ready", b + 1)
                ge(dve, "normed_copied", 32 * G * (b + 1))
                dve.tensor_copy(slot[:, :], slot_f[:, :, :].rearrange("p k r -> p (k r)")).then_inc(s("slot_ready"), 1)
                ids = dest_all[:, b, :, :] if isinstance(b, int) else \
                    dest_all[:, bass.ds(b, 1), :, :].rearrange("p a r k -> p (a r) k")
                dve.tensor_copy(token_rows[:, :, :, DEST].bitcast(I32), ids).then_inc(s("dest_ready"), 1)
                ge(dve, "exp_done", b + 1)
                dve.tensor_reduce(expsum[:, :], expo[:, :, :], AX.X, ALU.add).then_inc(s("expsum_ready"), 1)
                ge(dve, "expsum_ready", b + 1)
                dve.reciprocal(rsum[:, :], expsum[:, :]).then_inc(s("rsum_ready"), 1)
                ge(dve, "rsum_ready", b + 1)
                dve.tensor_tensor(token_rows[:, :, :, GATE], expo[:, :, 0:TOPK], rsum[:, :].unsqueeze(2).to_broadcast([P, R, TOPK]),
                                  ALU.mult).then_inc(s("gates_ready"), 1)

            attend(0, 0)
            residual(0, 0)
            attend(0, 1)
            unit(0, 0)
            residual(0, 1)
            unit(0, 1)

            def a2(b, has_before, has_after):
                if has_before:
                    rms_norm(b - 1, 1)
                if has_after:
                    attend(b + 1, 0)
                if has_before:
                    choose(b - 1)
                if has_after:
                    residual(b + 1, 0)
                first_sum(b, 0)
                if has_after:
                    unit(b + 1, 0)
                if has_after:
                    attend(b + 1, 1)
                modulate(b, 0)
                if has_before:
                    place(b - 1)
                first_sum(b, 1)
                rms_norm(b, 0)
                if has_after:
                    residual(b + 1, 1)
                modulate(b, 1)
                if has_after:
                    unit(b + 1, 1)

            a2(0, False, True)
            with dve.Fori(1, B - 1) as b:
                a2(b, True, True)
            a2(B - 1, True, False)
            rms_norm(B - 1, 1)
            choose(B - 1)
            place(B - 1)

            m = [0]

            def step(ins):
                m[0] += 1
                ins.then_inc(s("tab_step"), 1)
                dve.wait_ge(s("tab_step"), m[0])

            dve.wait_ge(s("count_mm"), 1)
            step(dve.tensor_copy(count[:, :], nb[0][0:1, 0:E]))
            dve.tensor_tensor(pad_f[:, :], count[:, :], region[0:1, :], ALU.add)
            step(dve.tensor_tensor(cmp_level[:, :, :], count[:, :].unsqueeze(2).to_broadcast([1, E, TOK // P]),
                                   level[:, :].unsqueeze(1).to_broadcast([1, E, TOK // P]), ALU.is_gt))
            dve.tensor_copy(pad_at[:, :], pad_f[:, :]).then_inc(s("pads_ready"), 1)
            step(dve.tensor_reduce(tiles[:, :], cmp_level[:, :, :], AX.X, ALU.add))
            step(dve.tensor_copy(tiles_end[:, 0:1], tiles[:, 0:1]))
            for e in range(1, E):
                step(dve.tensor_tensor(tiles_end[:, e:e + 1], tiles_end[:, e - 1:e], tiles[:, e:e + 1], ALU.add))
            step(dve.tensor_tensor(past, tile_no[:, :].unsqueeze(2).to_broadcast([1, NT, E]),
                                   tiles_end[:, :].unsqueeze(1).to_broadcast([1, NT, E]), ALU.is_ge))
            step(dve.tensor_tensor(past_tiles, past, tiles[:, :].unsqueeze(1).to_broadcast([1, NT, E]), ALU.mult))
            expert, start, row, used, dummy, diff = range(6)
            step(dve.tensor_reduce(tab[:, expert, :], past, AX.X, ALU.add))
            step(dve.tensor_reduce(tab[:, start, :], past_tiles, AX.X, ALU.add))
            step(dve.tensor_scalar(tab[:, used, :], tab[:, expert, :], float(E), None, ALU.is_lt))
            step(dve.tensor_tensor(tab[:, diff, :], tile_no[:, :], tab[:, start, :], ALU.subtract))
            step(dve.tensor_scalar(tab[:, diff, :], tab[:, diff, :], float(P), None, ALU.mult))
            step(dve.tensor_scalar(tab[:, row, :], tab[:, expert, :], float(CAP), None, ALU.mult))
            step(dve.tensor_tensor(tab[:, row, :], tab[:, row, :], tab[:, diff, :], ALU.add))
            step(dve.tensor_scalar(tab[:, row, :], tab[:, row, :], pad_f[:, E - 1:E], None, ALU.subtract))
            step(dve.tensor_tensor(tab[:, row, :], tab[:, row, :], tab[:, used, :], ALU.mult))
            step(dve.tensor_scalar(tab[:, row, :], tab[:, row, :], pad_f[:, E - 1:E], None, ALU.add))
            step(dve.tensor_scalar(tab[:, expert, :], tab[:, expert, :], float(E - 1), None, ALU.min))
            dve.tensor_copy(tile_row[:, :], tab[:, row, :])
            dve.tensor_copy(tile_expert[:, :], tab[:, expert, :]).then_inc(s("tables_ready"), 1)

            def z(b):
                for j in range(G):
                    g = G * b + j
                    hv = group(h_all, b, j)
                    dve.tensor_tensor(by_tile(hv), by_tile(hv), mod_rows(b, MOD_GATE_B), ALU.mult).then_inc(s("z_scaled"), 1)
                    ge(dve, "z_scaled", g + 1)
                    dve.tensor_tensor(hv, hv, group(x_all, b, j), ALU.add).then_inc(s("z_ready"), 1)

            with dve.Fori(0, B) as b:
                z(b)

            def x_out(j, p):
                ge(dve, "x_T", j + 1)
                ge(dve, "v2_mm", j - 1)
                dve.tensor_scalar(xT[p][:, :], xtb[:, 0:P], vec[:, NSCALE:NSCALE + 1], None, ALU.mult).then_inc(s("xT_ready"), 1)

            def gated(j, p):
                ge(dve, "v2_mm", j + 1)
                ge(dve, "g_ready", j + 1)
                ge(dve, "hid_T", j - 1)
                dve.tensor_tensor(hid[p][:, :], vb_[:, 0:HM], act_g[p][:, :], ALU.mult).then_inc(s("hid2_ready"), 1)

            def y_out(j, u):
                ge(dve, "y_mm", j + 1)
                dve.tensor_scalar(y_sb[u][:, :], yb[:, 0:D], slots_in[u][:, GATE:GATE + 1], None, ALU.mult).then_inc(s("y_ready"), 1)

            def b_step(i, u):
                j = UN * i + u
                if u == 0:
                    x_out(j, 0)
                if not (isinstance(j, int) and j < 2):
                    y_out(j - 2, (u - 2) % UN)
                if u < UN - 1:
                    x_out(j + 1, (u + 1) % 2)
                gated(j, u % 2)

            for u in range(UN):
                b_step(0, u)
            with dve.Fori(1, NT // UN) as i:
                for u in range(UN):
                    b_step(i, u)
            y_out(NT - 2, UN - 2)
            y_out(NT - 1, UN - 1)

            def combine(b, j):
                g = G * b + j
                ge(dve, f"pair{j}", 32 * (b + 1))
                ge(dve, f"stored{j}", 16 * b)
                dve.tensor_tensor(res[j][:, :], pair_in[j][0][:, :], pair_in[j][1][:, :], ALU.add).then_inc(s("pairsum"), 1)
                ge(dve, "pairsum", g + 1)
                dve.tensor_tensor(by_tile(res[j][:, :]), by_tile(res[j][:, :]), mod_rows(b, MOD_GATE_B), ALU.mult).then_inc(s("pairgate"), 1)
                ge(dve, "pairgate", g + 1)
                dve.tensor_tensor(res[j][:, :], res[j][:, :], group(h_all, b, j), ALU.add).then_inc(s("res_ready"), 1)

            for j in range(G):
                combine(0, j)
            with dve.Fori(1, B) as b:
                for j in range(G):
                    combine(b, j)

        @block.tensor
        def _(pe):
            for name in ("normed_T", "rank_mm"):
                pe.sem_inc(s(name), 1)
            pe.wait_ge(s("silu_rows"), 1)
            for b in range(B):
                pe.matmul(banks[b][:, :], silu_cb[:, b, :], wmod_sb[:, 0:4 * D], start=True, stop=True)
                ins = pe.matmul(banks[B + b][:, 0:2 * D], silu_cb[:, b, :], wmod_sb[:, 4 * D:6 * D], start=True, stop=True)
            ins.then_inc(s("mod_mm"), 1)
            pe.wait_ge(s("in_w"), 48)
            pe.wait_ge(s("pool_const"), 2)
            pe.wait_ge(s("mod_lo"), B)
            pe.wait_ge(s("mod_hi"), B)

            def turn(bank, src, done):
                for t in range(GT):
                    ins = pe.transpose(bank[:, t * P:(t + 1) * P], src[:, t * P:(t + 1) * P], ident[:, :])
                ins.then_inc(s(done), 1)

            def kvs(b, j):
                g = G * b + j
                ge(pe, "kfeat_ready", g + 1)
                ge(pe, "v_ready", g + 1)
                if j == 0:
                    ge(pe, "kvs_ready", b)
                for t in range(GT):
                    ins = pe.matmul(kvb[:, 0:D + 1], kfeat[j][:, t * D:(t + 1) * D], vones[j][:, t, 0:D + 1],
                                    start=(j == 0 and t == 0), stop=(j == G - 1 and t == GT - 1))
                ins.then_inc(s("kvs_mm"), 1)

            def a1(b, first):
                for j in range(G):
                    g = G * b + j
                    ge(pe, "unit1_ready", g + 1)
                    ge(pe, "ln1_ready", g - 1)
                    turn(trb[j], unit1[j], "unit1_T")
                    if not (first and j == 0):
                        pb, pj = (b, 0) if j == 1 else (b - 1, 1)
                        kvs(pb, pj)
                    ge(pe, "ln1_ready", g + 1)
                    ge(pe, "kfeat_ready", g)
                    for t in range(GT):
                        ins = pe.matmul(kb[:, t * D:(t + 1) * D], ln1T[j][:, t * P:(t + 1) * P], wk_sb[:, :], start=True, stop=True)
                    ins.then_inc(s("k_mm"), 1)
                    ge(pe, "v_ready", g)
                    for t in range(GT):
                        ins = pe.matmul(vb[:, t * D:(t + 1) * D], ln1T[j][:, t * P:(t + 1) * P], wv_sb[:, :], start=True, stop=True)
                    ins.then_inc(s("v_mm"), 1)
                    ge(pe, "q_ready", g)
                    pe.matmul(qb[:, :], wq_sb[:, :], ln1T[j][:, :], start=True, stop=True).then_inc(s("q_mm"), 1)

            a1(0, True)
            with pe.Fori(1, B) as b:
                a1(b, False)
            kvs(B - 1, 1)

            pe.wait_ge(s("in_w2"), 64)

            def read_out(b, j):
                g = G * b + j
                ge(pe, f"qf{j}", 16 * (b + 1))
                ge(pe, "kvs_ready", b + 1)
                ge(pe, "att_ready", g)
                for t in range(GT):
                    c0 = (t % 2) * NKV
                    ins = pe.matmul(nb[t // 2][:, c0:c0 + NKV], qf[j][:, t * P:(t + 1) * P], batch(kvs_all, b), start=True, stop=True)
                ins.then_inc(s("num_mm"), 1)

            def att_turn(b, j):
                g = G * b + j
                ge(pe, "att_ready", g + 1)
                ge(pe, "attT_ready", g)
                turn(ta, att[j], "att_T")

            def project(b, j):
                g = G * b + j
                ge(pe, "attT_ready", g + 1)
                ge(pe, "add1_ready", g)
                if isinstance(b, int) and b == 0:
                    pass
                elif j == 0:
                    ge(pe, "x2_ready", G * (b - 1))
                else:
                    ge(pe, "x2_ready", G * b)
                for t in range(GT):
                    ins = pe.matmul(wb[:, t * D:(t + 1) * D], attT[:, t * P:(t + 1) * P], wo_sb[:, :], start=True, stop=True)
                ins.then_inc(s("wo_mm"), 1)

            def unit2_turn(b, j):
                g = G * b + j
                ge(pe, "unit2_ready", g + 1)
                ge(pe, "ln2_ready", g)
                turn(tl, unit2[j], "unit2_T")

            def ffn1(b, j):
                g = G * b + j
                ge(pe, "ln2_ready", g + 1)
                for c in range(FC):
                    ge(pe, "hid_ready", FC * g + c - 1)
                    pe.matmul(fb[c % 2][:, :], w1_sb[:, c * P:(c + 1) * P], ln2T[j][:, :], start=True, stop=True).then_inc(s("ff1_mm"), 1)

            def ffn2(b, j):
                g = G * b + j
                ge(pe, "ffn_ready", g)
                for c in range(FC):
                    ge(pe, "hid_ready", FC * g + c + 1)
                    ins = pe.matmul(ob[:, :], w2_sb[:, c, :], hidT[:, c, :], start=(c == 0), stop=(c == FC - 1))
                ins.then_inc(s("ff2_mm"), 1)

            def gate(b, j, after):
                g = G * b + j
                ge(pe, "ffn_ready", g + 1)
                ge(pe, "add1_ready", after)
                ge(pe, "x2_ready", g)
                dg = gate_diag[:, b, :] if isinstance(b, int) else gate_diag[:, bass.ds(b, 1), :].rearrange("p a n -> p (a n)")
                for t in range(GT):
                    ins = pe.matmul(wb[:, t * D:(t + 1) * D], ffnT[j][:, t * P:(t + 1) * P], dg, start=True, stop=True)
                ins.then_inc(s("gate_mm"), 1)

            def router(b, att_turns, ln2_turns):
                for j in range(G):
                    g = G * b + j
                    ge(pe, "normed_ready", g + 1)
                    bank = ta if j == 0 else tl
                    ge(pe, "attT_ready" if j == 0 else "ln2_ready", att_turns if j == 0 else ln2_turns)
                    turn(bank, normed[j], "normed_T")
                for j in range(G):
                    g = G * b + j
                    ge(pe, "xn_ready", g + 1)
                    for t in range(GT):
                        c0 = SC0 + (j * GT + t) * E
                        ins = pe.matmul(nb[0][:, c0:c0 + RPAD], xnT[j][:, t * P:(t + 1) * P], wr_sb[:, :], start=True, stop=True)
                    ins.then_inc(s("score_mm"), 1)

            def rank(b):
                ge(pe, "picked_ready", b + 1)
                ge(pe, "carry_ready", b + 1)
                o = nb[1][:, SC0:SC0 + R * E]
                pv = picked[:, :, :].rearrange("p r e -> p (r e)")
                pe.matmul(o, before[:, :], pv, start=True, stop=False)
                for r in range(R - 1):
                    n = R - 1 - r
                    pe.matmul(o[:, (r + 1) * E:].rearrange("p (r e) -> p r e", e=E), ones[:, :],
                              picked[:, r:r + 1, :].to_broadcast([P, n, E]), start=False, stop=False)
                pe.matmul(o.rearrange("p (r e) -> p r e", e=E), ones[:, :],
                          carry[:, :].unsqueeze(1).to_broadcast([P, R, E]), start=False, stop=True).then_inc(s("rank_mm"), 1)

            pe.wait_ge(s("mod_ready"), 2)
            read_out(0, 0)
            att_turn(0, 0)
            project(0, 0)
            read_out(0, 1)
            unit2_turn(0, 0)
            att_turn(0, 1)
            project(0, 1)

            def a2(b, has_before, has_after):
                ffn1(b, 0)
                unit2_turn(b, 1)
                if has_after:
                    read_out(b + 1, 0)
                ffn2(b, 0)
                if has_after:
                    att_turn(b + 1, 0)
                if has_before:
                    router(b - 1, G * (b + 1) + 1 if has_after else G * B, G * b + 2)
                if has_after:
                    project(b + 1, 0)
                ffn1(b, 1)
                gate(b, 0, G * (b + 1) + (1 if has_after else 0))
                if has_before:
                    rank(b - 1)
                if has_after:
                    unit2_turn(b + 1, 0)
                    read_out(b + 1, 1)
                ffn2(b, 1)
                if has_after:
                    att_turn(b + 1, 1)
                gate(b, 1, G * (b + 1) + (1 if has_after else 0))
                if has_after:
                    project(b + 1, 1)

            a2(0, False, True)
            with pe.Fori(1, B - 1) as b:
                a2(b, True, True)
            a2(B - 1, True, False)
            router(B - 1, G * B, G * B)
            rank(B - 1)
            ge(pe, "carry_ready", B + 1)
            pe.matmul(nb[0][:, 0:E], ones[:, :], carry[:, :], start=True, stop=True).then_inc(s("count_mm"), 1)

            pe.wait_ge(s("in_exp"), 16 * (1 + HC))
            pe.wait_ge(s("tables_ready"), 1)

            def x_turn(i, u):
                j = UN * i + u
                ge(pe, f"in_s{u}", 16 * (i + 1))
                ge(pe, "xT_ready", j)
                pe.transpose(xtb[:, 0:P], slots_in[u][:, 0:D], ident[:, :]).then_inc(s("x_T"), 1)

            def experts_of(i):
                first = UN * i if isinstance(i, int) and i == 0 else UN * i - 4
                n = UN + (UN * i - first if isinstance(i, int) else 4)
                e = tile_expert[0:1, first:first + n] if isinstance(i, int) else tile_expert[0:1, bass.ds(first, n)]
                values = nc.values_load_multi_w_load_instructions(
                    e, [mybir.EngineType.PE], min_val=0, max_val=E - 1,
                    skip_runtime_bounds_check_because="the table is made above, within these bounds")[1]
                return {u - (n - UN): v for u, v in enumerate(values)}

            def up(j, p, e, half):
                v = up_sb[:, bass.ds(e, 1), half * HM:(half + 1) * HM].rearrange("p a n -> p (a n)")
                if half == 1:
                    ge(pe, "xT_ready", j + 1)
                    ge(pe, "g_ready", j)
                    pe.matmul(gb_[:, 0:HM], xT[p][:, :], v, start=True, stop=True).then_inc(s("g_mm"), 1)
                else:
                    ge(pe, "hid2_ready", j)
                    pe.matmul(vb_[:, 0:HM], xT[p][:, :], v, start=True, stop=True).then_inc(s("v2_mm"), 1)

            def hid_turn(j, p):
                ge(pe, "hid2_ready", j + 1)
                ge(pe, "hT_ready", 2 * j)
                for c in range(HC):
                    n = min(P, HM - c * P)
                    ins = pe.transpose(htb[0:n, c * P:(c + 1) * P], hid[p][:, c * P:c * P + n], ident[:, :])
                ins.then_inc(s("hid_T"), 1)

            def down(j, p, e):
                ge(pe, "hT_ready", 2 * (j + 1))
                ge(pe, "y_ready", j)
                for c in range(HC):
                    n = min(P, HM - c * P)
                    w = down_sb[0:n, bass.ds(e, 1), c * D:(c + 1) * D].rearrange("p a n -> p (a n)")
                    ins = pe.matmul(yb[:, 0:D], hT[p][0:n, c * P:(c + 1) * P], w, start=(c == 0), stop=(c == HC - 1))
                ins.then_inc(s("y_mm"), 1)

            def b_step(i, u, experts):
                j = UN * i + u
                if u == 0:
                    x_turn(i, 0)
                if not (isinstance(j, int) and j < 2):
                    down(j - 2, u % 2, experts[u - 2])
                if not (isinstance(j, int) and j < 1):
                    hid_turn(j - 1, (u + 1) % 2)
                up(j, u % 2, experts[u], 1)
                if u < UN - 1:
                    x_turn(i, u + 1)
                up(j, u % 2, experts[u], 0)

            experts = experts_of(0)
            for u in range(UN):
                b_step(0, u, experts)
            with pe.Fori(1, NT // UN) as i:
                experts = experts_of(i)
                for u in range(UN):
                    b_step(i, u, experts)
            experts = experts_of(NT // UN - 1)
            down(NT - 2, 0, experts[UN - 2])
            hid_turn(NT - 1, 1)
            down(NT - 1, 1, experts[UN - 1])


def kernel(**inputs):
    import numpy as np
    import concourse.bacc as bacc
    from concourse.bass_utils import run_bass_kernel_spmd as run

    a = {k.replace("L0_", ""): np.asarray(v) for k, v in inputs.items()}
    columns = [a["attn_gamma1"], a["attn_beta1"], a["ffn_norm_scale"], a["attn_b2"], *a["attn_b1"].reshape(FC, P)]
    arrays = {
        "x": a["attn_x"],
        "c_t": a["c"].T,
        "wmod": a["wmod"],
        "vecs": np.stack(columns, axis=1),
        "wq": a["attn_wq"].reshape(D, D),
        "wk": a["attn_wk"].reshape(D, D),
        "wv": a["attn_wv"].reshape(D, D),
        "wo": a["attn_wo"].reshape(D, D),
        "w1": a["attn_w1"],
        "w2": a["attn_w2"],
        "wr_t": a["ffn_w_router"].T,
        "w_up": a["ffn_w_up"].transpose(2, 0, 1),
        "w_down": a["ffn_w_down"].transpose(2, 0, 1),
    }
    nc = bacc.Bacc("TRN2", target_bir_lowering=False, num_devices=1)
    arrays = {f"in_{k}": np.ascontiguousarray(v) for k, v in arrays.items()}
    args = [nc.dram_tensor(k, v.shape, mybir.dt.from_np(v.dtype), kind="ExternalInput").ap() for k, v in arrays.items()]
    out = nc.dram_tensor("out", (B, L, D), F32, kind="ExternalOutput").ap()
    build(nc, *args, out)
    r = run(nc, [arrays], core_ids=[0])
    return r.results[0]["out"]
```

```python
from contextlib import ExitStack

import concourse.bass as bass
from concourse import mybir

F32 = mybir.dt.float32
BF16 = mybir.dt.bfloat16
I32 = mybir.dt.int32
U32 = mybir.dt.uint32
ALU = mybir.AluOpType
ACT = mybir.ActivationFunctionType
AX = mybir.AxisListType

P = 128
B, L, D = 4, 1024, 128
H, DH = 16, 8
F = 512
FC = F // P
E, TOPK, HM = 8, 2, 352
HC = -(-HM // P)
LASTH = HM - (HC - 1) * P
R = L // P
GT = 4
G = R // GT
GN = GT * D
NKV = D + H
STAB = 0.001
EPS_OUT, EPS_IN = 1e-5, 1e-6
TOK = B * L
CAP = TOK + P
ROW = D + 2
GATE, DEST = D, D + 1
NT = 72
UN = 8
NOWHERE = 1 << 20
RPAD = 96
MOD_SHIFT_A, MOD_SCALE_A, MOD_GATE_A, MOD_SHIFT_B, MOD_SCALE_B, MOD_GATE_B = range(6)
GAMMA, BETA, NSCALE, BIAS2, BIAS1 = 0, 1, 2, 3, 4


def build(nc, x, c_t, wmod, vecs, wq, wk, wv, wo, w1, w2, wr_t, w_up, w_down, out):
    rows_dram = nc.dram_tensor("expert_rows", (E * CAP, ROW), F32).ap()
    pair_dram = nc.dram_tensor("pair_outputs", (TOPK * TOK, D), F32).ap()

    with ExitStack() as ctx:
        def sb(name, shape, dt=F32):
            return ctx.enter_context(nc.sbuf_tensor(name, shape, dt))

        def sem(name):
            return ctx.enter_context(nc.semaphore(name))

        cT = sb("cT", [P, B])
        silu_c = sb("silu_c", [P, B])
        silu_cb = sb("silu_cb", [P, B, P])
        wmod_sb = sb("wmod_sb", [P, 6 * D])
        mod = sb("mod", [P, B, 6, D])
        vec = sb("vec", [P, 4 + FC])
        wq_sb, wk_sb, wv_sb, wo_sb = (sb(n, [P, D]) for n in ("wq_sb", "wk_sb", "wv_sb", "wo_sb"))
        w1_sb = sb("w1_sb", [P, F])
        w2_sb = sb("w2_sb", [P, FC, D])
        wr_sb = sb("wr_sb", [P, RPAD])
        up_sb = sb("up_sb", [P, E, 2 * HM])
        down_sb = sb("down_sb", [P, E, HC * D])
        ident = sb("ident", [P, P])
        before = sb("before", [P, P], BF16)
        ones = sb("ones", [P, P], BF16)
        same_head = sb("same_head", [P, NKV])
        neg_half = sb("neg_half", [P, GT])
        expert_no = sb("expert_no", [P, E])
        region = sb("region", [P, E])
        tile_no = sb("tile_no", [1, NT])
        level = sb("level", [1, TOK // P])
        dest_all = sb("dest_all", [P, B, R, TOPK], I32)
        gate_diag = sb("gate_diag", [P, B, P])
        gate_sign = sb("gate_sign", [P, B, 2, D])
        x_all = sb("x_all", [P, B, R * D])
        h_all = sb("h_all", [P, B, R * D])
        q_all = sb("q_all", [P, B, G * GN])
        kvs_all = sb("kvs_all", [P, B, NKV])
        wo_gate = sb("wo_gate", [P, B, D])
        gated_h = sb("gated_h", [P, GN])
        xhat = [sb(f"xhat{j}", [P, GN]) for j in range(G)]
        scaled = [sb(f"scaled{j}", [P, GN]) for j in range(G)]
        unit1 = [sb(f"unit1{j}", [P, GN]) for j in range(G)]
        ln1T = [sb(f"ln1T{j}", [P, GN]) for j in range(G)]
        kfeat = [sb(f"kfeat{j}", [P, GN]) for j in range(G)]
        vones = [sb(f"vones{j}", [P, GT, D + 4]) for j in range(G)]
        def stats(name):
            return [(sb(f"{name}_st{j}", [P, GT, 6]), sb(f"{name}_mv{j}", [P, GT, 2]),
                     sb(f"{name}_ve{j}", [P, GT]), sb(f"{name}_rs{j}", [P, GT])) for j in range(G)]
        st_x, st_h, st_a, st_y = stats("x"), stats("h"), stats("a"), stats("y")
        sumsq = [sb(f"sumsq{j}", [P, GT]) for j in range(G)]
        ms_eps = [sb(f"ms_eps{j}", [P, GT]) for j in range(G)]
        rms = [sb(f"rms{j}", [P, GT]) for j in range(G)]
        rden = sb("rden", [P, GT, H])
        attT = [sb(f"attT{j}", [P, GN]) for j in range(G)]
        add1 = [sb(f"add1{j}", [P, GN]) for j in range(G)]
        unit2 = [sb(f"unit2{j}", [P, GN]) for j in range(G)]
        hidT = sb("hidT", [P, FC, GN])
        yhat = sb("yhat", [P, GN])
        square = sb("square", [P, GN])
        ffnT, ln2T, xnT, qf, att = xhat, ln1T, kfeat, unit1, scaled
        score = sb("score", [P, GT, E])
        top = sb("top", [P, GT, E])
        top_ix = sb("top_ix", [P, GT, E], U32)
        top_f = sb("top_f", [P, TOPK, GT])
        onehot = sb("onehot", [P, TOPK, GT, E])
        picked = sb("picked", [P, GT, E], BF16)
        picked_n = sb("picked_n", [P, E])
        carry = sb("carry", [P, E], BF16)
        carry_f = sb("carry_f", [P, E])
        expin = sb("expin", [P, GT, E])
        expo = sb("expo", [P, GT, E])
        expsum = sb("expsum", [P, GT])
        rsum = sb("rsum", [P, GT])
        slotrow = sb("slotrow", [P, GT, E])
        pickrow = sb("pickrow", [P, TOPK, GT, E])
        slot_f = sb("slot_f", [P, TOPK, GT])
        slot = [sb(f"slot{j}", [P, TOPK, GT], U32) for j in range(G)]
        token_rows = sb("token_rows", [P, R, TOPK, ROW])
        pad_rows = sb("pad_rows", [P, ROW])
        count = sb("count", [1, E])
        cmp_level = sb("cmp_level", [1, E, TOK // P])
        tiles = sb("tiles", [1, E])
        tiles_end = sb("tiles_end", [1, E])
        q_free = q_all[:, :, :].rearrange("p b n -> p (b n)")
        hid_free = hidT[:, :, :].rearrange("p c n -> p (c n)")
        past = q_free[0:1, 0:NT * E].rearrange("p (t e) -> p t e", t=NT)
        past_tiles = q_free[0:1, NT * E:2 * NT * E].rearrange("p (t e) -> p t e", t=NT)
        tab = sb("tab", [1, 6, NT])
        pad_f = sb("pad_f", [1, E])
        pad_at = sb("pad_at", [1, E], I32)
        tile_row = sb("tile_row", [1, NT], I32)
        tile_expert = sb("tile_expert", [1, NT], I32)
        slots_in = [token_rows[:, s_, 0, :] for s_ in range(UN)]
        xT = [sb(f"xT{s}", [P, P]) for s in range(2)]
        act_g = [hid_free[:, s_ * HM:(s_ + 1) * HM] for s_ in range(2)]
        hid = [hid_free[:, (2 + s_) * HM:(3 + s_) * HM] for s_ in range(2)]
        hT = [sb(f"hT{s}", [P, HC * P]) for s in range(2)]
        y_sb = [sb(f"y_sb{s}", [P, D]) for s in range(UN)]
        pair_in = [[q_free[:, (TOPK * j + k) * GN:(TOPK * j + k + 1) * GN] for k in range(TOPK)] for j in range(G)]
        res = [q_free[:, (TOPK * G + j) * GN:(TOPK * G + j + 1) * GN] for j in range(G)]

        banks = [ctx.enter_context(nc.psum_tensor(f"bank{i}", [P, 512], F32)) for i in range(8)]
        trb, kb, vb, qb, kvb = banks[0:2], banks[2], banks[3], banks[4], banks[5]
        rb, tl, wb, ob, fb, nb = banks[0], banks[1], banks[2], banks[3], banks[4:6], banks[6:8]
        xtb, gb_, vb_, htb, yb = banks[0], banks[1], banks[2], banks[4], banks[5]

        S = {}

        def s(name):
            if name not in S:
                S[name] = sem(name)
            return S[name]

        STARTED = {"rows_free", "normed_T", "exp_done", "rank_mm", "gates_ready", "ms_ready"}

        def ge(eng, name, value):
            if isinstance(value, int) and value <= 0:
                return
            eng.wait_ge(s(name), value + (name in STARTED))

        def ge_apart(eng, name, value, passed):
            ge(eng, name, value)
            if not isinstance(value, int):
                eng.sem_inc(s(passed), 1)

        for name in ("sp_passed", "act_passed", "pool_passed", "dve_passed", "in_c", "in_vec", "in_x0", "in_x1", "in_x2", "in_x3", "in_w", "in_w2", "in_exp",
                     "k_const", "pool_const", "silu_done", "silu_rows", "mod_mm", "mod_hi", "mod_lo", "mod_ready", "gate_step",
                     "x_raw", "x_stats", "x_ve", "x_rstd", "xhat_ready", "scaled_ready", "h_ready", "h_raw", "h_stats",
                     "h_ve", "h_rstd", "unit1_ready", "unit1_T", "ln1_ready", "k_mm", "v_mm", "q_mm",
                     "kfeat_ready", "v_ready", "q_ready", "kvs_mm", "kvs_ready",
                     "qf_ready", "num_mm", "rden_ready", "att_ready", "att_T", "attT_ready", "wo_gate_ready", "half_base", "wo_mm", "add1_ready",
                     "a_raw", "a_stats", "a_ve", "a_rstd", "base_ready", "unit2_ready", "unit2_T", "ln2_ready",
                     "ff1_mm", "hid_ready", "ff2_mm", "ffn_ready", "gate_mm", "x2_ready", "y_raw", "y_stats",
                     "y_ve", "y_rstd", "yhat_ready", "yscaled", "h3_ready", "square_done", "ms_ready", "rms_ready", "normed_ready",
                     "rows_free", "doubled", "normed_T", "xn_ready", "score_mm", "score_ready", "top_ready", "topix_ready", "topf_ready", "onehot_ready",
                     "picked_ready", "pickedn_ready", "carry_ready", "below_ready", "rank_mm", "expin_ready", "exp_done", "expsum_ready", "rsum_ready",
                     "gates_ready", "dest_ready", "slotrow_ready", "pickrow_ready", "slotf_ready", "slot_ready", "scattered0", "scattered1",
                     "count_mm", "tab_step", "pads_ready", "tables_ready", "pads_written",
                     "z_scaled", "z_ready",
                     *(f"in_s{u}" for u in range(UN)), "x_T", "xT_ready", "g_mm", "g_ready", "v2_mm", "hid2_ready",
                     "hid_T", "hT_ready", "y_mm", "y_ready", *(f"out_s{u}" for u in range(UN)),
                     "pair0", "pair1", "pairsum", "pairgate", "res_ready", "stored0", "stored1"):
            s(name)

        block = ctx.enter_context(nc.Block())

        def batch(t, b):
            return t[:, b, :] if isinstance(b, int) else t[:, bass.ds(b, 1), :].rearrange("p a n -> p (a n)")

        def group(t, b, j):
            return t[:, b, j * GN:(j + 1) * GN] if isinstance(b, int) else \
                t[:, bass.ds(b, 1), j * GN:(j + 1) * GN].rearrange("p a n -> p (a n)")

        def tile(t, b, r):
            return t[:, b, r * D:(r + 1) * D] if isinstance(b, int) else \
                t[:, bass.ds(b, 1), r * D:(r + 1) * D].rearrange("p a n -> p (a n)")

        def mod_rows(b, which):
            m = mod[:, b, which, :] if isinstance(b, int) else \
                mod[:, bass.ds(b, 1), which, :].rearrange("p a n -> p (a n)")
            return m.unsqueeze(1).to_broadcast([P, GT, D])

        def by_tile(ap):
            return ap.rearrange("p (t d) -> p t d", t=GT)

        def at(b, j, step):
            return b + (j + step) // G, (j + step) % G

        def exists(b, j, step):
            return not isinstance(b, int) or 0 <= G * b + j + step < G * B

        def groups(eng, a1):
            for j in range(G):
                a1(0, j)
            with eng.Fori(1, B - 1) as b:
                for j in range(G):
                    a1(b, j)
            for j in range(G):
                a1(B - 1, j)

        def steps(eng, a2):
            for j in range(G):
                a2(0, j)
            with eng.Fori(1, B - 1) as b:
                for j in range(G):
                    a2(b, j)
            for g in range(G * (B - 1), G * B + 2):
                a2(g // G, g % G)

        @block.sync
        def _(sp):
            sp.sem_inc(s("rows_free"), 1)
            xv = x.rearrange("b (p r) d -> b p (r d)", p=P)
            sp.dma_start(cT[:, :], c_t).then_inc(s("in_c"), 16)
            sp.dma_start(x_all[:, 0, :], xv[0]).then_inc(s("in_x0"), 16)
            sp.dma_start(wmod_sb[:, :], wmod).then_inc(s("in_c"), 16)
            sp.dma_start(vec[:, :], vecs).then_inc(s("in_vec"), 16)
            for t, w in ((wk_sb, wk), (wv_sb, wv), (wq_sb, wq)):
                sp.dma_start(t[:, :], w).then_inc(s("in_w"), 16)
            for b in range(1, B):
                sp.dma_start(x_all[:, b, :], xv[b]).then_inc(s(f"in_x{b}"), 16)
            sp.dma_start(wo_sb[:, :], wo).then_inc(s("in_w2"), 16)
            sp.dma_start(w1_sb[:, :], w1).then_inc(s("in_w2"), 16)
            sp.dma_start(w2_sb[:, :, :], w2.rearrange("(c p) e -> p c e", p=P)).then_inc(s("in_w2"), 16)
            sp.wait_ge(s("pool_const"), 1)
            sp.dma_start(wr_sb[:, 0:E], wr_t).then_inc(s("in_w2"), 16)
            sp.dma_start(up_sb[:, :, :].rearrange("p e n -> p (e n)"), w_up.rearrange("p e n -> p (e n)")).then_inc(s("in_exp"), 16)
            for c in range(HC):
                n = min(P, HM - c * P)
                sp.dma_start(down_sb[0:n, :, c * D:(c + 1) * D], w_down[c * P:c * P + n]).then_inc(s("in_exp"), 16)

            def free_rows(b, j):
                ge_apart(sp, f"scattered{j}", 16 * TOPK * GT * (b + 1), "sp_passed")
                sp.sem_inc(s("rows_free"), 1)

            with sp.Fori(0, B) as b:
                for j in range(G):
                    free_rows(b, j)

            sp.wait_ge(s("pads_ready"), 1)
            for e in range(E):
                at = sp.value_load(pad_at[0:1, e:e + 1], min_val=0, max_val=E * CAP - P)
                sp.dma_start(rows_dram[bass.ds(at, P), :], pad_rows[:, :]).then_inc(s("pads_written"), 16)
            sp.wait_ge(s("pads_written"), 16 * E)
            for j in range(G):
                sp.wait_ge(s(f"scattered{j}"), 16 * TOPK * GT * B)
            sp.wait_ge(s("tables_ready"), 1)

            def load_slots(i, first):
                t = tile_row[0:1, 0:UN] if first else tile_row[0:1, bass.ds(UN * i, UN)]
                rows = nc.values_load_multi_w_load_instructions(
                    t, [mybir.EngineType.SP], min_val=0, max_val=E * CAP - P,
                    skip_runtime_bounds_check_because="the table is made above, within these bounds")[1]
                for u in range(UN):
                    if not first:
                        ge_apart(sp, f"out_s{u}", 16 * i, "sp_passed")
                    sp.dma_start(slots_in[u][:, :], rows_dram[bass.ds(rows[u], P), :]).then_inc(s(f"in_s{u}"), 16)

            load_slots(0, True)
            with sp.Fori(1, NT // UN) as i:
                load_slots(i, False)

            for u in range(UN):
                ge(sp, f"out_s{u}", 16 * (NT // UN))
            pv = pair_dram.rearrange("(k b p r) d -> k b p (r d)", k=TOPK, b=B, p=P)
            ov = out.rearrange("b (p r) d -> b p (r d)", p=P)

            def ds(b):
                return bass.ds(b, 1)

            def fetch(b, j):
                ge(sp, "pairsum", G * (b - 1) + j + 1)
                for k in range(TOPK):
                    sp.dma_start(pair_in[j][k][:, :],
                                 pv[k, ds(b), :, j * GN:(j + 1) * GN].rearrange("a p n -> p (a n)")).then_inc(s(f"pair{j}"), 16)

            def store(b, j):
                ge(sp, "res_ready", G * b + j + 1)
                sp.dma_start(ov[ds(b), :, j * GN:(j + 1) * GN].rearrange("a p n -> p (a n)"), res[j][:, :]).then_inc(s(f"stored{j}"), 16)

            for j in range(G):
                fetch(0, j)
            with sp.Fori(1, B) as b:
                for j in range(G):
                    fetch(b, j)
                    store(b - 1, j)
            for j in range(G):
                store(B - 1, j)
            for j in range(G):
                sp.wait_ge(s(f"stored{j}"), 16 * B)

        @block.gpsimd
        def _(pool):
            pool.sem_inc(s("ms_ready"), 1)
            n = [0]

            def step(ins):
                n[0] += 1
                ins.then_inc(s("k_const"), 1)
                pool.wait_ge(s("k_const"), n[0])

            pool.memset(wr_sb[:, :], 0.0).then_inc(s("pool_const"), 1)
            pool.memset(neg_half[:, :], -0.5)
            step(pool.memset(ident[:, :], 0.0))
            step(pool.affine_select(out=ident[:, :], in_=ident[:, :], compare_op=ALU.not_equal, fill=1.0, base=0,
                                    pattern=[[-1, P]], channel_multiplier=1))
            pool.memset(ones[:, :], 1.0)
            pool.memset(before[:, :], 1.0)
            for j in range(G):
                pool.memset(vones[j][:, :, D:D + 1], 1.0)
            pool.memset(pad_rows[:, :], 0.0)
            step(pool.memset(same_head[:, :], 1.0))
            step(pool.affine_select(out=before[:, :], in_=before[:, :], compare_op=ALU.is_gt, fill=0.0, base=0,
                                    pattern=[[1, P]], channel_multiplier=-1))
            for cols, reps in ((same_head[:, 0:D], [0, DH]), (same_head[:, D:NKV], [0, 1])):
                v = cols.rearrange("p (h d) -> p h d", h=H)
                step(pool.affine_select(out=v, in_=v, compare_op=ALU.is_ge, fill=0.0, base=0,
                                        pattern=[[-DH, H], reps], channel_multiplier=1))
                step(pool.affine_select(out=v, in_=v, compare_op=ALU.is_ge, fill=0.0, base=DH - 1,
                                        pattern=[[DH, H], reps], channel_multiplier=-1))
            pool.iota(pad_rows[:, DEST:DEST + 1].bitcast(I32), pattern=[[0, 1]], base=NOWHERE, channel_multiplier=1)
            pool.iota(expert_no[:, :], pattern=[[1, E]], base=0, channel_multiplier=0, allow_small_or_imprecise_dtypes=True)
            pool.iota(region[:, :], pattern=[[CAP, E]], base=0, channel_multiplier=0, allow_small_or_imprecise_dtypes=True)
            pool.iota(tile_no[:, :], pattern=[[1, NT]], base=0, channel_multiplier=0, allow_small_or_imprecise_dtypes=True)
            pool.iota(level[:, :], pattern=[[P, TOK // P]], base=0, channel_multiplier=0, allow_small_or_imprecise_dtypes=True)
            step(pool.iota(dest_all[:, :, :, :], pattern=[[L, B], [1, R], [TOK, TOPK]], base=0, channel_multiplier=R))
            pool.memset(square[0:1, 0:1], 0.0).then_inc(s("pool_const"), 1)

            def rsqrt(name, mv, ve, rs, eps, g):
                ge_apart(pool, f"{name}_stats", g + 1, "pool_passed")
                pool.tensor_scalar(ve[:, :], mv[:, :, 1], eps, None, ALU.add).then_inc(s(f"{name}_ve"), 1)
                ge(pool, f"{name}_ve", g + 1)
                pool.tensor_tensor(rs[:, :], ve[:, :], neg_half[:, :], ALU.pow).then_inc(s(f"{name}_rstd"), 1)

            def scale_x(b, j):
                ge_apart(pool, "xhat_ready", G * b + j + 1, "pool_passed")
                pool.tensor_tensor(by_tile(scaled[j][:, :]), by_tile(xhat[j][:, :]), mod_rows(b, MOD_SCALE_A), ALU.mult)\
                    .then_inc(s("scaled_ready"), 1)

            def base(b, j):
                ge(pool, "h_ready", G * b + j + 1)
                ge_apart(pool, "half_base", G * b + j, "pool_passed")
                pool.tensor_tensor(by_tile(gated_h[:, :]), by_tile(group(h_all, b, j)), mod_rows(b, MOD_GATE_A), ALU.mult)\
                    .then_inc(s("half_base"), 1)
                ge_apart(pool, "half_base", G * b + j + 1, "pool_passed")
                pool.tensor_tensor(group(x_all, b, j), gated_h[:, :], group(x_all, b, j), ALU.add).then_inc(s("base_ready"), 1)

            def a1(b, j):
                if exists(b, j, 1):
                    scale_x(*at(b, j, 1))
                rsqrt("h", *st_h[j][1:], EPS_IN, G * b + j)
                if exists(b, j, 2):
                    rsqrt("x", *st_x[j][1:], EPS_OUT, G * b + j + 2)
                if isinstance(b, int) and G * b + j == 0:
                    pool.wait_ge(s("mod_ready"), 2)
                base(b, j)

            rsqrt("x", *st_x[0][1:], EPS_OUT, 0)
            pool.wait_ge(s("mod_ready"), 1)
            scale_x(0, 0)
            rsqrt("x", *st_x[1][1:], EPS_OUT, 1)
            groups(pool, a1)

            pool.wait_ge(s("in_w2"), 64)
            pool.tensor_tensor(wo_gate[:, :, :], wo_sb[:, :].unsqueeze(1).to_broadcast([P, B, D]), mod[:, :, MOD_GATE_A, :],
                               ALU.mult).then_inc(s("wo_gate_ready"), 1)

            def rms_rsqrt(b, j):
                g = G * b + j
                ge_apart(pool, "square_done", g + 1, "pool_passed")
                pool.tensor_scalar(ms_eps[j][:, :], sumsq[j][:, :], 1.0 / D, EPS_IN, ALU.mult, ALU.add).then_inc(s("ms_ready"), 1)
                ge(pool, "ms_ready", g + 1)
                pool.tensor_tensor(rms[j][:, :], ms_eps[j][:, :], neg_half[:, :], ALU.pow).then_inc(s("rms_ready"), 1)

            def scatter(b, j):
                g = G * b + j
                ge(pool, "slot_ready", g + 1)
                ge(pool, "gates_ready", g + 1)
                ge(pool, "normed_ready", g + 1)
                ge_apart(pool, "doubled", g + 1, "pool_passed")
                for t in range(GT):
                    for k in range(TOPK):
                        pool.indirect_dma_start(rows_dram, bass.IndirectOffsetOnAxis(ap=slot[j][:, k, t:t + 1], axis=0),
                                                token_rows[:, j * GT + t, k, :], None, bounds_check=E * CAP - 1,
                                                oob_is_err=False).then_inc(s(f"scattered{j}"), 16)

            def a2(b, j):
                if exists(b, j, -1):
                    bb, jj = at(b, j, -1)
                    rsqrt("y", *st_y[jj][1:], EPS_OUT, G * bb + jj)
                if exists(b, j, 1):
                    bb, jj = at(b, j, 1)
                    rsqrt("a", *st_a[jj][1:], EPS_IN, G * bb + jj)
                if exists(b, j, -1):
                    rms_rsqrt(*at(b, j, -1))
                if exists(b, j, -2):
                    scatter(*at(b, j, -2))

            rsqrt("a", *st_a[0][1:], EPS_IN, 0)
            steps(pool, a2)

            def send(i, u):
                ge_apart(pool, "y_ready", UN * i + u + 1, "pool_passed")
                pool.indirect_dma_start(pair_dram, bass.IndirectOffsetOnAxis(ap=slots_in[u][:, DEST:DEST + 1].bitcast(U32), axis=0),
                                        y_sb[u][:, :], None, bounds_check=TOPK * TOK - 1,
                                        oob_is_err=False).then_inc(s(f"out_s{u}"), 16)

            with pool.Fori(0, NT // UN) as i:
                for u in range(UN):
                    send(i, u)

        @block.scalar
        def _(act):
            for name in ("exp_done",):
                act.sem_inc(s(name), 1)
            gamma, beta = vec[:, GAMMA:GAMMA + 1], vec[:, BETA:BETA + 1]
            act.wait_ge(s("in_c"), 32)
            act.activation(silu_c[:, :], cT[:, :], ACT.Silu).then_inc(s("silu_done"), 1)
            for b in range(B):
                act.wait_ge(s("mod_mm"), b + 1)
                act.activation(mod[:, b, 0:4, :].rearrange("p a d -> p (a d)"), banks[b][:, :], ACT.Copy).then_inc(s("mod_lo"), 1)
            act.wait_ge(s("in_vec"), 16)

            def a1(b):
                for j in range(G):
                    g = G * b + j
                    ge(act, "unit1_T", g + 1)
                    ge(act, "k_mm", g - 1)
                    ge(act, "v_mm", g - 1)
                    ge(act, "q_mm", g - 1)
                    act.activation(ln1T[j][:, :], trb[j][:, :], ACT.Identity, bias=beta, scale=gamma).then_inc(s("ln1_ready"), 1)
                    ge(act, "v_mm", g + 1)
                    ge(act, "kvs_mm", g - 1)
                    act.activation(vones[j][:, :, 0:D], by_tile(vb[:, :]), ACT.Copy).then_inc(s("v_ready"), 1)

            a1(0)
            with act.Fori(1, B) as b:
                a1(b)

            def q_copy(b, j):
                g = G * b + j
                ge(act, "num_mm", g - 1)
                ge_apart(act, "q_ready", g + 1, "act_passed")
                act.activation(qf[j][:, :], group(q_all, b, j), ACT.Copy).then_inc(s("qf_ready"), 1)

            def att_out(b, j):
                g = G * b + j
                ge(act, "att_T", g + 1)
                ge(act, "gate_mm", g - 1)
                act.activation(attT[j][:, :], nb[0][:, :], ACT.Copy).then_inc(s("attT_ready"), 1)

            def ln2_out(b, j):
                g = G * b + j
                ge(act, "unit2_T", g + 1)
                ge(act, "ff1_mm", FC * (g - 1))
                act.activation(ln2T[j][:, :], tl[:, :], ACT.Identity, bias=beta, scale=gamma).then_inc(s("ln2_ready"), 1)

            def gelu1(b, j):
                g = G * b + j
                for c in range(FC):
                    ge(act, "ff1_mm", FC * g + c + 1)
                    if c == 0:
                        ge(act, "ff2_mm", g)
                    act.activation(hidT[:, c, :], fb[c % 2][:, :], ACT.Gelu, bias=vec[:, BIAS1 + c:BIAS1 + c + 1]).then_inc(s("hid_ready"), 1)

            def gelu2(b, j):
                g = G * b + j
                ge(act, "ff2_mm", g + 1)
                ge(act, "gate_mm", g - 1)
                act.activation(ffnT[j][:, :], ob[:, :], ACT.Gelu, bias=vec[:, BIAS2:BIAS2 + 1]).then_inc(s("ffn_ready"), 1)

            def squares(b, j):
                g = G * b + j
                ge(act, "h3_ready", g + 1)
                ge(act, "ms_ready", g - 1)
                ge_apart(act, "square_done", g, "act_passed")
                for t in range(GT):
                    ins = act.activation(square[:, t * D:(t + 1) * D], tile(h_all, b, j * GT + t), ACT.Square,
                                         accum_out=sumsq[j][:, t:t + 1])
                ins.then_inc(s("square_done"), 1)

            def double(b, j):
                g = G * b + j
                ge_apart(act, "normed_ready", g + 1, "act_passed")
                for t in range(GT):
                    ins = act.activation(token_rows[:, j * GT + t, 1, 0:D], tile(h_all, b, j * GT + t), ACT.Copy,
                                         scale=rms[j][:, t:t + 1])
                ins.then_inc(s("doubled"), 1)

            def xn_out(b, j):
                ge(act, "normed_T", G * b + j + 1)
                act.activation(xnT[j][:, :], rb[:, :], ACT.Copy, scale=vec[:, NSCALE:NSCALE + 1]).then_inc(s("xn_ready"), 1)

            def exps(b, j):
                g = G * b + j
                ge(act, "expin_ready", g + 1)
                ge(act, "gates_ready", g)
                act.activation(expo[:, :, :], expin[:, :, :], ACT.Exp).then_inc(s("exp_done"), 1)

            def a2(b, j):
                if exists(b, j, 1) and not (isinstance(b, int) and G * b + j == 0):
                    att_out(*at(b, j, 1))
                if exists(b, j, 2):
                    q_copy(*at(b, j, 2))
                if exists(b, j, 0):
                    gelu1(b, j)
                if exists(b, j, -2):
                    exps(*at(b, j, -2))
                if exists(b, j, -1):
                    squares(*at(b, j, -1))
                if exists(b, j, 0):
                    gelu2(b, j)
                if exists(b, j, 1):
                    ln2_out(*at(b, j, 1))
                if exists(b, j, -1):
                    xn_out(*at(b, j, -1))
                    double(*at(b, j, -1))

            q_copy(0, 0)
            q_copy(0, 1)
            att_out(0, 0)
            att_out(0, 1)
            ln2_out(0, 0)
            steps(act, a2)

            def silu(j, p):
                ge(act, "g_mm", j + 1)
                ge(act, "hid2_ready", j - 1)
                act.activation(act_g[p][:, :], gb_[:, 0:HM], ACT.Silu).then_inc(s("g_ready"), 1)

            def hidden_out(j, p):
                ge(act, "hid_T", j + 1)
                ge(act, "y_mm", j - 1)
                act.activation(hT[p][:, 0:(HC - 1) * P], htb[:, 0:(HC - 1) * P], ACT.Copy).then_inc(s("hT_ready"), 1)
                act.activation(hT[p][0:LASTH, (HC - 1) * P:], htb[0:LASTH, (HC - 1) * P:HC * P], ACT.Copy).then_inc(s("hT_ready"), 1)

            def b_step(j, u, one_before):
                if one_before:
                    hidden_out(j - 1, (u + 1) % 2)
                silu(j, u % 2)

            for u in range(UN):
                b_step(u, u, u >= 1)
            with act.Fori(1, NT // UN) as i:
                for u in range(UN):
                    b_step(UN * i + u, u, True)
            hidden_out(NT - 1, 1)

        @block.vector
        def _(dve):
            for name in ("gates_ready",):
                dve.sem_inc(s(name), 1)
            dve.wait_ge(s("silu_done"), 1)
            dve.tensor_copy(silu_cb[:, :, :], silu_c[:, :].unsqueeze(2).to_broadcast([P, B, P])).then_inc(s("silu_rows"), 1)

            def norm_stats(name, st, src, g):
                for t in range(GT):
                    ins = dve.bn_stats(st[0][:, t, :], src[t])
                ins.then_inc(s(f"{name}_raw"), 1)
                ge_apart(dve, f"{name}_raw", g + 1, "dve_passed")
                for t in range(GT):
                    ins = dve.bn_aggr(st[1][:, t, :], st[0][:, t, :])
                ins.then_inc(s(f"{name}_stats"), 1)

            def normalise(name, st, src, dst, done, g):
                ge(dve, f"{name}_rstd", g + 1)
                for t in range(GT):
                    ins = dve.tensor_scalar(dst[:, t * D:(t + 1) * D], src[t], st[1][:, t, 0:1], st[3][:, t:t + 1],
                                            ALU.subtract, ALU.mult)
                ins.then_inc(s(done), 1)

            def x_tiles(b, j):
                return [tile(x_all, b, j * GT + t) for t in range(GT)]

            def h_tiles(b, j):
                return [tile(h_all, b, j * GT + t) for t in range(GT)]

            dve.wait_ge(s("in_x0"), 16)
            norm_stats("x", st_x[0], x_tiles(0, 0), 0)
            for b in range(B):
                dve.wait_ge(s("mod_mm"), b + 1)
                dve.tensor_copy(mod[:, b, 4:6, :].rearrange("p a d -> p (a d)"), banks[B + b][:, 0:2 * D]).then_inc(s("mod_hi"), 1)
            dve.wait_ge(s("mod_hi"), B)
            dve.wait_ge(s("mod_lo"), B)
            for m in (MOD_SCALE_A, MOD_SCALE_B):
                ins = dve.tensor_scalar(mod[:, :, m, :], mod[:, :, m, :], 1.0, None, ALU.add)
            ins.then_inc(s("mod_ready"), 1)
            normalise("x", st_x[0], x_tiles(0, 0), xhat[0], "xhat_ready", 0)
            norm_stats("x", st_x[1], x_tiles(0, 1), 1)
            for b in range(1, B):
                dve.wait_ge(s(f"in_x{b}"), 16)

            def gates():
                for n_, m in enumerate((MOD_GATE_A, MOD_GATE_B)):
                    v, sign = mod[:, :, m, :], gate_sign[:, :, n_, :]
                    dve.tensor_scalar(sign, v, 0.0, 0.5, ALU.is_ge, ALU.subtract).then_inc(s("gate_step"), 1)
                    dve.wait_ge(s("gate_step"), 4 * n_ + 1)
                    dve.tensor_tensor(v, v, sign, ALU.mult).then_inc(s("gate_step"), 1)
                    dve.wait_ge(s("gate_step"), 4 * n_ + 2)
                    dve.tensor_scalar(v, v, 0.125, 4.0, ALU.max, ALU.mult).then_inc(s("gate_step"), 1)
                    dve.wait_ge(s("gate_step"), 4 * n_ + 3)
                    dve.tensor_tensor(v, v, sign, ALU.mult).then_inc(s("gate_step"), 1)
                dve.wait_ge(s("gate_step"), 8)
                dve.wait_ge(s("pool_const"), 2)
                dve.tensor_tensor(gate_diag[:, :, :], mod[:, :, MOD_GATE_A, :], ident[:, :].unsqueeze(1).to_broadcast([P, B, P]),
                                  ALU.mult).then_inc(s("mod_ready"), 1)
                dve.memset(carry[:, :], 0.0)
                dve.memset(carry_f[:, :], 0.0).then_inc(s("carry_ready"), 1)
            def features(b, j):
                g = G * b + j
                ge(dve, "k_mm", g + 1)
                ge(dve, "kvs_mm", g - 1)
                dve.tensor_scalar(kfeat[j][:, :], kb[:, :], 0.0, STAB, ALU.max, ALU.add).then_inc(s("kfeat_ready"), 1)
                ge(dve, "q_mm", g + 1)
                dve.tensor_scalar(group(q_all, b, j), qb[:, :], 0.0, STAB, ALU.max, ALU.add).then_inc(s("q_ready"), 1)

            def keep_kvs(b):
                ge(dve, "kvs_mm", G * (b + 1))
                kv = batch(kvs_all, b)
                dve.tensor_tensor(kv[:, 0:D], kvb[:, 0:D], same_head[:, 0:D], ALU.mult)
                dve.tensor_scalar(kv[:, D:NKV], same_head[:, D:NKV], kvb[:, D:D + 1], None, ALU.mult).then_inc(s("kvs_ready"), 1)

            def a1(b, j):
                g = G * b + j
                if exists(b, j, 1):
                    nb_, nj = at(b, j, 1)
                    normalise("x", st_x[nj], x_tiles(nb_, nj), xhat[nj], "xhat_ready", g + 1)
                ge(dve, "scaled_ready", g + 1)
                dve.tensor_tensor(by_tile(group(h_all, b, j)), by_tile(scaled[j][:, :]), mod_rows(b, MOD_SHIFT_A), ALU.add)\
                    .then_inc(s("h_ready"), 1)
                ge_apart(dve, "h_ready", g + 1, "dve_passed")
                norm_stats("h", st_h[j], h_tiles(b, j), g)
                if exists(b, j, 2):
                    norm_stats("x", st_x[j], x_tiles(*at(b, j, 2)), g + 2)
                normalise("h", st_h[j], h_tiles(b, j), unit1[j], "unit1_ready", g)
                if j == 1 and exists(b, j, -2):
                    keep_kvs(b - 1)
                if exists(b, j, -1):
                    features(*at(b, j, -1))
                if isinstance(b, int) and g == 0:
                    gates()

            groups(dve, a1)
            features(B - 1, 1)
            keep_kvs(B - 1)

            def attend(b, j):
                g = G * b + j
                ge(dve, "num_mm", g + 1)
                for h in range(2):
                    v = nb[h][:, 0:2 * NKV].rearrange("p (t n) -> p t n", t=2)
                    ins = dve.reciprocal(rden[:, 2 * h:2 * h + 2, :], v[:, :, D:NKV])
                ins.then_inc(s("rden_ready"), 1)
                ge(dve, "att_T", g - 1)
                ge(dve, "rden_ready", g + 1)
                for h in range(2):
                    v = nb[h][:, 0:2 * NKV].rearrange("p (t n) -> p t n", t=2)[:, :, 0:D]
                    ins = dve.tensor_tensor(
                        att[j][:, 2 * h * D:(2 * h + 2) * D].rearrange("p (t h d) -> p t h d", t=2, h=H),
                        v.rearrange("p t (h d) -> p t h d", h=H),
                        rden[:, 2 * h:2 * h + 2, :].unsqueeze(3).to_broadcast([P, 2, H, DH]), ALU.mult)
                ins.then_inc(s("att_ready"), 1)

            def residual(b, j):
                g = G * b + j
                ge(dve, "wo_mm", g + 1)
                dve.tensor_tensor(add1[j][:, :], wb[:, :], group(h_all, b, j), ALU.add).then_inc(s("add1_ready"), 1)
                ge_apart(dve, "add1_ready", g + 1, "dve_passed")
                norm_stats("a", st_a[j], [add1[j][:, t * D:(t + 1) * D] for t in range(GT)], g)

            def unit(b, j):
                g = G * b + j
                ge(dve, "unit2_T", g - 1)
                normalise("a", st_a[j], [add1[j][:, t * D:(t + 1) * D] for t in range(GT)], unit2[j], "unit2_ready", g)

            def first_sum(b, j):
                g = G * b + j
                ge(dve, "base_ready", g + 1)
                ge(dve, "gate_mm", g + 1)
                dve.tensor_tensor(group(x_all, b, j), wb[:, :], group(x_all, b, j), ALU.add).then_inc(s("x2_ready"), 1)
                ge_apart(dve, "x2_ready", g + 1, "dve_passed")
                norm_stats("y", st_y[j], x_tiles(b, j), g)

            def modulate(b, j):
                g = G * b + j
                normalise("y", st_y[j], x_tiles(b, j), yhat, "yhat_ready", g)
                ge(dve, "yhat_ready", g + 1)
                dve.tensor_tensor(by_tile(yhat[:, :]), by_tile(yhat[:, :]), mod_rows(b, MOD_SCALE_B), ALU.mult).then_inc(s("yscaled"), 1)
                ge(dve, "yscaled", g + 1)
                dve.tensor_tensor(by_tile(group(h_all, b, j)), by_tile(yhat[:, :]), mod_rows(b, MOD_SHIFT_B), ALU.add).then_inc(s("h3_ready"), 1)

            def rms_norm(b, j):
                g = G * b + j
                ge(dve, "rms_ready", g + 1)
                ge(dve, "normed_T", g - 1)
                ge(dve, "rows_free", g - 1)
                for t in range(GT):
                    ins = dve.tensor_scalar(token_rows[:, j * GT + t, 0, 0:D], tile(h_all, b, j * GT + t), rms[j][:, t:t + 1],
                                            None, ALU.mult)
                ins.then_inc(s("normed_ready"), 1)

            def choose(b, j):
                g = G * b + j
                ge(dve, "score_mm", g + 1)
                dve.tensor_copy(score[:, :, :], rb[:, 0:GT * E].rearrange("p (r e) -> p r e", e=E)).then_inc(s("score_ready"), 1)
                ge_apart(dve, "score_ready", g + 1, "dve_passed")
                for t in range(GT):
                    ins = dve.max(top[:, t, :], score[:, t, :])
                ins.then_inc(s("top_ready"), 1)
                ge_apart(dve, "top_ready", g + 1, "dve_passed")
                for t in range(GT):
                    ins = dve.max_index(top_ix[:, t, :], top[:, t, :], score[:, t, :])
                ins.then_inc(s("topix_ready"), 1)
                ge(dve, "exp_done", g)
                dve.tensor_tensor(expin[:, :, :], top[:, :, :], top[:, :, 0:1].to_broadcast([P, GT, E]), ALU.subtract).then_inc(s("expin_ready"), 1)
                ge(dve, "topix_ready", g + 1)
                dve.tensor_copy(top_f[:, :, :], top_ix[:, :, 0:TOPK].rearrange("p r k -> p k r")).then_inc(s("topf_ready"), 1)
                ge(dve, "topf_ready", g + 1)
                dve.tensor_tensor(onehot[:, :, :, :].rearrange("p k r e -> p (k r) e"),
                                  top_f[:, :, :].rearrange("p k r -> p (k r)").unsqueeze(2).to_broadcast([P, TOPK * GT, E]),
                                  expert_no[:, :].unsqueeze(1).to_broadcast([P, TOPK * GT, E]), ALU.is_equal).then_inc(s("onehot_ready"), 1)
                ge(dve, "rank_mm", g)
                ge(dve, "onehot_ready", g + 1)
                dve.tensor_tensor(picked[:, :, :], onehot[:, 0, :, :], onehot[:, 1, :, :], ALU.add).then_inc(s("picked_ready"), 1)

            def place(b, j):
                g = G * b + j
                ge(dve, "rank_mm", g + 1)
                dve.tensor_tensor(slotrow[:, :, :], rb[:, 0:GT * E].rearrange("p (r e) -> p r e", e=E),
                                  region[:, :].unsqueeze(1).to_broadcast([P, GT, E]), ALU.add).then_inc(s("slotrow_ready"), 1)
                dve.tensor_reduce(picked_n[:, :], picked[:, :, :].rearrange("p r e -> p e r"), AX.X, ALU.add).then_inc(s("pickedn_ready"), 1)
                ge(dve, "exp_done", g + 1)
                dve.tensor_reduce(expsum[:, :], expo[:, :, :], AX.X, ALU.add).then_inc(s("expsum_ready"), 1)
                ge(dve, "slotrow_ready", g + 1)
                for k in range(TOPK):
                    ins = dve.tensor_tensor(pickrow[:, k, :, :], onehot[:, k, :, :], slotrow[:, :, :], ALU.mult)
                ins.then_inc(s("pickrow_ready"), 1)
                ge(dve, "expsum_ready", g + 1)
                dve.reciprocal(rsum[:, :], expsum[:, :]).then_inc(s("rsum_ready"), 1)
                ge(dve, "pickedn_ready", g + 1)
                dve.tensor_tensor(carry_f[:, :], carry_f[:, :], picked_n[:, :], ALU.add).then_inc(s("below_ready"), 1)
                ge(dve, "pickrow_ready", g + 1)
                dve.tensor_reduce(slot_f[:, :, :].rearrange("p k r -> p (k r)"), pickrow[:, :, :, :].rearrange("p k r e -> p (k r) e"),
                                  AX.X, ALU.add).then_inc(s("slotf_ready"), 1)
                ids = dest_all[:, b, j * GT:(j + 1) * GT, :] if isinstance(b, int) else \
                    dest_all[:, bass.ds(b, 1), j * GT:(j + 1) * GT, :].rearrange("p a r k -> p (a r) k")
                dve.tensor_copy(token_rows[:, j * GT:(j + 1) * GT, :, DEST].bitcast(I32), ids)
                ge(dve, "below_ready", g + 1)
                dve.tensor_copy(carry[:, :], carry_f[:, :]).then_inc(s("carry_ready"), 1)
                ge(dve, "rsum_ready", g + 1)
                dve.tensor_tensor(token_rows[:, j * GT:(j + 1) * GT, :, GATE], expo[:, :, 0:TOPK],
                                  rsum[:, :].unsqueeze(2).to_broadcast([P, GT, TOPK]), ALU.mult).then_inc(s("gates_ready"), 1)
                ge(dve, "slotf_ready", g + 1)
                dve.tensor_copy(slot[j][:, :, :], slot_f[:, :, :]).then_inc(s("slot_ready"), 1)

            def a2(b, j):
                if exists(b, j, -1):
                    first_sum(*at(b, j, -1))
                if exists(b, j, -2):
                    choose(*at(b, j, -2))
                if exists(b, j, -1):
                    modulate(*at(b, j, -1))
                if exists(b, j, 1):
                    residual(*at(b, j, 1))
                if exists(b, j, -2):
                    place(*at(b, j, -2))
                if exists(b, j, 1):
                    unit(*at(b, j, 1))
                if exists(b, j, -1):
                    rms_norm(*at(b, j, -1))
                if exists(b, j, 2):
                    attend(*at(b, j, 2))

            attend(0, 0)
            residual(0, 0)
            attend(0, 1)
            unit(0, 0)
            steps(dve, a2)

            m = [0]

            def step(ins):
                m[0] += 1
                ins.then_inc(s("tab_step"), 1)
                dve.wait_ge(s("tab_step"), m[0])

            dve.wait_ge(s("count_mm"), 1)
            step(dve.tensor_copy(count[:, :], wb[0:1, 0:E]))
            dve.tensor_tensor(pad_f[:, :], count[:, :], region[0:1, :], ALU.add)
            step(dve.tensor_tensor(cmp_level[:, :, :], count[:, :].unsqueeze(2).to_broadcast([1, E, TOK // P]),
                                   level[:, :].unsqueeze(1).to_broadcast([1, E, TOK // P]), ALU.is_gt))
            dve.tensor_copy(pad_at[:, :], pad_f[:, :]).then_inc(s("pads_ready"), 1)
            step(dve.tensor_reduce(tiles[:, :], cmp_level[:, :, :], AX.X, ALU.add))
            step(dve.tensor_copy(tiles_end[:, 0:1], tiles[:, 0:1]))
            for e in range(1, E):
                step(dve.tensor_tensor(tiles_end[:, e:e + 1], tiles_end[:, e - 1:e], tiles[:, e:e + 1], ALU.add))
            step(dve.tensor_tensor(past, tile_no[:, :].unsqueeze(2).to_broadcast([1, NT, E]),
                                   tiles_end[:, :].unsqueeze(1).to_broadcast([1, NT, E]), ALU.is_ge))
            step(dve.tensor_tensor(past_tiles, past, tiles[:, :].unsqueeze(1).to_broadcast([1, NT, E]), ALU.mult))
            expert, start, row, used, dummy, diff = range(6)
            step(dve.tensor_reduce(tab[:, expert, :], past, AX.X, ALU.add))
            step(dve.tensor_reduce(tab[:, start, :], past_tiles, AX.X, ALU.add))
            step(dve.tensor_scalar(tab[:, used, :], tab[:, expert, :], float(E), None, ALU.is_lt))
            step(dve.tensor_tensor(tab[:, diff, :], tile_no[:, :], tab[:, start, :], ALU.subtract))
            step(dve.tensor_scalar(tab[:, diff, :], tab[:, diff, :], float(P), None, ALU.mult))
            step(dve.tensor_scalar(tab[:, row, :], tab[:, expert, :], float(CAP), None, ALU.mult))
            step(dve.tensor_tensor(tab[:, row, :], tab[:, row, :], tab[:, diff, :], ALU.add))
            step(dve.tensor_scalar(tab[:, row, :], tab[:, row, :], pad_f[:, E - 1:E], None, ALU.subtract))
            step(dve.tensor_tensor(tab[:, row, :], tab[:, row, :], tab[:, used, :], ALU.mult))
            step(dve.tensor_scalar(tab[:, row, :], tab[:, row, :], pad_f[:, E - 1:E], None, ALU.add))
            step(dve.tensor_scalar(tab[:, expert, :], tab[:, expert, :], float(E - 1), None, ALU.min))
            dve.tensor_copy(tile_row[:, :], tab[:, row, :])
            dve.tensor_copy(tile_expert[:, :], tab[:, expert, :]).then_inc(s("tables_ready"), 1)

            def z(b):
                for j in range(G):
                    g = G * b + j
                    hv = group(h_all, b, j)
                    dve.tensor_tensor(by_tile(hv), by_tile(hv), mod_rows(b, MOD_GATE_B), ALU.mult).then_inc(s("z_scaled"), 1)
                    ge(dve, "z_scaled", g + 1)
                    dve.tensor_tensor(hv, hv, group(x_all, b, j), ALU.add).then_inc(s("z_ready"), 1)

            with dve.Fori(0, B) as b:
                z(b)

            def x_out(j, p):
                ge(dve, "x_T", j + 1)
                ge(dve, "v2_mm", j - 1)
                dve.tensor_scalar(xT[p][:, :], xtb[:, 0:P], vec[:, NSCALE:NSCALE + 1], None, ALU.mult).then_inc(s("xT_ready"), 1)

            def gated(j, p):
                ge(dve, "v2_mm", j + 1)
                ge(dve, "g_ready", j + 1)
                ge(dve, "hid_T", j - 1)
                dve.tensor_tensor(hid[p][:, :], vb_[:, 0:HM], act_g[p][:, :], ALU.mult).then_inc(s("hid2_ready"), 1)

            def y_out(j, u):
                ge(dve, "y_mm", j + 1)
                dve.tensor_scalar(y_sb[u][:, :], yb[:, 0:D], slots_in[u][:, GATE:GATE + 1], None, ALU.mult).then_inc(s("y_ready"), 1)

            def b_step(i, u):
                j = UN * i + u
                if u == 0:
                    x_out(j, 0)
                if not (isinstance(j, int) and j < 2):
                    y_out(j - 2, (u - 2) % UN)
                if u < UN - 1:
                    x_out(j + 1, (u + 1) % 2)
                gated(j, u % 2)

            for u in range(UN):
                b_step(0, u)
            with dve.Fori(1, NT // UN) as i:
                for u in range(UN):
                    b_step(i, u)
            y_out(NT - 2, UN - 2)
            y_out(NT - 1, UN - 1)

            def combine(b, j):
                g = G * b + j
                ge(dve, f"pair{j}", 32 * (b + 1))
                ge(dve, f"stored{j}", 16 * b)
                dve.tensor_tensor(res[j][:, :], pair_in[j][0][:, :], pair_in[j][1][:, :], ALU.add).then_inc(s("pairsum"), 1)
                ge(dve, "pairsum", g + 1)
                dve.tensor_tensor(by_tile(res[j][:, :]), by_tile(res[j][:, :]), mod_rows(b, MOD_GATE_B), ALU.mult).then_inc(s("pairgate"), 1)
                ge(dve, "pairgate", g + 1)
                dve.tensor_tensor(res[j][:, :], res[j][:, :], group(h_all, b, j), ALU.add).then_inc(s("res_ready"), 1)

            for j in range(G):
                combine(0, j)
            with dve.Fori(1, B) as b:
                for j in range(G):
                    combine(b, j)

        @block.tensor
        def _(pe):
            for name in ("normed_T", "rank_mm"):
                pe.sem_inc(s(name), 1)
            pe.wait_ge(s("silu_rows"), 1)
            for b in range(B):
                pe.matmul(banks[b][:, :], silu_cb[:, b, :], wmod_sb[:, 0:4 * D], start=True, stop=True)
                pe.matmul(banks[B + b][:, 0:2 * D], silu_cb[:, b, :], wmod_sb[:, 4 * D:6 * D], start=True, stop=True).then_inc(s("mod_mm"), 1)
            pe.wait_ge(s("in_w"), 48)
            pe.wait_ge(s("pool_const"), 2)
            pe.wait_ge(s("mod_lo"), B)
            pe.wait_ge(s("mod_hi"), B)

            def turn(bank, src, done):
                for t in range(GT):
                    ins = pe.transpose(bank[:, t * P:(t + 1) * P], src[:, t * P:(t + 1) * P], ident[:, :])
                ins.then_inc(s(done), 1)

            def kvs(b, j):
                g = G * b + j
                ge(pe, "kfeat_ready", g + 1)
                ge(pe, "v_ready", g + 1)
                if j == 0:
                    ge(pe, "kvs_ready", b)
                for t in range(GT):
                    ins = pe.matmul(kvb[:, 0:D + 1], kfeat[j][:, t * D:(t + 1) * D], vones[j][:, t, 0:D + 1],
                                    start=(j == 0 and t == 0), stop=(j == G - 1 and t == GT - 1))
                ins.then_inc(s("kvs_mm"), 1)

            def a1(b, first):
                for j in range(G):
                    g = G * b + j
                    ge(pe, "unit1_ready", g + 1)
                    ge(pe, "ln1_ready", g - 1)
                    turn(trb[j], unit1[j], "unit1_T")
                    ge(pe, "ln1_ready", g + 1)
                    ge(pe, "v_ready", g)
                    for t in range(GT):
                        ins = pe.matmul(vb[:, t * D:(t + 1) * D], ln1T[j][:, t * P:(t + 1) * P], wv_sb[:, :], start=True, stop=True)
                    ins.then_inc(s("v_mm"), 1)
                    ge(pe, "kfeat_ready", g)
                    for t in range(GT):
                        ins = pe.matmul(kb[:, t * D:(t + 1) * D], ln1T[j][:, t * P:(t + 1) * P], wk_sb[:, :], start=True, stop=True)
                    ins.then_inc(s("k_mm"), 1)
                    if not (first and j == 0):
                        kvs(*at(b, j, -1))
                    ge(pe, "q_ready", g)
                    pe.matmul(qb[:, :], wq_sb[:, :], ln1T[j][:, :], start=True, stop=True).then_inc(s("q_mm"), 1)

            a1(0, True)
            with pe.Fori(1, B) as b:
                a1(b, False)
            kvs(B - 1, 1)

            pe.wait_ge(s("in_w2"), 64)

            def read_out(b, j):
                g = G * b + j
                ge(pe, "kvs_ready", b + 1)
                ge(pe, "attT_ready", g)
                ge(pe, "qf_ready", g + 1)
                for t in range(GT):
                    c0 = (t % 2) * NKV
                    ins = pe.matmul(nb[t // 2][:, c0:c0 + NKV], qf[j][:, t * P:(t + 1) * P], batch(kvs_all, b), start=True, stop=True)
                ins.then_inc(s("num_mm"), 1)

            def att_turn(b, j):
                ge(pe, "att_ready", G * b + j + 1)
                turn(nb[0], att[j], "att_T")

            def project(b, j):
                g = G * b + j
                ge(pe, "attT_ready", g + 1)
                ge(pe, "add1_ready", g)
                ge(pe, "x2_ready", g - 1)
                for t in range(GT):
                    ins = pe.matmul(wb[:, t * D:(t + 1) * D], attT[j][:, t * P:(t + 1) * P], wo_sb[:, :], start=True, stop=True)
                ins.then_inc(s("wo_mm"), 1)

            def unit2_turn(b, j):
                g = G * b + j
                ge(pe, "ln2_ready", g)
                ge(pe, "unit2_ready", g + 1)
                turn(tl, unit2[j], "unit2_T")

            def ffn1(b, j):
                g = G * b + j
                ge(pe, "ln2_ready", g + 1)
                for c in range(FC):
                    ge(pe, "hid_ready", FC * g + c - 1)
                    pe.matmul(fb[c % 2][:, :], w1_sb[:, c * P:(c + 1) * P], ln2T[j][:, :], start=True, stop=True).then_inc(s("ff1_mm"), 1)

            def ffn2(b, j):
                g = G * b + j
                ge(pe, "ffn_ready", g)
                for c in range(FC):
                    ge(pe, "hid_ready", FC * g + c + 1)
                    ins = pe.matmul(ob[:, :], w2_sb[:, c, :], hidT[:, c, :], start=(c == 0), stop=(c == FC - 1))
                ins.then_inc(s("ff2_mm"), 1)

            def gate(b, j, attended):
                g = G * b + j
                ge(pe, "add1_ready", attended)
                ge(pe, "x2_ready", g)
                ge(pe, "ffn_ready", g + 1)
                for t in range(GT):
                    cols, tok = slice(t * D, (t + 1) * D), slice(t * P, (t + 1) * P)
                    pe.matmul(wb[:, cols], attT[j][:, tok], batch(wo_gate, b), start=True, stop=False)
                    ins = pe.matmul(wb[:, cols], ffnT[j][:, tok], batch(gate_diag, b), start=False, stop=True)
                ins.then_inc(s("gate_mm"), 1)

            def turn_normed(b, j):
                g = G * b + j
                ge(pe, "slotrow_ready", g)
                ge(pe, "normed_ready", g + 1)
                for t in range(GT):
                    ins = pe.transpose(rb[:, t * P:(t + 1) * P], token_rows[:, j * GT + t, 0, 0:D], ident[:, :])
                ins.then_inc(s("normed_T"), 1)

            def scores(b, j):
                ge(pe, "xn_ready", G * b + j + 1)
                for t in range(GT):
                    ins = pe.matmul(rb[:, t * E:t * E + RPAD], xnT[j][:, t * P:(t + 1) * P], wr_sb[:, :], start=True, stop=True)
                ins.then_inc(s("score_mm"), 1)

            def rank(b, j):
                g = G * b + j
                ge(pe, "carry_ready", g + 1)
                ge(pe, "picked_ready", g + 1)
                o = rb[:, 0:GT * E]
                pv = picked[:, :, :].rearrange("p r e -> p (r e)")
                pe.matmul(o, before[:, :], pv, start=True, stop=False)
                for r in range(GT - 1):
                    n = GT - 1 - r
                    pe.matmul(o[:, (r + 1) * E:].rearrange("p (r e) -> p r e", e=E), ones[:, :],
                              picked[:, r:r + 1, :].to_broadcast([P, n, E]), start=False, stop=False)
                pe.matmul(o.rearrange("p (r e) -> p r e", e=E), ones[:, :],
                          carry[:, :].unsqueeze(1).to_broadcast([P, GT, E]), start=False, stop=True).then_inc(s("rank_mm"), 1)

            def a2(b, j):
                if exists(b, j, 0):
                    ffn1(b, j)
                if exists(b, j, -2):
                    rank(*at(b, j, -2))
                if exists(b, j, 1):
                    project(*at(b, j, 1))
                if exists(b, j, 0):
                    ffn2(b, j)
                if exists(b, j, 2):
                    read_out(*at(b, j, 2))
                if exists(b, j, 0):
                    gate(b, j, G * b + j + (2 if exists(b, j, 1) else 1))
                if exists(b, j, 1):
                    unit2_turn(*at(b, j, 1))
                if exists(b, j, -1):
                    turn_normed(*at(b, j, -1))
                if exists(b, j, 2):
                    att_turn(*at(b, j, 2))
                if exists(b, j, -1):
                    scores(*at(b, j, -1))

            pe.wait_ge(s("wo_gate_ready"), 1)
            read_out(0, 0)
            att_turn(0, 0)
            project(0, 0)
            read_out(0, 1)
            att_turn(0, 1)
            unit2_turn(0, 0)
            steps(pe, a2)
            ge(pe, "carry_ready", G * B + 1)
            pe.matmul(wb[:, 0:E], ones[:, :], carry[:, :], start=True, stop=True).then_inc(s("count_mm"), 1)

            pe.wait_ge(s("in_exp"), 16 * (1 + HC))
            pe.wait_ge(s("tables_ready"), 1)

            def x_turn(i, u):
                j = UN * i + u
                ge(pe, f"in_s{u}", 16 * (i + 1))
                ge(pe, "xT_ready", j)
                pe.transpose(xtb[:, 0:P], slots_in[u][:, 0:D], ident[:, :]).then_inc(s("x_T"), 1)

            def experts_of(i):
                first = UN * i if isinstance(i, int) and i == 0 else UN * i - 4
                n = UN + (UN * i - first if isinstance(i, int) else 4)
                e = tile_expert[0:1, first:first + n] if isinstance(i, int) else tile_expert[0:1, bass.ds(first, n)]
                values = nc.values_load_multi_w_load_instructions(
                    e, [mybir.EngineType.PE], min_val=0, max_val=E - 1,
                    skip_runtime_bounds_check_because="the table is made above, within these bounds")[1]
                return {u - (n - UN): v for u, v in enumerate(values)}

            def up(j, p, e, half):
                v = up_sb[:, bass.ds(e, 1), half * HM:(half + 1) * HM].rearrange("p a n -> p (a n)")
                if half == 1:
                    ge(pe, "xT_ready", j + 1)
                    ge(pe, "g_ready", j)
                    pe.matmul(gb_[:, 0:HM], xT[p][:, :], v, start=True, stop=True).then_inc(s("g_mm"), 1)
                else:
                    ge(pe, "hid2_ready", j)
                    pe.matmul(vb_[:, 0:HM], xT[p][:, :], v, start=True, stop=True).then_inc(s("v2_mm"), 1)

            def hid_turn(j, p):
                ge(pe, "hid2_ready", j + 1)
                ge(pe, "hT_ready", 2 * j)
                for c in range(HC):
                    n = min(P, HM - c * P)
                    ins = pe.transpose(htb[0:n, c * P:(c + 1) * P], hid[p][:, c * P:c * P + n], ident[:, :])
                ins.then_inc(s("hid_T"), 1)

            def down(j, p, e):
                ge(pe, "hT_ready", 2 * (j + 1))
                ge(pe, "y_ready", j)
                for c in range(HC):
                    n = min(P, HM - c * P)
                    w = down_sb[0:n, bass.ds(e, 1), c * D:(c + 1) * D].rearrange("p a n -> p (a n)")
                    ins = pe.matmul(yb[:, 0:D], hT[p][0:n, c * P:(c + 1) * P], w, start=(c == 0), stop=(c == HC - 1))
                ins.then_inc(s("y_mm"), 1)

            def b_step(i, u, experts):
                j = UN * i + u
                if u == 0:
                    x_turn(i, 0)
                if not (isinstance(j, int) and j < 2):
                    down(j - 2, u % 2, experts[u - 2])
                if not (isinstance(j, int) and j < 1):
                    hid_turn(j - 1, (u + 1) % 2)
                up(j, u % 2, experts[u], 1)
                if u < UN - 1:
                    x_turn(i, u + 1)
                up(j, u % 2, experts[u], 0)

            experts = experts_of(0)
            for u in range(UN):
                b_step(0, u, experts)
            with pe.Fori(1, NT // UN) as i:
                experts = experts_of(i)
                for u in range(UN):
                    b_step(i, u, experts)
            experts = experts_of(NT // UN - 1)
            down(NT - 2, 0, experts[UN - 2])
            hid_turn(NT - 1, 1)
            down(NT - 1, 1, experts[UN - 1])


def kernel(**inputs):
    import numpy as np
    import concourse.bacc as bacc
    from concourse.bass_utils import run_bass_kernel_spmd as run

    a = {k.replace("L0_", ""): np.asarray(v) for k, v in inputs.items()}
    columns = [a["attn_gamma1"], a["attn_beta1"], a["ffn_norm_scale"], a["attn_b2"], *a["attn_b1"].reshape(FC, P)]
    arrays = {
        "x": a["attn_x"],
        "c_t": a["c"].T,
        "wmod": a["wmod"],
        "vecs": np.stack(columns, axis=1),
        "wq": a["attn_wq"].reshape(D, D),
        "wk": a["attn_wk"].reshape(D, D),
        "wv": a["attn_wv"].reshape(D, D),
        "wo": a["attn_wo"].reshape(D, D),
        "w1": a["attn_w1"],
        "w2": a["attn_w2"],
        "wr_t": a["ffn_w_router"].T,
        "w_up": a["ffn_w_up"].transpose(2, 0, 1),
        "w_down": a["ffn_w_down"].transpose(2, 0, 1),
    }
    nc = bacc.Bacc("TRN2", target_bir_lowering=False, num_devices=1)
    arrays = {f"in_{k}": np.ascontiguousarray(v) for k, v in arrays.items()}
    args = [nc.dram_tensor(k, v.shape, mybir.dt.from_np(v.dtype), kind="ExternalInput").ap() for k, v in arrays.items()]
    out = nc.dram_tensor("out", (B, L, D), F32, kind="ExternalOutput").ap()
    build(nc, *args, out)
    r = run(nc, [arrays], core_ids=[0])
    return r.results[0]["out"]
```

```python
from contextlib import ExitStack

import concourse.bass as bass
from concourse import mybir

F32 = mybir.dt.float32
BF16 = mybir.dt.bfloat16
I32 = mybir.dt.int32
U32 = mybir.dt.uint32
ALU = mybir.AluOpType
ACT = mybir.ActivationFunctionType
AX = mybir.AxisListType

P = 128
B, L, D = 4, 1024, 128
H, DH = 16, 8
F = 512
FC = F // P
E, TOPK, HM = 8, 2, 352
HC = -(-HM // P)
R = L // P
GT = 4
G = R // GT
GN = GT * D
NKV = D + H
STAB = 0.001
EPS_OUT, EPS_IN = 1e-5, 1e-6
TOK = B * L
CAP = TOK + P
ROW = D + 2
GATE, DEST = D, D + 1
NT = 72
UN = 8
NOWHERE = 1 << 20
RPAD = 96
MOD_SHIFT_A, MOD_SCALE_A, MOD_GATE_A, MOD_SHIFT_B, MOD_SCALE_B, MOD_GATE_B = range(6)
GAMMA, BETA, NSCALE, BIAS2, BIAS1 = 0, 1, 2, 3, 4


def build(nc, x, c_t, wmod, vecs, wq, wk, wv, wo, w1, w2, wr_t, w_up, w_down, out):
    rows_dram = nc.dram_tensor("expert_rows", (E * CAP, ROW), F32).ap()
    pair_dram = nc.dram_tensor("pair_outputs", (TOPK * TOK, D), F32).ap()

    with ExitStack() as ctx:
        def sb(name, shape, dt=F32):
            return ctx.enter_context(nc.sbuf_tensor(name, shape, dt))

        def sem(name):
            return ctx.enter_context(nc.semaphore(name))

        cT = sb("cT", [P, B])
        silu_c = sb("silu_c", [P, B])
        silu_cb = sb("silu_cb", [P, B, P])
        wmod_sb = sb("wmod_sb", [P, 6 * D])
        mod = sb("mod", [P, B, 6, D])
        vec = sb("vec", [P, 4 + FC])
        wq_sb, wk_sb, wv_sb, wo_sb = (sb(n, [P, D]) for n in ("wq_sb", "wk_sb", "wv_sb", "wo_sb"))
        w1_sb = sb("w1_sb", [P, F])
        w2_sb = sb("w2_sb", [P, FC, D])
        wr_sb = sb("wr_sb", [P, RPAD])
        up_sb = sb("up_sb", [P, E, 2 * HM])
        down_sb = sb("down_sb", [P, E, HC * D])
        ident = sb("ident", [P, P])
        before = sb("before", [P, P], BF16)
        ones = sb("ones", [P, P], BF16)
        same_head = sb("same_head", [P, NKV])
        neg_half = sb("neg_half", [P, GT])
        expert_no = sb("expert_no", [P, E])
        region = sb("region", [P, E])
        tile_no = sb("tile_no", [1, NT])
        level = sb("level", [1, TOK // P])
        dest_all = sb("dest_all", [P, B, R, TOPK], I32)
        gate_diag = sb("gate_diag", [P, B, P])
        gate_sign = sb("gate_sign", [P, B, 2, D])
        x_all = sb("x_all", [P, B, R * D])
        h_all = sb("h_all", [P, B, R * D])
        q_all = sb("q_all", [P, B, G * GN])
        kvs_all = sb("kvs_all", [P, B, NKV])
        wo_gate = sb("wo_gate", [P, B, D])
        gated_h = sb("gated_h", [P, GN])
        centred = [sb(f"centred{j}", [P, GN]) for j in range(G)]
        unit1 = [sb(f"unit1{j}", [P, GN]) for j in range(G)]
        ln1T = [sb(f"ln1T{j}", [P, GN]) for j in range(G)]
        kfeat = [sb(f"kfeat{j}", [P, GN]) for j in range(G)]
        vones = [sb(f"vones{j}", [P, GT, D + 4]) for j in range(G)]
        def stats(name):
            return [(sb(f"{name}_st{j}", [P, GT, 6]), sb(f"{name}_mv{j}", [P, GT, 2]),
                     sb(f"{name}_ve{j}", [P, GT]), sb(f"{name}_rs{j}", [P, GT])) for j in range(G)]
        st_x, st_h, st_a, st_y = stats("x"), stats("h"), stats("a"), stats("y")
        sumsq = [sb(f"sumsq{j}", [P, GT]) for j in range(G)]
        ms_eps = [sb(f"ms_eps{j}", [P, GT]) for j in range(G)]
        rms = [sb(f"rms{j}", [P, GT]) for j in range(G)]
        rden = sb("rden", [P, GT, H])
        att = [sb(f"att{j}", [P, GN]) for j in range(G)]
        attT = [sb(f"attT{j}", [P, GN]) for j in range(G)]
        add1 = [sb(f"add1{j}", [P, GN]) for j in range(G)]
        unit2 = [sb(f"unit2{j}", [P, GN]) for j in range(G)]
        hidT = sb("hidT", [P, FC, GN])
        yhat = sb("yhat", [P, GN])
        square = sb("square", [P, GN])
        ffnT, ln2T, xnT, qf = centred, ln1T, kfeat, unit1
        score = sb("score", [P, GT, E])
        top = sb("top", [P, GT, E])
        top_ix = sb("top_ix", [P, GT, E], U32)
        top_f = sb("top_f", [P, TOPK, GT])
        onehot = sb("onehot", [P, TOPK, GT, E])
        picked = sb("picked", [P, GT, E], BF16)
        picked_n = sb("picked_n", [P, E])
        carry = sb("carry", [P, E], BF16)
        carry_f = sb("carry_f", [P, E])
        expin = sb("expin", [P, GT, E])
        expo = sb("expo", [P, GT, E])
        expsum = sb("expsum", [P, GT])
        rsum = sb("rsum", [P, GT])
        slotrow = sb("slotrow", [P, GT, E])
        pickrow = sb("pickrow", [P, TOPK, GT, E])
        slot_f = sb("slot_f", [P, TOPK, GT])
        slot = [sb(f"slot{j}", [P, TOPK, GT], U32) for j in range(G)]
        token_rows = sb("token_rows", [P, R, TOPK, ROW])
        pad_rows = sb("pad_rows", [P, ROW])
        count = sb("count", [1, E])
        cmp_level = sb("cmp_level", [1, E, TOK // P])
        tiles = sb("tiles", [1, E])
        tiles_end = sb("tiles_end", [1, E])
        q_free = q_all[:, :, :].rearrange("p b n -> p (b n)")
        hid_free = hidT[:, :, :].rearrange("p c n -> p (c n)")
        past = q_free[0:1, 0:NT * E].rearrange("p (t e) -> p t e", t=NT)
        past_tiles = q_free[0:1, NT * E:2 * NT * E].rearrange("p (t e) -> p t e", t=NT)
        tab = sb("tab", [1, 6, NT])
        pad_f = sb("pad_f", [1, E])
        pad_at = sb("pad_at", [1, E], I32)
        tile_row = sb("tile_row", [1, NT], I32)
        tile_expert = sb("tile_expert", [1, NT], I32)
        slots_in = [token_rows[:, s_, 0, :] for s_ in range(UN)]
        xT = [sb(f"xT{s}", [P, P]) for s in range(2)]
        up_now = hid_free[:, 0:4 * HC * P].rearrange("p (s h n) -> p s h n", s=2, h=2)
        act_g = [q_free[:, (6 * GT + s_ * HC) * P:(6 * GT + (s_ + 1) * HC) * P] for s_ in range(2)]
        hT = [sb(f"hT{s}", [P, HC * P]) for s in range(2)]
        y_sb = [sb(f"y_sb{s}", [P, D]) for s in range(UN)]
        banks = [ctx.enter_context(nc.psum_tensor(f"bank{i}", [P, 512], F32)) for i in range(8)]
        trb, kb, vb, qb, kvb = banks[0:2], banks[2], banks[3], banks[4], banks[5]
        rb, tl, wb, ob, fb, nb = banks[0], banks[1], banks[2], banks[3], banks[4:6], banks[6:8]
        xtb, gb_, vb_, yb = banks[0], banks[1], banks[2], banks[5]

        S = {}

        def s(name):
            if name not in S:
                S[name] = sem(name)
            return S[name]

        STARTED = {"rows_free", "normed_T", "exp_done", "rank_mm", "gates_ready", "ms_ready"}

        def ge(eng, name, value):
            if isinstance(value, int) and value <= 0:
                return
            eng.wait_ge(s(name), value + (name in STARTED))

        def ge_apart(eng, name, value, passed):
            ge(eng, name, value)
            if not isinstance(value, int):
                eng.sem_inc(s(passed), 1)

        for name in ("sp_passed", "act_passed", "pool_passed", "dve_passed", "in_c", "in_vec", "in_x0", "in_x1", "in_x2", "in_x3", "in_w", "in_w2", "in_exp",
                     "k_const", "pool_const", "silu_done", "silu_rows", "mod_mm", "mod_hi", "mod_lo", "mod_ready", "gate_step",
                     "x_raw", "x_stats", "x_ve", "x_rstd", "centred_ready", "h_ready", "h_raw", "h_stats",
                     "h_ve", "h_rstd", "unit1_ready", "unit1_T", "ln1_ready", "k_mm", "v_mm", "q_mm",
                     "kfeat_ready", "v_ready", "q_ready", "kvs_mm", "kvs_ready",
                     "qf_ready", "num_mm", "rden_ready", "att_ready", "att_T", "attT_ready", "wo_gate_ready", "half_base", "wo_mm", "add1_ready",
                     "a_raw", "a_stats", "a_ve", "a_rstd", "base_ready", "unit2_ready", "unit2_T", "ln2_ready",
                     "ff1_mm", "hid_ready", "ff2_mm", "ffn_ready", "gate_mm", "x2_ready", "y_raw", "y_stats",
                     "y_ve", "y_rstd", "yhat_ready", "h3_ready", "square_done", "ms_ready", "rms_ready", "normed_ready",
                     "rows_free", "doubled", "normed_T", "xn_ready", "score_mm", "score_ready", "top_ready", "topix_ready", "topf_ready", "onehot_ready",
                     "picked_ready", "pickedn_ready", "carry_ready", "below_ready", "rank_mm", "expin_ready", "exp_done", "expsum_ready", "rsum_ready",
                     "gates_ready", "slotrow_ready", "pickrow_ready", "slotf_ready", "slot_ready", "scattered0", "scattered1",
                     "count_mm", "tab_step", "pads_ready", "tables_ready", "pads_written",
                     "dve_z_scaled", "pool_z_scaled", "dve_z_ready", "pool_z_ready",
                     *(f"in_s{u}" for u in range(UN)), "x_T", "xT_ready", "g_mm", "g_ready", "v2_mm", 
                     "up_ready", "up_padded", "hT_ready", "y_mm", "y_ready", *(f"out_s{u}" for u in range(UN)),
                     *(f"pair{b}" for b in range(B)), "pairsum0", "pairsum1", "pairgate", "res_ready", "stored"):
            s(name)

        block = ctx.enter_context(nc.Block())

        def batch(t, b):
            return t[:, b, :] if isinstance(b, int) else t[:, bass.ds(b, 1), :].rearrange("p a n -> p (a n)")

        def group(t, b, j):
            return t[:, b, j * GN:(j + 1) * GN] if isinstance(b, int) else \
                t[:, bass.ds(b, 1), j * GN:(j + 1) * GN].rearrange("p a n -> p (a n)")

        def tile(t, b, r):
            return t[:, b, r * D:(r + 1) * D] if isinstance(b, int) else \
                t[:, bass.ds(b, 1), r * D:(r + 1) * D].rearrange("p a n -> p (a n)")

        def mod_rows(b, which):
            return mod_row(b, which).unsqueeze(1).to_broadcast([P, GT, D])

        def mod_row(b, which):
            return mod[:, b, which, :] if isinstance(b, int) else \
                mod[:, bass.ds(b, 1), which, :].rearrange("p a n -> p (a n)")

        def by_tile(ap):
            return ap.rearrange("p (t d) -> p t d", t=GT)

        def at(b, j, step):
            return b + (j + step) // G, (j + step) % G

        def exists(b, j, step):
            return not isinstance(b, int) or 0 <= G * b + j + step < G * B

        def slot_tiles(eng, start, tile_step):
            it = start(0)
            for u in range(UN):
                tile_step(0, u, it)
            with eng.Fori(1, NT // UN - 1) as i:
                it = start(i)
                for u in range(UN):
                    tile_step(i, u, it)
            it = start(NT // UN - 1)
            for u in range(UN):
                tile_step(NT // UN - 1, u, it)

        def is_last(i, u):
            return isinstance(i, int) and UN * i + u == NT - 1

        def groups(eng, a1):
            for j in range(G):
                a1(0, j)
            with eng.Fori(1, B - 1) as b:
                for j in range(G):
                    a1(b, j)
            for j in range(G):
                a1(B - 1, j)

        def steps(eng, a2):
            for j in range(G):
                a2(0, j)
            with eng.Fori(1, B - 1) as b:
                for j in range(G):
                    a2(b, j)
            for g in range(G * (B - 1), G * B + 2):
                a2(g // G, g % G)

        def z(eng, b):
            mine, before_ = ("dve_z", 0) if eng is nc.vector else ("pool_z", G)
            for j in range(G):
                g = G * b + j - before_
                hv = group(h_all, b, j)
                eng.tensor_tensor(by_tile(hv), by_tile(hv), mod_rows(b, MOD_GATE_B), ALU.mult).then_inc(s(mine + "_scaled"), 1)
                ge_apart(eng, mine + "_scaled", g + 1, "dve_passed" if eng is nc.vector else "pool_passed")
                eng.tensor_tensor(hv, hv, group(x_all, b, j), ALU.add).then_inc(s(mine + "_ready"), 1)

        def pair_sum(eng, b, j):
            eng.tensor_tensor(group(q_all, b, j), group(q_all, b, j), group(x_all, b, j), ALU.add).then_inc(s(f"pairsum{j}"), 1)

        @block.sync
        def _(sp):
            sp.sem_inc(s("rows_free"), 1)
            xv = x.rearrange("b (p r) d -> b p (r d)", p=P)
            sp.dma_start(cT[:, :], c_t).then_inc(s("in_c"), 16)
            sp.dma_start(x_all[:, 0, :], xv[0]).then_inc(s("in_x0"), 16)
            sp.dma_start(wmod_sb[:, :], wmod).then_inc(s("in_c"), 16)
            sp.dma_start(vec[:, :], vecs).then_inc(s("in_vec"), 16)
            for t, w in ((wk_sb, wk), (wv_sb, wv), (wq_sb, wq)):
                sp.dma_start(t[:, :], w).then_inc(s("in_w"), 16)
            for b in range(1, B):
                sp.dma_start(x_all[:, b, :], xv[b]).then_inc(s(f"in_x{b}"), 16)
            sp.dma_start(wo_sb[:, :], wo).then_inc(s("in_w2"), 16)
            sp.dma_start(w1_sb[:, :], w1).then_inc(s("in_w2"), 16)
            sp.dma_start(w2_sb[:, :, :], w2.rearrange("(c p) e -> p c e", p=P)).then_inc(s("in_w2"), 16)
            sp.wait_ge(s("pool_const"), 1)
            sp.dma_start(wr_sb[:, 0:E], wr_t).then_inc(s("in_w2"), 16)
            sp.dma_start(up_sb[:, :, :].rearrange("p e n -> p (e n)"), w_up.rearrange("p e n -> p (e n)")).then_inc(s("in_exp"), 16)
            for c in range(HC):
                n = min(P, HM - c * P)
                sp.dma_start(down_sb[0:n, :, c * D:(c + 1) * D], w_down[c * P:c * P + n]).then_inc(s("in_exp"), 16)

            def free_rows(b, j):
                ge_apart(sp, f"scattered{j}", 16 * TOPK * GT * (b + 1), "sp_passed")
                sp.sem_inc(s("rows_free"), 1)

            with sp.Fori(0, B - 1) as b:
                for j in range(G):
                    free_rows(b, j)

            sp.wait_ge(s("pads_ready"), 1)
            pad_rows_at = nc.values_load_multi_w_load_instructions(
                pad_at[0:1, 0:E], [mybir.EngineType.SP], min_val=0, max_val=E * CAP - P,
                skip_runtime_bounds_check_because="an expert has at most as many rows as there are tokens")[1]
            for e in range(E):
                sp.dma_start(rows_dram[bass.ds(pad_rows_at[e], P), :], pad_rows[:, :]).then_inc(s("pads_written"), 16)
            sp.wait_ge(s("pads_written"), 16 * E)
            for j in range(G):
                sp.wait_ge(s(f"scattered{j}"), 16 * TOPK * GT * B)
            sp.wait_ge(s("tables_ready"), 1)

            def load_slots(i, first):
                t = tile_row[0:1, 0:UN] if first else tile_row[0:1, bass.ds(UN * i, UN)]
                rows = nc.values_load_multi_w_load_instructions(
                    t, [mybir.EngineType.SP], min_val=0, max_val=E * CAP - P,
                    skip_runtime_bounds_check_because="the chip makes the table within these bounds")[1]
                for u in range(UN):
                    if not first:
                        ge_apart(sp, f"out_s{u}", 16 * i, "sp_passed")
                    sp.dma_start(slots_in[u][:, :], rows_dram[bass.ds(rows[u], P), :]).then_inc(s(f"in_s{u}"), 16)

            load_slots(0, True)
            with sp.Fori(1, NT // UN) as i:
                load_slots(i, False)

            for u in range(UN):
                ge(sp, f"out_s{u}", 16 * (NT // UN))
            pv = pair_dram.rearrange("(k b p r) d -> k b p (r d)", k=TOPK, b=B, p=P)
            ov = out.rearrange("b (p r) d -> b p (r d)", p=P)

            sp.wait_ge(s("dve_z_ready"), G)
            sp.wait_ge(s("pool_z_ready"), G * (B - 1))
            for b in range(B):
                for k, place_ in enumerate((q_all, x_all)):
                    sp.dma_start(place_[:, b, :], pv[k, b]).then_inc(s(f"pair{b}"), 16)
            for b in range(B):
                for j in range(G):
                    sp.wait_ge(s("res_ready"), G * b + j + 1)
                    sp.dma_start(ov[b, :, j * GN:(j + 1) * GN], group(h_all, b, j)).then_inc(s("stored"), 16)
            sp.wait_ge(s("stored"), 16 * G * B)

        @block.gpsimd
        def _(pool):
            pool.sem_inc(s("ms_ready"), 1)
            n = [0]

            def step(ins):
                n[0] += 1
                ins.then_inc(s("k_const"), 1)
                pool.wait_ge(s("k_const"), n[0])

            pool.memset(wr_sb[:, :], 0.0).then_inc(s("pool_const"), 1)
            pool.memset(neg_half[:, :], -0.5)
            step(pool.memset(ident[:, :], 0.0))
            step(pool.affine_select(out=ident[:, :], in_=ident[:, :], compare_op=ALU.not_equal, fill=1.0, base=0,
                                    pattern=[[-1, P]], channel_multiplier=1))
            pool.memset(ones[:, :], 1.0)
            pool.memset(before[:, :], 1.0)
            for j in range(G):
                pool.memset(vones[j][:, :, D:D + 1], 1.0)
            pool.memset(pad_rows[:, :], 0.0)
            step(pool.memset(same_head[:, :], 1.0))
            step(pool.affine_select(out=before[:, :], in_=before[:, :], compare_op=ALU.is_gt, fill=0.0, base=0,
                                    pattern=[[1, P]], channel_multiplier=-1))
            for cols, reps in ((same_head[:, 0:D], [0, DH]), (same_head[:, D:NKV], [0, 1])):
                v = cols.rearrange("p (h d) -> p h d", h=H)
                step(pool.affine_select(out=v, in_=v, compare_op=ALU.is_ge, fill=0.0, base=0,
                                        pattern=[[-DH, H], reps], channel_multiplier=1))
                step(pool.affine_select(out=v, in_=v, compare_op=ALU.is_ge, fill=0.0, base=DH - 1,
                                        pattern=[[DH, H], reps], channel_multiplier=-1))
            pool.iota(pad_rows[:, DEST:DEST + 1].bitcast(I32), pattern=[[0, 1]], base=NOWHERE, channel_multiplier=1)
            pool.iota(expert_no[:, :], pattern=[[1, E]], base=0, channel_multiplier=0, allow_small_or_imprecise_dtypes=True)
            pool.iota(region[:, :], pattern=[[CAP, E]], base=0, channel_multiplier=0, allow_small_or_imprecise_dtypes=True)
            pool.iota(tile_no[:, :], pattern=[[1, NT]], base=0, channel_multiplier=0, allow_small_or_imprecise_dtypes=True)
            pool.iota(level[:, :], pattern=[[P, TOK // P]], base=0, channel_multiplier=0, allow_small_or_imprecise_dtypes=True)
            step(pool.iota(dest_all[:, :, :, :], pattern=[[L, B], [1, R], [TOK, TOPK]], base=0, channel_multiplier=R))
            pool.memset(square[0:1, 0:1], 0.0).then_inc(s("pool_const"), 1)

            def rsqrt(name, mv, ve, rs, eps, g):
                ge_apart(pool, f"{name}_stats", g + 1, "pool_passed")
                pool.tensor_scalar(ve[:, :], mv[:, :, 1], eps, None, ALU.add).then_inc(s(f"{name}_ve"), 1)
                ge(pool, f"{name}_ve", g + 1)
                pool.tensor_tensor(rs[:, :], ve[:, :], neg_half[:, :], ALU.pow).then_inc(s(f"{name}_rstd"), 1)

            def base(b, j):
                ge(pool, "h_ready", G * b + j + 1)
                ge_apart(pool, "half_base", G * b + j, "pool_passed")
                pool.tensor_tensor(by_tile(gated_h[:, :]), by_tile(group(h_all, b, j)), mod_rows(b, MOD_GATE_A), ALU.mult)\
                    .then_inc(s("half_base"), 1)
                ge_apart(pool, "half_base", G * b + j + 1, "pool_passed")
                pool.tensor_tensor(group(x_all, b, j), gated_h[:, :], group(x_all, b, j), ALU.add).then_inc(s("base_ready"), 1)

            def a1(b, j):
                rsqrt("h", *st_h[j][1:], EPS_IN, G * b + j)
                if exists(b, j, 2):
                    rsqrt("x", *st_x[j][1:], EPS_OUT, G * b + j + 2)
                if isinstance(b, int) and G * b + j == 0:
                    pool.wait_ge(s("mod_ready"), 2)
                base(b, j)

            rsqrt("x", *st_x[0][1:], EPS_OUT, 0)
            rsqrt("x", *st_x[1][1:], EPS_OUT, 1)
            groups(pool, a1)

            pool.wait_ge(s("in_w2"), 64)
            pool.tensor_tensor(wo_gate[:, :, :], wo_sb[:, :].unsqueeze(1).to_broadcast([P, B, D]), mod[:, :, MOD_GATE_A, :],
                               ALU.mult).then_inc(s("wo_gate_ready"), 1)

            def rms_rsqrt(b, j):
                g = G * b + j
                ge_apart(pool, "square_done", g + 1, "pool_passed")
                pool.tensor_scalar(ms_eps[j][:, :], sumsq[j][:, :], 1.0 / D, EPS_IN, ALU.mult, ALU.add).then_inc(s("ms_ready"), 1)
                ge(pool, "ms_ready", g + 1)
                pool.tensor_tensor(rms[j][:, :], ms_eps[j][:, :], neg_half[:, :], ALU.pow).then_inc(s("rms_ready"), 1)

            def scatter(b, j):
                g = G * b + j
                ge(pool, "slot_ready", g + 1)
                ge(pool, "gates_ready", g + 1)
                ge(pool, "normed_ready", g + 1)
                ge_apart(pool, "doubled", g + 1, "pool_passed")
                for t in range(GT):
                    for k in range(TOPK):
                        pool.indirect_dma_start(rows_dram, bass.IndirectOffsetOnAxis(ap=slot[j][:, k, t:t + 1], axis=0),
                                                token_rows[:, j * GT + t, k, :], None, bounds_check=E * CAP - 1,
                                                oob_is_err=False).then_inc(s(f"scattered{j}"), 16)

            def a2(b, j):
                if exists(b, j, -1):
                    bb, jj = at(b, j, -1)
                    rsqrt("y", *st_y[jj][1:], EPS_OUT, G * bb + jj)
                if exists(b, j, 1):
                    bb, jj = at(b, j, 1)
                    rsqrt("a", *st_a[jj][1:], EPS_IN, G * bb + jj)
                if exists(b, j, -1):
                    rms_rsqrt(*at(b, j, -1))
                if exists(b, j, -2):
                    scatter(*at(b, j, -2))

            rsqrt("a", *st_a[0][1:], EPS_IN, 0)
            steps(pool, a2)

            with pool.Fori(1, B) as b:
                z(pool, b)

            def send(i, u):
                ge_apart(pool, "y_ready", UN * i + u + 1, "pool_passed")
                pool.indirect_dma_start(pair_dram, bass.IndirectOffsetOnAxis(ap=slots_in[u][:, DEST:DEST + 1].bitcast(U32), axis=0),
                                        y_sb[u][:, :], None, bounds_check=TOPK * TOK - 1,
                                        oob_is_err=False).then_inc(s(f"out_s{u}"), 16)

            with pool.Fori(0, NT // UN) as i:
                for u in range(UN):
                    send(i, u)

            for b in range(B):
                pool.wait_ge(s(f"pair{b}"), 32)
                pair_sum(pool, b, 1)

        @block.scalar
        def _(act):
            for name in ("exp_done",):
                act.sem_inc(s(name), 1)
            gamma, beta = vec[:, GAMMA:GAMMA + 1], vec[:, BETA:BETA + 1]
            act.wait_ge(s("in_c"), 32)
            act.activation(silu_c[:, :], cT[:, :], ACT.Silu).then_inc(s("silu_done"), 1)
            for b in range(B):
                act.wait_ge(s("mod_mm"), b + 1)
                act.activation(mod[:, b, 0:4, :].rearrange("p a d -> p (a d)"), banks[b][:, :], ACT.Copy).then_inc(s("mod_lo"), 1)
            act.wait_ge(s("in_vec"), 16)

            def a1(b):
                for j in range(G):
                    g = G * b + j
                    ge(act, "unit1_T", g + 1)
                    ge(act, "k_mm", g - 1)
                    ge(act, "v_mm", g - 1)
                    ge(act, "q_mm", g - 1)
                    act.activation(ln1T[j][:, :], trb[j][:, :], ACT.Identity, bias=beta, scale=gamma).then_inc(s("ln1_ready"), 1)
                    ge(act, "v_mm", g + 1)
                    ge(act, "kvs_mm", g - 1)
                    act.activation(vones[j][:, :, 0:D], by_tile(vb[:, :]), ACT.Copy).then_inc(s("v_ready"), 1)

            a1(0)
            with act.Fori(1, B) as b:
                a1(b)

            def q_copy(b, j):
                g = G * b + j
                ge(act, "num_mm", g - 1)
                ge_apart(act, "q_ready", g + 1, "act_passed")
                act.activation(qf[j][:, :], group(q_all, b, j), ACT.Copy).then_inc(s("qf_ready"), 1)

            def att_out(b, j):
                g = G * b + j
                ge(act, "att_T", g + 1)
                ge(act, "gate_mm", g - 1)
                act.activation(attT[j][:, :], nb[0][:, :], ACT.Copy).then_inc(s("attT_ready"), 1)

            def ln2_out(b, j):
                g = G * b + j
                ge(act, "unit2_T", g + 1)
                ge(act, "ff1_mm", FC * (g - 1))
                act.activation(ln2T[j][:, :], tl[:, :], ACT.Identity, bias=beta, scale=gamma).then_inc(s("ln2_ready"), 1)

            def gelu1(b, j):
                g = G * b + j
                for c in range(FC):
                    ge(act, "ff1_mm", FC * g + c + 1)
                    if c == 0:
                        ge(act, "ff2_mm", g)
                    act.activation(hidT[:, c, :], fb[c % 2][:, :], ACT.Gelu, bias=vec[:, BIAS1 + c:BIAS1 + c + 1]).then_inc(s("hid_ready"), 1)

            def gelu2(b, j):
                g = G * b + j
                ge(act, "ff2_mm", g + 1)
                ge(act, "gate_mm", g - 1)
                act.activation(ffnT[j][:, :], ob[:, :], ACT.Gelu, bias=vec[:, BIAS2:BIAS2 + 1]).then_inc(s("ffn_ready"), 1)

            def squares(b, j):
                g = G * b + j
                ge(act, "h3_ready", g + 1)
                ge(act, "ms_ready", g - 1)
                ge_apart(act, "square_done", g, "act_passed")
                for t in range(GT):
                    ins = act.activation(square[:, t * D:(t + 1) * D], tile(h_all, b, j * GT + t), ACT.Square,
                                         accum_out=sumsq[j][:, t:t + 1])
                ins.then_inc(s("square_done"), 1)

            def double(b, j):
                g = G * b + j
                ge_apart(act, "normed_ready", g + 1, "act_passed")
                for t in range(GT):
                    ins = act.activation(token_rows[:, j * GT + t, 1, 0:D], tile(h_all, b, j * GT + t), ACT.Copy,
                                         scale=rms[j][:, t:t + 1])
                ins.then_inc(s("doubled"), 1)

            def xn_out(b, j):
                ge(act, "normed_T", G * b + j + 1)
                act.activation(xnT[j][:, :], rb[:, :], ACT.Copy, scale=vec[:, NSCALE:NSCALE + 1]).then_inc(s("xn_ready"), 1)

            def exps(b, j):
                g = G * b + j
                ge(act, "expin_ready", g + 1)
                ge(act, "gates_ready", g)
                act.activation(expo[:, :, :], expin[:, :, :], ACT.Exp).then_inc(s("exp_done"), 1)

            def a2(b, j):
                if exists(b, j, 1) and not (isinstance(b, int) and G * b + j == 0):
                    att_out(*at(b, j, 1))
                if exists(b, j, 2):
                    q_copy(*at(b, j, 2))
                if exists(b, j, 0):
                    gelu1(b, j)
                if exists(b, j, -2):
                    exps(*at(b, j, -2))
                if exists(b, j, -1):
                    squares(*at(b, j, -1))
                if exists(b, j, 0):
                    gelu2(b, j)
                if exists(b, j, 1):
                    ln2_out(*at(b, j, 1))
                if exists(b, j, -1):
                    xn_out(*at(b, j, -1))
                    double(*at(b, j, -1))

            q_copy(0, 0)
            q_copy(0, 1)
            att_out(0, 0)
            att_out(0, 1)
            ln2_out(0, 0)
            steps(act, a2)

            def fetch_up(j, p, e):
                ge_apart(act, "v2_mm", j - 1, "act_passed")
                act.activation(up_now[:, p, :, 0:HM], up_sb[:, bass.ds(e, 1), :].rearrange("p a (h n) -> p (a h) n", h=2),
                               ACT.Copy).then_inc(s("up_ready"), 1)

            def silu(j, p):
                ge(act, "hT_ready", j - 1)
                ge(act, "g_mm", j + 1)
                act.activation(act_g[p][:, :], gb_[:, 0:HC * P], ACT.Silu).then_inc(s("g_ready"), 1)

            def experts_of(i):
                n = UN if isinstance(i, int) and i == NT // UN - 1 else 2 * UN
                e = tile_expert[0:1, UN * i:UN * i + n] if isinstance(i, int) else tile_expert[0:1, bass.ds(UN * i, n)]
                return nc.values_load_multi_w_load_instructions(
                    e, [mybir.EngineType.Activation], min_val=0, max_val=E - 1,
                    skip_runtime_bounds_check_because="the chip makes the table within these bounds")[1]

            def tile_step(i, u, experts):
                j = UN * i + u
                if not is_last(i, u):
                    fetch_up(j + 1, (u + 1) % 2, experts[u + 1])
                silu(j, u % 2)

            act.wait_ge(s("in_exp"), 16 * (1 + HC))
            act.wait_ge(s("tables_ready"), 1)
            act.wait_ge(s("ff2_mm"), G * B)
            fetch_up(0, 0, experts_of(0)[0])
            slot_tiles(act, experts_of, tile_step)

        @block.vector
        def _(dve):
            for name in ("gates_ready",):
                dve.sem_inc(s(name), 1)
            dve.wait_ge(s("silu_done"), 1)
            dve.tensor_copy(silu_cb[:, :, :], silu_c[:, :].unsqueeze(2).to_broadcast([P, B, P])).then_inc(s("silu_rows"), 1)

            def norm_stats(name, st, src, g):
                for t in range(GT):
                    ins = dve.bn_stats(st[0][:, t, :], src[t])
                ins.then_inc(s(f"{name}_raw"), 1)
                ge_apart(dve, f"{name}_raw", g + 1, "dve_passed")
                for t in range(GT):
                    ins = dve.bn_aggr(st[1][:, t, :], st[0][:, t, :])
                ins.then_inc(s(f"{name}_stats"), 1)

            def normalise(name, st, src, dst, done, g):
                ge(dve, f"{name}_rstd", g + 1)
                for t in range(GT):
                    ins = dve.tensor_scalar(dst[:, t * D:(t + 1) * D], src[t], st[1][:, t, 0:1], st[3][:, t:t + 1],
                                            ALU.subtract, ALU.mult)
                ins.then_inc(s(done), 1)

            def centre(b, j, which, name, st, dst, done):
                ge(dve, f"{name}_stats", G * b + j + 1)
                for t, src in enumerate(x_tiles(b, j)):
                    ins = dve.scalar_tensor_tensor(dst[:, t * D:(t + 1) * D], src, st[1][:, t, 0:1], mod_row(b, which),
                                                   ALU.subtract, ALU.mult)
                ins.then_inc(s(done), 1)

            def spread(b, j, which, name, st, src, ready, done):
                ge(dve, ready, G * b + j + 1)
                ge(dve, f"{name}_rstd", G * b + j + 1)
                for t, dst in enumerate(h_tiles(b, j)):
                    ins = dve.scalar_tensor_tensor(dst, src[:, t * D:(t + 1) * D], st[3][:, t:t + 1], mod_row(b, which),
                                                   ALU.mult, ALU.add)
                ins.then_inc(s(done), 1)

            def x_tiles(b, j):
                return [tile(x_all, b, j * GT + t) for t in range(GT)]

            def h_tiles(b, j):
                return [tile(h_all, b, j * GT + t) for t in range(GT)]

            dve.wait_ge(s("in_x0"), 16)
            norm_stats("x", st_x[0], x_tiles(0, 0), 0)
            for b in range(B):
                dve.wait_ge(s("mod_mm"), b + 1)
                dve.tensor_copy(mod[:, b, 4:6, :].rearrange("p a d -> p (a d)"), banks[B + b][:, 0:2 * D]).then_inc(s("mod_hi"), 1)
            dve.wait_ge(s("mod_hi"), B)
            dve.wait_ge(s("mod_lo"), B)
            for m in (MOD_SCALE_A, MOD_SCALE_B):
                ins = dve.tensor_scalar(mod[:, :, m, :], mod[:, :, m, :], 1.0, None, ALU.add)
            ins.then_inc(s("mod_ready"), 1)
            dve.wait_ge(s("mod_ready"), 1)
            centre(0, 0, MOD_SCALE_A, "x", st_x[0], centred[0], "centred_ready")
            norm_stats("x", st_x[1], x_tiles(0, 1), 1)
            for b in range(1, B):
                dve.wait_ge(s(f"in_x{b}"), 16)

            def gates():
                for n_, m in enumerate((MOD_GATE_A, MOD_GATE_B)):
                    v, sign = mod[:, :, m, :], gate_sign[:, :, n_, :]
                    dve.tensor_scalar(sign, v, 0.0, 0.5, ALU.is_ge, ALU.subtract).then_inc(s("gate_step"), 1)
                    dve.wait_ge(s("gate_step"), 4 * n_ + 1)
                    dve.tensor_tensor(v, v, sign, ALU.mult).then_inc(s("gate_step"), 1)
                    dve.wait_ge(s("gate_step"), 4 * n_ + 2)
                    dve.tensor_scalar(v, v, 0.125, 4.0, ALU.max, ALU.mult).then_inc(s("gate_step"), 1)
                    dve.wait_ge(s("gate_step"), 4 * n_ + 3)
                    dve.tensor_tensor(v, v, sign, ALU.mult).then_inc(s("gate_step"), 1)
                dve.wait_ge(s("gate_step"), 8)
                dve.wait_ge(s("pool_const"), 2)
                dve.tensor_tensor(gate_diag[:, :, :], mod[:, :, MOD_GATE_A, :], ident[:, :].unsqueeze(1).to_broadcast([P, B, P]),
                                  ALU.mult).then_inc(s("mod_ready"), 1)
                dve.memset(carry[:, :], 0.0)
                dve.memset(carry_f[:, :], 0.0).then_inc(s("carry_ready"), 1)
            def features(b, j):
                g = G * b + j
                ge(dve, "k_mm", g + 1)
                ge(dve, "kvs_mm", g - 1)
                dve.tensor_scalar(kfeat[j][:, :], kb[:, :], 0.0, STAB, ALU.max, ALU.add).then_inc(s("kfeat_ready"), 1)
                ge(dve, "q_mm", g + 1)
                dve.tensor_scalar(group(q_all, b, j), qb[:, :], 0.0, STAB, ALU.max, ALU.add).then_inc(s("q_ready"), 1)

            def keep_kvs(b):
                ge(dve, "kvs_mm", G * (b + 1))
                kv = batch(kvs_all, b)
                dve.tensor_tensor(kv[:, 0:D], kvb[:, 0:D], same_head[:, 0:D], ALU.mult)
                dve.tensor_scalar(kv[:, D:NKV], same_head[:, D:NKV], kvb[:, D:D + 1], None, ALU.mult).then_inc(s("kvs_ready"), 1)

            def a1(b, j):
                g = G * b + j
                spread(b, j, MOD_SHIFT_A, "x", st_x[j], centred[j], "centred_ready", "h_ready")
                ge_apart(dve, "h_ready", g + 1, "dve_passed")
                norm_stats("h", st_h[j], h_tiles(b, j), g)
                if exists(b, j, 1):
                    nb_, nj = at(b, j, 1)
                    centre(nb_, nj, MOD_SCALE_A, "x", st_x[nj], centred[nj], "centred_ready")
                if exists(b, j, 2):
                    norm_stats("x", st_x[j], x_tiles(*at(b, j, 2)), g + 2)
                normalise("h", st_h[j], h_tiles(b, j), unit1[j], "unit1_ready", g)
                if j == 1 and exists(b, j, -2):
                    keep_kvs(b - 1)
                if exists(b, j, -1):
                    features(*at(b, j, -1))
                if isinstance(b, int) and g == 0:
                    gates()

            groups(dve, a1)
            features(B - 1, 1)
            keep_kvs(B - 1)

            def attend(b, j):
                g = G * b + j
                ge(dve, "num_mm", g + 1)
                for h in range(2):
                    v = nb[h][:, 0:2 * NKV].rearrange("p (t n) -> p t n", t=2)
                    ins = dve.reciprocal(rden[:, 2 * h:2 * h + 2, :], v[:, :, D:NKV])
                ins.then_inc(s("rden_ready"), 1)
                ge(dve, "att_T", g - 1)
                ge(dve, "rden_ready", g + 1)
                for h in range(2):
                    v = nb[h][:, 0:2 * NKV].rearrange("p (t n) -> p t n", t=2)[:, :, 0:D]
                    ins = dve.tensor_tensor(
                        att[j][:, 2 * h * D:(2 * h + 2) * D].rearrange("p (t h d) -> p t h d", t=2, h=H),
                        v.rearrange("p t (h d) -> p t h d", h=H),
                        rden[:, 2 * h:2 * h + 2, :].unsqueeze(3).to_broadcast([P, 2, H, DH]), ALU.mult)
                ins.then_inc(s("att_ready"), 1)

            def residual(b, j):
                g = G * b + j
                ge(dve, "wo_mm", g + 1)
                dve.tensor_tensor(add1[j][:, :], wb[:, :], group(h_all, b, j), ALU.add).then_inc(s("add1_ready"), 1)
                ge_apart(dve, "add1_ready", g + 1, "dve_passed")
                norm_stats("a", st_a[j], [add1[j][:, t * D:(t + 1) * D] for t in range(GT)], g)

            def unit(b, j):
                g = G * b + j
                ge(dve, "unit2_T", g - 1)
                normalise("a", st_a[j], [add1[j][:, t * D:(t + 1) * D] for t in range(GT)], unit2[j], "unit2_ready", g)

            def first_sum(b, j):
                g = G * b + j
                ge(dve, "base_ready", g + 1)
                ge(dve, "gate_mm", g + 1)
                dve.tensor_tensor(group(x_all, b, j), wb[:, :], group(x_all, b, j), ALU.add).then_inc(s("x2_ready"), 1)
                ge_apart(dve, "x2_ready", g + 1, "dve_passed")
                norm_stats("y", st_y[j], x_tiles(b, j), g)

            def modulate(b, j):
                centre(b, j, MOD_SCALE_B, "y", st_y[j], yhat, "yhat_ready")
                spread(b, j, MOD_SHIFT_B, "y", st_y[j], yhat, "yhat_ready", "h3_ready")

            def rms_norm(b, j):
                g = G * b + j
                ge(dve, "rms_ready", g + 1)
                ge(dve, "normed_T", g - 1)
                ge(dve, "rows_free", g - 1)
                for t in range(GT):
                    ins = dve.tensor_scalar(token_rows[:, j * GT + t, 0, 0:D], tile(h_all, b, j * GT + t), rms[j][:, t:t + 1],
                                            None, ALU.mult)
                ins.then_inc(s("normed_ready"), 1)

            def choose(b, j):
                g = G * b + j
                ge(dve, "score_mm", g + 1)
                dve.tensor_copy(score[:, :, :], rb[:, 0:GT * E].rearrange("p (r e) -> p r e", e=E)).then_inc(s("score_ready"), 1)
                ge_apart(dve, "score_ready", g + 1, "dve_passed")
                for t in range(GT):
                    ins = dve.max(top[:, t, :], score[:, t, :])
                ins.then_inc(s("top_ready"), 1)
                ge_apart(dve, "top_ready", g + 1, "dve_passed")
                for t in range(GT):
                    ins = dve.max_index(top_ix[:, t, :], top[:, t, :], score[:, t, :])
                ins.then_inc(s("topix_ready"), 1)
                ge(dve, "exp_done", g)
                dve.tensor_tensor(expin[:, :, :], top[:, :, :], top[:, :, 0:1].to_broadcast([P, GT, E]), ALU.subtract).then_inc(s("expin_ready"), 1)
                ge(dve, "topix_ready", g + 1)
                dve.tensor_copy(top_f[:, :, :], top_ix[:, :, 0:TOPK].rearrange("p r k -> p k r")).then_inc(s("topf_ready"), 1)
                ge(dve, "topf_ready", g + 1)
                dve.tensor_tensor(onehot[:, :, :, :].rearrange("p k r e -> p (k r) e"),
                                  top_f[:, :, :].rearrange("p k r -> p (k r)").unsqueeze(2).to_broadcast([P, TOPK * GT, E]),
                                  expert_no[:, :].unsqueeze(1).to_broadcast([P, TOPK * GT, E]), ALU.is_equal).then_inc(s("onehot_ready"), 1)
                ge(dve, "rank_mm", g)
                ge(dve, "onehot_ready", g + 1)
                dve.tensor_tensor(picked[:, :, :], onehot[:, 0, :, :], onehot[:, 1, :, :], ALU.add).then_inc(s("picked_ready"), 1)

            def place(b, j):
                g = G * b + j
                ge(dve, "rank_mm", g + 1)
                dve.tensor_tensor(slotrow[:, :, :], rb[:, 0:GT * E].rearrange("p (r e) -> p r e", e=E),
                                  region[:, :].unsqueeze(1).to_broadcast([P, GT, E]), ALU.add).then_inc(s("slotrow_ready"), 1)
                dve.tensor_reduce(picked_n[:, :], picked[:, :, :].rearrange("p r e -> p e r"), AX.X, ALU.add).then_inc(s("pickedn_ready"), 1)
                ge(dve, "exp_done", g + 1)
                dve.tensor_reduce(expsum[:, :], expo[:, :, :], AX.X, ALU.add).then_inc(s("expsum_ready"), 1)
                ge(dve, "slotrow_ready", g + 1)
                for k in range(TOPK):
                    ins = dve.tensor_tensor(pickrow[:, k, :, :], onehot[:, k, :, :], slotrow[:, :, :], ALU.mult)
                ins.then_inc(s("pickrow_ready"), 1)
                ge(dve, "expsum_ready", g + 1)
                dve.reciprocal(rsum[:, :], expsum[:, :]).then_inc(s("rsum_ready"), 1)
                ge(dve, "pickedn_ready", g + 1)
                dve.tensor_tensor(carry_f[:, :], carry_f[:, :], picked_n[:, :], ALU.add).then_inc(s("below_ready"), 1)
                ge(dve, "pickrow_ready", g + 1)
                dve.tensor_reduce(slot_f[:, :, :].rearrange("p k r -> p (k r)"), pickrow[:, :, :, :].rearrange("p k r e -> p (k r) e"),
                                  AX.X, ALU.add).then_inc(s("slotf_ready"), 1)
                ids = dest_all[:, b, j * GT:(j + 1) * GT, :] if isinstance(b, int) else \
                    dest_all[:, bass.ds(b, 1), j * GT:(j + 1) * GT, :].rearrange("p a r k -> p (a r) k")
                dve.tensor_copy(token_rows[:, j * GT:(j + 1) * GT, :, DEST].bitcast(I32), ids)
                ge(dve, "below_ready", g + 1)
                dve.tensor_copy(carry[:, :], carry_f[:, :]).then_inc(s("carry_ready"), 1)
                ge(dve, "rsum_ready", g + 1)
                dve.tensor_tensor(token_rows[:, j * GT:(j + 1) * GT, :, GATE], expo[:, :, 0:TOPK],
                                  rsum[:, :].unsqueeze(2).to_broadcast([P, GT, TOPK]), ALU.mult).then_inc(s("gates_ready"), 1)
                ge(dve, "slotf_ready", g + 1)
                dve.tensor_copy(slot[j][:, :, :], slot_f[:, :, :]).then_inc(s("slot_ready"), 1)

            def a2(b, j):
                if exists(b, j, -1):
                    first_sum(*at(b, j, -1))
                if exists(b, j, -2):
                    choose(*at(b, j, -2))
                if exists(b, j, 1):
                    residual(*at(b, j, 1))
                if exists(b, j, -1):
                    modulate(*at(b, j, -1))
                if exists(b, j, -2):
                    place(*at(b, j, -2))
                if exists(b, j, 1):
                    unit(*at(b, j, 1))
                if exists(b, j, -1):
                    rms_norm(*at(b, j, -1))
                if exists(b, j, 2):
                    attend(*at(b, j, 2))

            attend(0, 0)
            residual(0, 0)
            attend(0, 1)
            unit(0, 0)
            steps(dve, a2)

            m = [0]

            def step(ins):
                m[0] += 1
                ins.then_inc(s("tab_step"), 1)
                dve.wait_ge(s("tab_step"), m[0])

            dve.wait_ge(s("count_mm"), 1)
            step(dve.tensor_copy(count[:, :], wb[0:1, 0:E]))
            dve.tensor_tensor(pad_f[:, :], count[:, :], region[0:1, :], ALU.add)
            step(dve.tensor_tensor(cmp_level[:, :, :], count[:, :].unsqueeze(2).to_broadcast([1, E, TOK // P]),
                                   level[:, :].unsqueeze(1).to_broadcast([1, E, TOK // P]), ALU.is_gt))
            dve.tensor_copy(pad_at[:, :], pad_f[:, :]).then_inc(s("pads_ready"), 1)
            step(dve.tensor_reduce(tiles[:, :], cmp_level[:, :, :], AX.X, ALU.add))
            step(dve.tensor_copy(tiles_end[:, 0:1], tiles[:, 0:1]))
            for e in range(1, E):
                step(dve.tensor_tensor(tiles_end[:, e:e + 1], tiles_end[:, e - 1:e], tiles[:, e:e + 1], ALU.add))
            step(dve.tensor_tensor(past, tile_no[:, :].unsqueeze(2).to_broadcast([1, NT, E]),
                                   tiles_end[:, :].unsqueeze(1).to_broadcast([1, NT, E]), ALU.is_ge))
            step(dve.tensor_tensor(past_tiles, past, tiles[:, :].unsqueeze(1).to_broadcast([1, NT, E]), ALU.mult))
            expert, start, row, used, dummy, diff = range(6)
            step(dve.tensor_reduce(tab[:, expert, :], past, AX.X, ALU.add))
            step(dve.tensor_reduce(tab[:, start, :], past_tiles, AX.X, ALU.add))
            step(dve.tensor_scalar(tab[:, used, :], tab[:, expert, :], float(E), None, ALU.is_lt))
            step(dve.tensor_tensor(tab[:, diff, :], tile_no[:, :], tab[:, start, :], ALU.subtract))
            step(dve.tensor_scalar(tab[:, diff, :], tab[:, diff, :], float(P), None, ALU.mult))
            step(dve.tensor_scalar(tab[:, row, :], tab[:, expert, :], float(CAP), None, ALU.mult))
            step(dve.tensor_tensor(tab[:, row, :], tab[:, row, :], tab[:, diff, :], ALU.add))
            step(dve.tensor_scalar(tab[:, row, :], tab[:, row, :], pad_f[:, E - 1:E], None, ALU.subtract))
            step(dve.tensor_tensor(tab[:, row, :], tab[:, row, :], tab[:, used, :], ALU.mult))
            step(dve.tensor_scalar(tab[:, row, :], tab[:, row, :], pad_f[:, E - 1:E], None, ALU.add))
            step(dve.tensor_scalar(tab[:, expert, :], tab[:, expert, :], float(E - 1), None, ALU.min))
            dve.tensor_copy(tile_row[:, :], tab[:, row, :])
            dve.tensor_copy(tile_expert[:, :], tab[:, expert, :]).then_inc(s("tables_ready"), 1)

            z(dve, 0)

            def x_out(j, p):
                ge(dve, "x_T", j + 1)
                ge(dve, "v2_mm", j - 1)
                dve.tensor_scalar(xT[p][:, :], xtb[:, 0:P], vec[:, NSCALE:NSCALE + 1], None, ALU.mult).then_inc(s("xT_ready"), 1)

            def gated(j, p):
                ge(dve, "g_ready", j + 1)
                ge(dve, "y_mm", j - 1)
                ge(dve, "v2_mm", j + 1)
                dve.tensor_tensor(hT[p][:, :], vb_[:, 0:HC * P], act_g[p][:, :], ALU.mult).then_inc(s("hT_ready"), 1)

            def y_out(j, u):
                ge(dve, "y_mm", j + 1)
                dve.tensor_scalar(y_sb[u][:, :], yb[:, 0:D], slots_in[u][:, GATE:GATE + 1], None, ALU.mult).then_inc(s("y_ready"), 1)

            def tile_step(i, u, _):
                j = UN * i + u
                if not is_last(i, u):
                    x_out(j + 1, (u + 1) % 2)
                gated(j, u % 2)
                if not (isinstance(j, int) and j == 0):
                    y_out(j - 1, (u - 1) % UN)

            dve.memset(up_now[:, :, :, HM:], 0.0).then_inc(s("up_padded"), 1)
            x_out(0, 0)
            slot_tiles(dve, lambda i: None, tile_step)
            y_out(NT - 1, UN - 1)

            ge(dve, "dve_z_ready", G)
            ge(dve, "pool_z_ready", G * (B - 1))

            for b in range(B):
                dve.wait_ge(s(f"pair{b}"), 32)
                pair_sum(dve, b, 0)
                for j in range(G):
                    dve.wait_ge(s(f"pairsum{j}"), b + 1)
                    v = by_tile(group(q_all, b, j))
                    dve.tensor_tensor(v, v, mod_rows(b, MOD_GATE_B), ALU.mult).then_inc(s("pairgate"), 1)
                for j in range(G):
                    dve.wait_ge(s("pairgate"), G * b + j + 1)
                    dve.tensor_tensor(group(h_all, b, j), group(q_all, b, j), group(h_all, b, j), ALU.add).then_inc(s("res_ready"), 1)

        @block.tensor
        def _(pe):
            for name in ("normed_T", "rank_mm"):
                pe.sem_inc(s(name), 1)
            pe.wait_ge(s("silu_rows"), 1)
            for b in range(B):
                pe.matmul(banks[b][:, :], silu_cb[:, b, :], wmod_sb[:, 0:4 * D], start=True, stop=True)
                pe.matmul(banks[B + b][:, 0:2 * D], silu_cb[:, b, :], wmod_sb[:, 4 * D:6 * D], start=True, stop=True).then_inc(s("mod_mm"), 1)
            pe.wait_ge(s("in_w"), 48)
            pe.wait_ge(s("pool_const"), 2)
            pe.wait_ge(s("mod_lo"), B)
            pe.wait_ge(s("mod_hi"), B)

            def turn(bank, src, done):
                for t in range(GT):
                    ins = pe.transpose(bank[:, t * P:(t + 1) * P], src[:, t * P:(t + 1) * P], ident[:, :])
                ins.then_inc(s(done), 1)

            def kvs(b, j):
                g = G * b + j
                ge(pe, "kfeat_ready", g + 1)
                ge(pe, "v_ready", g + 1)
                if j == 0:
                    ge(pe, "kvs_ready", b)
                for t in range(GT):
                    ins = pe.matmul(kvb[:, 0:D + 1], kfeat[j][:, t * D:(t + 1) * D], vones[j][:, t, 0:D + 1],
                                    start=(j == 0 and t == 0), stop=(j == G - 1 and t == GT - 1))
                ins.then_inc(s("kvs_mm"), 1)

            def a1(b, first):
                for j in range(G):
                    g = G * b + j
                    ge(pe, "unit1_ready", g + 1)
                    ge(pe, "ln1_ready", g - 1)
                    turn(trb[j], unit1[j], "unit1_T")
                    ge(pe, "ln1_ready", g + 1)
                    ge(pe, "v_ready", g)
                    for t in range(GT):
                        ins = pe.matmul(vb[:, t * D:(t + 1) * D], ln1T[j][:, t * P:(t + 1) * P], wv_sb[:, :], start=True, stop=True)
                    ins.then_inc(s("v_mm"), 1)
                    ge(pe, "kfeat_ready", g)
                    for t in range(GT):
                        ins = pe.matmul(kb[:, t * D:(t + 1) * D], ln1T[j][:, t * P:(t + 1) * P], wk_sb[:, :], start=True, stop=True)
                    ins.then_inc(s("k_mm"), 1)
                    if not (first and j == 0):
                        kvs(*at(b, j, -1))
                    ge(pe, "q_ready", g)
                    pe.matmul(qb[:, :], wq_sb[:, :], ln1T[j][:, :], start=True, stop=True).then_inc(s("q_mm"), 1)

            a1(0, True)
            with pe.Fori(1, B) as b:
                a1(b, False)
            kvs(B - 1, 1)

            pe.wait_ge(s("in_w2"), 64)

            def read_out(b, j):
                g = G * b + j
                ge(pe, "kvs_ready", b + 1)
                ge(pe, "attT_ready", g)
                ge(pe, "qf_ready", g + 1)
                for t in range(GT):
                    c0 = (t % 2) * NKV
                    ins = pe.matmul(nb[t // 2][:, c0:c0 + NKV], qf[j][:, t * P:(t + 1) * P], batch(kvs_all, b), start=True, stop=True)
                ins.then_inc(s("num_mm"), 1)

            def att_turn(b, j):
                ge(pe, "att_ready", G * b + j + 1)
                turn(nb[0], att[j], "att_T")

            def project(b, j):
                g = G * b + j
                ge(pe, "attT_ready", g + 1)
                ge(pe, "add1_ready", g)
                ge(pe, "x2_ready", g - 1)
                for t in range(GT):
                    ins = pe.matmul(wb[:, t * D:(t + 1) * D], attT[j][:, t * P:(t + 1) * P], wo_sb[:, :], start=True, stop=True)
                ins.then_inc(s("wo_mm"), 1)

            def unit2_turn(b, j):
                g = G * b + j
                ge(pe, "ln2_ready", g)
                ge(pe, "unit2_ready", g + 1)
                turn(tl, unit2[j], "unit2_T")

            def ffn1(b, j):
                g = G * b + j
                ge(pe, "ln2_ready", g + 1)
                for c in range(FC):
                    ge(pe, "hid_ready", FC * g + c - 1)
                    pe.matmul(fb[c % 2][:, :], w1_sb[:, c * P:(c + 1) * P], ln2T[j][:, :], start=True, stop=True).then_inc(s("ff1_mm"), 1)

            def ffn2(b, j):
                g = G * b + j
                ge(pe, "ffn_ready", g)
                for c in range(FC):
                    ge(pe, "hid_ready", FC * g + c + 1)
                    ins = pe.matmul(ob[:, :], w2_sb[:, c, :], hidT[:, c, :], start=(c == 0), stop=(c == FC - 1))
                ins.then_inc(s("ff2_mm"), 1)

            def gate(b, j, attended):
                g = G * b + j
                ge(pe, "add1_ready", attended)
                ge(pe, "x2_ready", g)
                ge(pe, "ffn_ready", g + 1)
                for t in range(GT):
                    cols, tok = slice(t * D, (t + 1) * D), slice(t * P, (t + 1) * P)
                    pe.matmul(wb[:, cols], attT[j][:, tok], batch(wo_gate, b), start=True, stop=False)
                    ins = pe.matmul(wb[:, cols], ffnT[j][:, tok], batch(gate_diag, b), start=False, stop=True)
                ins.then_inc(s("gate_mm"), 1)

            def turn_normed(b, j):
                g = G * b + j
                ge(pe, "slotrow_ready", g)
                ge(pe, "normed_ready", g + 1)
                for t in range(GT):
                    ins = pe.transpose(rb[:, t * P:(t + 1) * P], token_rows[:, j * GT + t, 0, 0:D], ident[:, :])
                ins.then_inc(s("normed_T"), 1)

            def scores(b, j):
                ge(pe, "xn_ready", G * b + j + 1)
                for t in range(GT):
                    ins = pe.matmul(rb[:, t * E:t * E + RPAD], xnT[j][:, t * P:(t + 1) * P], wr_sb[:, :], start=True, stop=True)
                ins.then_inc(s("score_mm"), 1)

            def rank(b, j):
                g = G * b + j
                ge(pe, "carry_ready", g + 1)
                ge(pe, "picked_ready", g + 1)
                o = rb[:, 0:GT * E]
                pv = picked[:, :, :].rearrange("p r e -> p (r e)")
                pe.matmul(o, before[:, :], pv, start=True, stop=False)
                for r in range(GT - 1):
                    n = GT - 1 - r
                    pe.matmul(o[:, (r + 1) * E:].rearrange("p (r e) -> p r e", e=E), ones[:, :],
                              picked[:, r:r + 1, :].to_broadcast([P, n, E]), start=False, stop=False)
                pe.matmul(o.rearrange("p (r e) -> p r e", e=E), ones[:, :],
                          carry[:, :].unsqueeze(1).to_broadcast([P, GT, E]), start=False, stop=True).then_inc(s("rank_mm"), 1)

            def a2(b, j):
                if exists(b, j, 1):
                    project(*at(b, j, 1))
                if exists(b, j, 0):
                    ffn1(b, j)
                if exists(b, j, -2):
                    rank(*at(b, j, -2))
                if exists(b, j, 0):
                    ffn2(b, j)
                if exists(b, j, 2):
                    read_out(*at(b, j, 2))
                if exists(b, j, 1):
                    unit2_turn(*at(b, j, 1))
                if exists(b, j, -1):
                    turn_normed(*at(b, j, -1))
                if exists(b, j, 0):
                    gate(b, j, G * b + j + (2 if exists(b, j, 1) else 1))
                if exists(b, j, 2):
                    att_turn(*at(b, j, 2))
                if exists(b, j, -1):
                    scores(*at(b, j, -1))

            pe.wait_ge(s("wo_gate_ready"), 1)
            read_out(0, 0)
            att_turn(0, 0)
            project(0, 0)
            read_out(0, 1)
            att_turn(0, 1)
            unit2_turn(0, 0)
            steps(pe, a2)
            ge(pe, "carry_ready", G * B + 1)
            pe.matmul(wb[:, 0:E], ones[:, :], carry[:, :], start=True, stop=True).then_inc(s("count_mm"), 1)

            pe.wait_ge(s("in_exp"), 16 * (1 + HC))
            pe.wait_ge(s("tables_ready"), 1)

            def x_turn(i, u):
                j = UN * i + u
                ge(pe, f"in_s{u}", 16 * (i + 1))
                ge(pe, "xT_ready", j)
                pe.transpose(xtb[:, 0:P], slots_in[u][:, 0:D], ident[:, :]).then_inc(s("x_T"), 1)

            def experts_of(i):
                before_ = 0 if isinstance(i, int) and i == 0 else UN
                n = UN + before_
                e = tile_expert[0:1, UN * i - before_:UN * i + UN] if isinstance(i, int) else tile_expert[0:1, bass.ds(UN * i - UN, n)]
                values = nc.values_load_multi_w_load_instructions(
                    e, [mybir.EngineType.PE], min_val=0, max_val=E - 1,
                    skip_runtime_bounds_check_because="the chip makes the table within these bounds")[1]
                return {u - before_: v for u, v in enumerate(values)}

            def up(j, p):
                ge(pe, "up_ready", j + 1)
                ge(pe, "xT_ready", j + 1)
                ge(pe, "g_ready", j)
                for half, bank, done in ((1, gb_, "g_mm"), (0, vb_, "v2_mm")):
                    if half == 0:
                        ge(pe, "hT_ready", j)
                    for c in range(HC):
                        ins = pe.matmul(bank[:, c * P:(c + 1) * P], up_now[:, p, half, c * P:(c + 1) * P], xT[p][:, :],
                                        start=True, stop=True)
                    ins.then_inc(s(done), 1)

            def down(j, p, e):
                ge(pe, "hT_ready", j + 1)
                ge(pe, "y_ready", j)
                for c in range(HC):
                    n = min(P, HM - c * P)
                    w = down_sb[0:n, bass.ds(e, 1), c * D:(c + 1) * D].rearrange("p a n -> p (a n)")
                    ins = pe.matmul(yb[:, 0:D], hT[p][0:n, c * P:(c + 1) * P], w, start=(c == 0), stop=(c == HC - 1))
                ins.then_inc(s("y_mm"), 1)

            def tile_step(i, u, experts):
                j = UN * i + u
                if not is_last(i, u):
                    x_turn(*((i, u + 1) if u < UN - 1 else (i + 1, 0)))
                up(j, u % 2)
                if not (isinstance(j, int) and j == 0):
                    down(j - 1, (u + 1) % 2, experts[u - 1])

            pe.wait_ge(s("up_padded"), 1)
            x_turn(0, 0)
            slot_tiles(pe, experts_of, tile_step)
            down(NT - 1, 1, experts_of(NT // UN - 1)[UN - 1])


def kernel(**inputs):
    import numpy as np
    import concourse.bacc as bacc
    from concourse.bass_utils import run_bass_kernel_spmd as run

    a = {k.replace("L0_", ""): np.asarray(v) for k, v in inputs.items()}
    columns = [a["attn_gamma1"], a["attn_beta1"], a["ffn_norm_scale"], a["attn_b2"], *a["attn_b1"].reshape(FC, P)]
    arrays = {
        "x": a["attn_x"],
        "c_t": a["c"].T,
        "wmod": a["wmod"],
        "vecs": np.stack(columns, axis=1),
        "wq": a["attn_wq"].reshape(D, D),
        "wk": a["attn_wk"].reshape(D, D),
        "wv": a["attn_wv"].reshape(D, D),
        "wo": a["attn_wo"].reshape(D, D),
        "w1": a["attn_w1"],
        "w2": a["attn_w2"],
        "wr_t": a["ffn_w_router"].T,
        "w_up": a["ffn_w_up"].transpose(2, 0, 1),
        "w_down": a["ffn_w_down"].transpose(2, 0, 1),
    }
    nc = bacc.Bacc("TRN2", target_bir_lowering=False, num_devices=1)
    arrays = {f"in_{k}": np.ascontiguousarray(v) for k, v in arrays.items()}
    args = [nc.dram_tensor(k, v.shape, mybir.dt.from_np(v.dtype), kind="ExternalInput").ap() for k, v in arrays.items()]
    out = nc.dram_tensor("out", (B, L, D), F32, kind="ExternalOutput").ap()
    build(nc, *args, out)
    r = run(nc, [arrays], core_ids=[0])
    return r.results[0]["out"]
```
